# Optimizing a Trainium2 kernel written in Bass

```python
import numpy as np
import jax
import jax.numpy as jnp

def _softmax(x, axis=-1):
    return jax.nn.softmax(x, axis=axis)

def _gelu(x):
    return jax.nn.gelu(x, approximate=True)

def _silu(x):
    return jax.nn.silu(x)

def _sigmoid(x):
    return jax.nn.sigmoid(x)

def _layernorm(x, axis=-1, eps=1e-05):
    m = jnp.mean(x, axis=axis, keepdims=True)
    v = jnp.var(x, axis=axis, keepdims=True)
    return (x - m) / jnp.sqrt(v + eps)

def _scatter_add(tgt, idx, src, axis=0):
    return tgt.at[idx].add(src)

def _segment_sum(src, seg, n):
    return jax.ops.segment_sum(src, seg, n)
kernel_name = 'mk_gnn_preln_d4_gnn_r64_1b151d'

def setup_inputs(seed: int=0):
    np.random.seed(seed)
    _w = jnp.asarray

    def _rec_inputs():
        import jax
        import jax.numpy as jnp
        _gk = jax.random.key(seed)
        x = -0.0005121 + 1.001 * jax.random.normal(jax.random.fold_in(_gk, 1), (50000, 160), jnp.float32)
        src = jax.random.randint(jax.random.fold_in(_gk, 2), (12500,), 0, 50000, jnp.int32)
        dst = jnp.minimum((50000 * jax.random.uniform(jax.random.fold_in(_gk, 3), (12500,)) ** 2.0).astype(jnp.int32), 49999)
        _o = jnp.argsort(dst, stable=True)
        src = src[_o]
        dst = dst[_o]
        edge_attr_10 = jax.random.uniform(jax.random.fold_in(_gk, 12), (12500, 10), jnp.float32, 0.0, 1)
        edge_attr_16 = 6.40344e-05 + 1.00026 * jax.random.normal(jax.random.fold_in(_gk, 13), (12500, 16), jnp.float32)
        edge_attr_3 = 0.00047201 + 1.00023 * jax.random.normal(jax.random.fold_in(_gk, 14), (12500, 3), jnp.float32)
        edge_attr_4 = 0.000735704 + 1.0001 * jax.random.normal(jax.random.fold_in(_gk, 15), (12500, 4), jnp.float32)
        edge_attr_64 = 0.000279952 + 1.00013 * jax.random.normal(jax.random.fold_in(_gk, 16), (12500, 64), jnp.float32)
        node_vec1 = -0.00719938 + 0.999885 * jax.random.normal(jax.random.fold_in(_gk, 18), (50000, 1), jnp.float32)
        node_vec1_n2 = -0.00719938 + 0.999885 * jax.random.normal(jax.random.fold_in(_gk, 19), (50000, 1), jnp.float32)
        node_vec1_n3 = -0.00719938 + 0.999885 * jax.random.normal(jax.random.fold_in(_gk, 20), (50000, 1), jnp.float32)
        return (x, src, dst, edge_attr_10, edge_attr_16, edge_attr_3, edge_attr_4, edge_attr_64, node_vec1, node_vec1_n2, node_vec1_n3)
    x, src, dst, edge_attr_10, edge_attr_16, edge_attr_3, edge_attr_4, edge_attr_64, node_vec1, node_vec1_n2, node_vec1_n3 = _rec_inputs()

    def _L0_gnn_setup():
        import jax, jax.numpy as jnp
        import numpy as np
        N = 20000
        E = 10000
        INV_SQRT3 = 0.5773502691896258
        INV8 = 0.125
        INV_SQRT32 = 0.17677669529663687
        INV64 = 0.015625
        INV32 = 0.03125
        INV_SQRT2048 = 0.022097086912079608
        key = jax.random.key(seed)
        ks = jax.random.split(key, 16)
        f32 = jnp.float32
        return {'node_features': jax.random.normal(ks[0], (N, 160), f32), 'edge_index': jax.random.randint(ks[1], (2, E), 0, N), 'edge_attr_tensor': jax.random.normal(ks[2], (E, 4), f32), 'node_attr_scalar_raw': jax.random.normal(ks[3], (N, 1), f32), 'Wm_ss': jax.random.normal(ks[4], (64, 64), f32), 'Wm_vv': jax.random.normal(ks[5], (32, 64), f32), 'Wm_sv': jax.random.normal(ks[6], (64, 32), f32), 'Wm_vs': jax.random.normal(ks[7], (32, 32), f32), 'Lm_s': jax.random.normal(ks[8], (64, 64), f32), 'Lm_v': jax.random.normal(ks[9], (32, 32), f32), 'Wu_ss': jax.random.normal(ks[10], (64, 64, 64), f32), 'Wu_vv': jax.random.normal(ks[11], (32, 32, 64), f32), 'Wu_sv': jax.random.normal(ks[12], (64, 32, 32), f32), 'Wu_vs': jax.random.normal(ks[13], (32, 64, 32), f32), 'Lu_s': jax.random.normal(ks[14], (64, 64), f32), 'Lu_v': jax.random.normal(ks[15], (32, 32), f32)}
    _L0_gnn_all = _L0_gnn_setup()
    _L0_gnn_in = {k: v for k, v in _L0_gnn_all.items() if k in ('Wm_ss', 'Wm_vv', 'Wm_sv', 'Wm_vs', 'Lm_s', 'Lm_v', 'Wu_ss', 'Wu_vv', 'Wu_sv', 'Wu_vs', 'Lu_s', 'Lu_v')}
    del _L0_gnn_all

    def _L1_gnn_setup():
        import jax, jax.numpy as jnp
        import numpy as np
        N_NODES = 10000
        N_EDGES = 5000
        MUL0, MUL1 = (64, 32)
        EDGE_DIM = 64
        W_NUMEL = 224
        DENOM = 32.0
        SQRT3 = 3.0 ** 0.5
        INV_SQRT3 = 1.0 / SQRT3
        INV_SQRT2 = 2.0 ** (-0.5)

        def _forward(node_feature, edge_attr, edge_feature, W_skip0, W_skip1, W_nl0, W_nl1, W_fc1, W_fc2, W_out_s, W_out_v, edge_index):
            N = node_feature.shape[0]
            E = edge_attr.shape[0]
            s = node_feature[:, :MUL0]
            v = node_feature[:, MUL0:].reshape(N, MUL1, 3)
            skip_s = s @ W_skip0
            skip_v = jnp.einsum('nmi,mk->nki', v, W_skip1)
            s = s @ W_nl0
            v = jnp.einsum('nmi,mk->nki', v, W_nl1)
            rhat = edge_attr / jnp.linalg.norm(edge_attr, axis=-1, keepdims=True)
            sh1 = SQRT3 * rhat
            w = jax.nn.relu(edge_feature @ W_fc1) @ W_fc2
            w0, w1, w2, w3, w4 = jnp.split(w, [64, 128, 160, 192], axis=-1)
            src, dst = (edge_index[0], edge_index[1])
            xs = s[dst]
            xv = v[dst]
            out0a = w0 * xs
            out0b = w3 * (jnp.einsum('emi,ei->em', xv, sh1) * INV_SQRT3)
            out1a = (w1 * xs)[:, :, None] * sh1[:, None, :]
            out1b = w2[:, :, None] * xv
            out1c = w4[:, :, None] * (jnp.cross(xv, sh1[:, None, :]) * INV_SQRT2)
            tp = jnp.concatenate([out0a, out0b, out1a.reshape(E, -1), out1b.reshape(E, -1), out1c.reshape(E, -1)], axis=-1)
            agg = jax.ops.segment_sum(tp, src, num_segments=N) / DENOM
            agg_s = agg[:, :96]
            agg_v = agg[:, 96:].reshape(N, 128, 3)
            out_s = agg_s @ W_out_s + skip_s
            out_v = jnp.einsum('nmi,mk->nki', agg_v, W_out_v) + skip_v
            fs = jax.nn.silu(out_s[:, :MUL0])
            gate = jax.nn.sigmoid(out_s[:, MUL0:MUL0 + 32])
            gv = gate[:, :, None] * out_v
            return jnp.concatenate([fs, gv.reshape(N, -1)], axis=-1)
        key = jax.random.key(seed)
        ks = jax.random.split(key, 12)

        def lin(k, fi, fo):
            return jax.random.normal(k, (fi, fo), jnp.float32) / np.float32(np.sqrt(fi))
        return {'node_feature': jax.random.normal(ks[0], (N_NODES, MUL0 + 3 * MUL1), jnp.float32), 'edge_attr': jax.random.normal(ks[1], (N_EDGES, 3), jnp.float32), 'edge_feature': jax.random.normal(ks[2], (N_EDGES, EDGE_DIM), jnp.float32), 'W_skip0': lin(ks[3], MUL0, 96), 'W_skip1': lin(ks[4], MUL1, 32), 'W_nl0': lin(ks[5], MUL0, MUL0), 'W_nl1': lin(ks[6], MUL1, MUL1), 'W_fc1': lin(ks[7], EDGE_DIM, 64), 'W_fc2': lin(ks[8], 64, W_NUMEL), 'W_out_s': lin(ks[9], 96, 96), 'W_out_v': lin(ks[10], 128, 32), 'edge_index': jax.random.randint(ks[11], (2, N_EDGES), 0, N_NODES)}
    _L1_gnn_all = _L1_gnn_setup()
    _L1_gnn_in = {k: v for k, v in _L1_gnn_all.items() if k in ('W_skip0', 'W_skip1', 'W_nl0', 'W_nl1', 'W_fc1', 'W_fc2', 'W_out_s', 'W_out_v')}
    del _L1_gnn_all

    def _L2_gnn_setup():
        import jax, jax.numpy as jnp
        import numpy as np
        N_NODES = 100000
        N_EDGES = 12500
        MUL_S = 64
        MUL_V = 32
        DIM = MUL_S + 3 * MUL_V
        EDGE_SCALAR_DIM = 16
        ISQ3 = 1.0 / np.sqrt(3.0)
        ISQ2 = 1.0 / np.sqrt(2.0)

        def _forward(x, edge_index, edge_feat, edge_scalars, W_ss, W_sv, W_vs, W_vv, W_rad, b_rad, L_s, L_v):
            src, dst = (edge_index[0], edge_index[1])
            n = x.shape[0]
            xs = x[:, :MUL_S]
            xv = x[:, MUL_S:].reshape(n, MUL_V, 3)
            xs_e = xs[src]
            xv_e = xv[src]
            es = edge_feat[:, 0]
            ev = edge_feat[:, 1:4]
            out_s = (jnp.einsum('eu,uo->eo', xs_e * es[:, None], W_ss) / np.sqrt(MUL_S) + jnp.einsum('eud,ed,uo->eo', xv_e, ev, W_vv) * ISQ3 / np.sqrt(MUL_V)) * ISQ2
            out_v = (jnp.einsum('eu,ed,uv->evd', xs_e, ev, W_sv) * ISQ3 / np.sqrt(MUL_S) + jnp.einsum('eud,e,uv->evd', xv_e, es, W_vs) * ISQ3 / np.sqrt(MUL_V)) * ISQ2
            messages = jnp.concatenate([out_s, out_v.reshape(-1, 3 * MUL_V)], axis=1)
            scale = jax.nn.sigmoid(edge_scalars @ W_rad.T + b_rad)
            messages = messages * scale
            agg = jax.ops.segment_sum(messages, dst, num_segments=n)
            h = x + agg
            hs = h[:, :MUL_S]
            hv = h[:, MUL_S:].reshape(n, MUL_V, 3)
            ys = hs @ L_s / np.sqrt(MUL_S)
            yv = jnp.einsum('nud,uv->nvd', hv, L_v) / np.sqrt(MUL_V)
            return jnp.concatenate([ys, yv.reshape(n, 3 * MUL_V)], axis=1)
        key = jax.random.key(seed)
        ks = jax.random.split(key, 12)
        x = jax.random.normal(ks[0], (N_NODES, DIM), dtype=jnp.float32)
        edge_index = jax.random.randint(ks[1], (2, N_EDGES), 0, N_NODES, dtype=jnp.int64)
        edge_feat = jax.random.normal(ks[2], (N_EDGES, 4), dtype=jnp.float32)
        edge_scalars = jax.random.normal(ks[3], (N_EDGES, EDGE_SCALAR_DIM), dtype=jnp.float32)
        W_ss = jax.random.normal(ks[4], (MUL_S, MUL_S), dtype=jnp.float32)
        W_sv = jax.random.normal(ks[5], (MUL_S, MUL_V), dtype=jnp.float32)
        W_vs = jax.random.normal(ks[6], (MUL_V, MUL_V), dtype=jnp.float32)
        W_vv = jax.random.normal(ks[7], (MUL_V, MUL_S), dtype=jnp.float32)
        W_rad = jax.random.normal(ks[8], (DIM, EDGE_SCALAR_DIM), dtype=jnp.float32) / np.sqrt(EDGE_SCALAR_DIM)
        b_rad = jax.random.normal(ks[9], (DIM,), dtype=jnp.float32) * 0.1
        L_s = jax.random.normal(ks[10], (MUL_S, MUL_S), dtype=jnp.float32)
        L_v = jax.random.normal(ks[11], (MUL_V, MUL_V), dtype=jnp.float32)
        return {'x': x, 'edge_index': edge_index, 'edge_feat': edge_feat, 'edge_scalars': edge_scalars, 'W_ss': W_ss, 'W_sv': W_sv, 'W_vs': W_vs, 'W_vv': W_vv, 'W_rad': W_rad, 'b_rad': b_rad, 'L_s': L_s, 'L_v': L_v}
    _L2_gnn_all = _L2_gnn_setup()
    _L2_gnn_in = {k: v for k, v in _L2_gnn_all.items() if k in ('W_ss', 'W_sv', 'W_vs', 'W_vv', 'W_rad', 'b_rad', 'L_s', 'L_v')}
    del _L2_gnn_all

    def _L3_gnn_setup():
        import jax, jax.numpy as jnp
        import numpy as np
        N = 25000
        E = 6250
        S = 64
        V = 32
        NB = 10
        H = 100
        WN = 192
        MID = 96
        NUM_NEIGHBORS = 16.0
        C_S = float(np.sin(np.pi / 8.0))
        C_X = float(np.cos(np.pi / 8.0))
        SQRT3 = float(np.sqrt(3.0))

        def fctp_scalar_attr(xs, xv, attr, Ws, Wv):
            s = xs * attr @ Ws
            v = jnp.einsum('nuc,uo->noc', xv * attr[:, :, None], Wv)
            return (s, v)
        key = jax.random.key(seed)
        k = jax.random.split(key, 24)

        def w(i, shape):
            return jax.random.normal(k[i], shape, jnp.float32) / np.sqrt(float(shape[0]))
        return {'node_input': jax.random.normal(k[0], (N, S + 3 * V), jnp.float32), 'node_attr': jax.random.normal(k[1], (N, 1), jnp.float32), 'node_crystal_attr': jax.random.normal(k[2], (N, 1), jnp.float32), 'sym_mask': jax.random.normal(k[3], (N, 1), jnp.float32), 'edge_attr': jax.random.normal(k[4], (E, 4), jnp.float32), 'edge_length_embedded': jax.random.uniform(k[5], (E, NB), dtype=jnp.float32), 'edge_src': jax.random.randint(k[6], (E,), 0, N), 'edge_dst': jax.random.randint(k[7], (E,), 0, N), 'Ws_sc_a': w(8, (S, S)), 'Wv_sc_a': w(9, (V, V)), 'Ws_sc_c': w(10, (S, S)), 'Wv_sc_c': w(11, (V, V)), 'Ws_l1_a': w(12, (S, S)), 'Wv_l1_a': w(13, (V, V)), 'Ws_l1_c': w(14, (S, S)), 'Wv_l1_c': w(15, (V, V)), 'W_fc1': w(16, (NB, H)), 'W_fc2': w(17, (H, WN)), 'Ws_l2_a': w(18, (MID, MID)), 'Wv_l2_a': w(19, (MID, MID)), 'Ws_l2_c': w(20, (MID, MID)), 'Wv_l2_c': w(21, (MID, MID)), 'Ws_l3': w(22, (MID, S)), 'Wv_l3': w(23, (MID, V))}
    _L3_gnn_all = _L3_gnn_setup()
    _L3_gnn_in = {k: v for k, v in _L3_gnn_all.items() if k in ('Ws_sc_a', 'Wv_sc_a', 'Ws_sc_c', 'Wv_sc_c', 'Ws_l1_a', 'Wv_l1_a', 'Ws_l1_c', 'Wv_l1_c', 'W_fc1', 'W_fc2', 'Ws_l2_a', 'Wv_l2_a', 'Ws_l2_c', 'Wv_l2_c', 'Ws_l3', 'Wv_l3')}
    del _L3_gnn_all
    return {'x': x, 'src': src, 'dst': dst, 'edge_attr_10': edge_attr_10, 'edge_attr_16': edge_attr_16, 'edge_attr_3': edge_attr_3, 'edge_attr_4': edge_attr_4, 'edge_attr_64': edge_attr_64, 'node_vec1': node_vec1, 'node_vec1_n2': node_vec1_n2, 'node_vec1_n3': node_vec1_n3, 'L0_gnn_Wm_ss': _L0_gnn_in['Wm_ss'], 'L0_gnn_Wm_vv': _L0_gnn_in['Wm_vv'], 'L0_gnn_Wm_sv': _L0_gnn_in['Wm_sv'], 'L0_gnn_Wm_vs': _L0_gnn_in['Wm_vs'], 'L0_gnn_Lm_s': _L0_gnn_in['Lm_s'], 'L0_gnn_Lm_v': _L0_gnn_in['Lm_v'], 'L0_gnn_Wu_ss': _L0_gnn_in['Wu_ss'], 'L0_gnn_Wu_vv': _L0_gnn_in['Wu_vv'], 'L0_gnn_Wu_sv': _L0_gnn_in['Wu_sv'], 'L0_gnn_Wu_vs': _L0_gnn_in['Wu_vs'], 'L0_gnn_Lu_s': _L0_gnn_in['Lu_s'], 'L0_gnn_Lu_v': _L0_gnn_in['Lu_v'], 'L1_gnn_W_skip0': _L1_gnn_in['W_skip0'], 'L1_gnn_W_skip1': _L1_gnn_in['W_skip1'], 'L1_gnn_W_nl0': _L1_gnn_in['W_nl0'], 'L1_gnn_W_nl1': _L1_gnn_in['W_nl1'], 'L1_gnn_W_fc1': _L1_gnn_in['W_fc1'], 'L1_gnn_W_fc2': _L1_gnn_in['W_fc2'], 'L1_gnn_W_out_s': _L1_gnn_in['W_out_s'], 'L1_gnn_W_out_v': _L1_gnn_in['W_out_v'], 'L2_gnn_W_ss': _L2_gnn_in['W_ss'], 'L2_gnn_W_sv': _L2_gnn_in['W_sv'], 'L2_gnn_W_vs': _L2_gnn_in['W_vs'], 'L2_gnn_W_vv': _L2_gnn_in['W_vv'], 'L2_gnn_W_rad': _L2_gnn_in['W_rad'], 'L2_gnn_b_rad': _L2_gnn_in['b_rad'], 'L2_gnn_L_s': _L2_gnn_in['L_s'], 'L2_gnn_L_v': _L2_gnn_in['L_v'], 'L3_gnn_Ws_sc_a': _L3_gnn_in['Ws_sc_a'], 'L3_gnn_Wv_sc_a': _L3_gnn_in['Wv_sc_a'], 'L3_gnn_Ws_sc_c': _L3_gnn_in['Ws_sc_c'], 'L3_gnn_Wv_sc_c': _L3_gnn_in['Wv_sc_c'], 'L3_gnn_Ws_l1_a': _L3_gnn_in['Ws_l1_a'], 'L3_gnn_Wv_l1_a': _L3_gnn_in['Wv_l1_a'], 'L3_gnn_Ws_l1_c': _L3_gnn_in['Ws_l1_c'], 'L3_gnn_Wv_l1_c': _L3_gnn_in['Wv_l1_c'], 'L3_gnn_W_fc1': _L3_gnn_in['W_fc1'], 'L3_gnn_W_fc2': _L3_gnn_in['W_fc2'], 'L3_gnn_Ws_l2_a': _L3_gnn_in['Ws_l2_a'], 'L3_gnn_Wv_l2_a': _L3_gnn_in['Wv_l2_a'], 'L3_gnn_Ws_l2_c': _L3_gnn_in['Ws_l2_c'], 'L3_gnn_Wv_l2_c': _L3_gnn_in['Wv_l2_c'], 'L3_gnn_Ws_l3': _L3_gnn_in['Ws_l3'], 'L3_gnn_Wv_l3': _L3_gnn_in['Wv_l3']}

def reference(x, src, dst, edge_attr_10, edge_attr_16, edge_attr_3, edge_attr_4, edge_attr_64, node_vec1, node_vec1_n2, node_vec1_n3, L0_gnn_Wm_ss, L0_gnn_Wm_vv, L0_gnn_Wm_sv, L0_gnn_Wm_vs, L0_gnn_Lm_s, L0_gnn_Lm_v, L0_gnn_Wu_ss, L0_gnn_Wu_vv, L0_gnn_Wu_sv, L0_gnn_Wu_vs, L0_gnn_Lu_s, L0_gnn_Lu_v, L1_gnn_W_skip0, L1_gnn_W_skip1, L1_gnn_W_nl0, L1_gnn_W_nl1, L1_gnn_W_fc1, L1_gnn_W_fc2, L1_gnn_W_out_s, L1_gnn_W_out_v, L2_gnn_W_ss, L2_gnn_W_sv, L2_gnn_W_vs, L2_gnn_W_vv, L2_gnn_W_rad, L2_gnn_b_rad, L2_gnn_L_s, L2_gnn_L_v, L3_gnn_Ws_sc_a, L3_gnn_Wv_sc_a, L3_gnn_Ws_sc_c, L3_gnn_Wv_sc_c, L3_gnn_Ws_l1_a, L3_gnn_Wv_l1_a, L3_gnn_Ws_l1_c, L3_gnn_Wv_l1_c, L3_gnn_W_fc1, L3_gnn_W_fc2, L3_gnn_Ws_l2_a, L3_gnn_Wv_l2_a, L3_gnn_Ws_l2_c, L3_gnn_Wv_l2_c, L3_gnn_Ws_l3, L3_gnn_Wv_l3):
    import jax
    import jax.numpy as jnp

    def _L0_gnn_ref(node_features, edge_index, edge_attr_tensor, node_attr_scalar_raw, Wm_ss, Wm_vv, Wm_sv, Wm_vs, Lm_s, Lm_v, Wu_ss, Wu_vv, Wu_sv, Wu_vs, Lu_s, Lu_v):
        import jax, jax.numpy as jnp
        import numpy as np
        N = 20000
        E = 10000
        INV_SQRT3 = 0.5773502691896258
        INV8 = 0.125
        INV_SQRT32 = 0.17677669529663687
        INV64 = 0.015625
        INV32 = 0.03125
        INV_SQRT2048 = 0.022097086912079608
        n = node_features.shape[0]
        e = edge_attr_tensor.shape[0]
        row, col = (edge_index[0], edge_index[1])
        r_vec = edge_attr_tensor[:, :3]
        dist = edge_attr_tensor[:, 3:4]
        xj = node_features[col]
        s = xj[:, :64]
        v = xj[:, 64:].reshape(e, 32, 3)
        m0 = s @ Wm_ss * dist * INV8 + jnp.einsum('eui,ei->eu', v, r_vec) @ Wm_vv * (INV_SQRT3 * INV_SQRT32)
        m1 = (s @ Wm_sv)[:, :, None] * r_vec[:, None, :] * INV8 + jnp.einsum('eui,uw->ewi', v, Wm_vs) * dist[:, :, None] * INV_SQRT32
        m0 = m0 + s @ Lm_s * INV8
        m1 = m1 + jnp.einsum('eui,uw->ewi', v, Lm_v) * INV_SQRT32
        msg = jnp.concatenate([m0, m1.reshape(e, 96)], axis=-1)
        agg = jax.ops.segment_sum(msg, row, num_segments=n)
        a0 = agg[:, :64]
        a1 = agg[:, 64:].reshape(n, 32, 3)
        xs = node_features[:, :64]
        xv = node_features[:, 64:].reshape(n, 32, 3)
        u0 = jnp.einsum('nu,nv,uvw->nw', xs, a0, Wu_ss) * INV64 + jnp.einsum('nui,nvi,uvw->nw', xv, a1, Wu_vv) * (INV_SQRT3 * INV32)
        u1 = jnp.einsum('nu,nvi,uvw->nwi', xs, a1, Wu_sv) * INV_SQRT2048 + jnp.einsum('nui,nv,uvw->nwi', xv, a0, Wu_vs) * INV_SQRT2048
        u0 = u0 + xs @ Lu_s * INV8
        u1 = u1 + jnp.einsum('nui,uw->nwi', xv, Lu_v) * INV_SQRT32
        upd = jnp.concatenate([u0, u1.reshape(n, 96)], axis=-1)
        return node_features + upd

    def _L1_gnn_ref(node_feature, edge_attr, edge_feature, W_skip0, W_skip1, W_nl0, W_nl1, W_fc1, W_fc2, W_out_s, W_out_v, edge_index):
        import jax, jax.numpy as jnp
        import numpy as np
        N_NODES = 10000
        N_EDGES = 5000
        MUL0, MUL1 = (64, 32)
        EDGE_DIM = 64
        W_NUMEL = 224
        DENOM = 32.0
        SQRT3 = 3.0 ** 0.5
        INV_SQRT3 = 1.0 / SQRT3
        INV_SQRT2 = 2.0 ** (-0.5)

        def _forward(node_feature, edge_attr, edge_feature, W_skip0, W_skip1, W_nl0, W_nl1, W_fc1, W_fc2, W_out_s, W_out_v, edge_index):
            N = node_feature.shape[0]
            E = edge_attr.shape[0]
            s = node_feature[:, :MUL0]
            v = node_feature[:, MUL0:].reshape(N, MUL1, 3)
            skip_s = s @ W_skip0
            skip_v = jnp.einsum('nmi,mk->nki', v, W_skip1)
            s = s @ W_nl0
            v = jnp.einsum('nmi,mk->nki', v, W_nl1)
            rhat = edge_attr / jnp.linalg.norm(edge_attr, axis=-1, keepdims=True)
            sh1 = SQRT3 * rhat
            w = jax.nn.relu(edge_feature @ W_fc1) @ W_fc2
            w0, w1, w2, w3, w4 = jnp.split(w, [64, 128, 160, 192], axis=-1)
            src, dst = (edge_index[0], edge_index[1])
            xs = s[dst]
            xv = v[dst]
            out0a = w0 * xs
            out0b = w3 * (jnp.einsum('emi,ei->em', xv, sh1) * INV_SQRT3)
            out1a = (w1 * xs)[:, :, None] * sh1[:, None, :]
            out1b = w2[:, :, None] * xv
            out1c = w4[:, :, None] * (jnp.cross(xv, sh1[:, None, :]) * INV_SQRT2)
            tp = jnp.concatenate([out0a, out0b, out1a.reshape(E, -1), out1b.reshape(E, -1), out1c.reshape(E, -1)], axis=-1)
            agg = jax.ops.segment_sum(tp, src, num_segments=N) / DENOM
            agg_s = agg[:, :96]
            agg_v = agg[:, 96:].reshape(N, 128, 3)
            out_s = agg_s @ W_out_s + skip_s
            out_v = jnp.einsum('nmi,mk->nki', agg_v, W_out_v) + skip_v
            fs = jax.nn.silu(out_s[:, :MUL0])
            gate = jax.nn.sigmoid(out_s[:, MUL0:MUL0 + 32])
            gv = gate[:, :, None] * out_v
            return jnp.concatenate([fs, gv.reshape(N, -1)], axis=-1)
        return _forward(node_feature, edge_attr, edge_feature, W_skip0, W_skip1, W_nl0, W_nl1, W_fc1, W_fc2, W_out_s, W_out_v, edge_index)

    def _L2_gnn_ref(x, edge_index, edge_feat, edge_scalars, W_ss, W_sv, W_vs, W_vv, W_rad, b_rad, L_s, L_v):
        import jax, jax.numpy as jnp
        import numpy as np
        N_NODES = 100000
        N_EDGES = 12500
        MUL_S = 64
        MUL_V = 32
        DIM = MUL_S + 3 * MUL_V
        EDGE_SCALAR_DIM = 16
        ISQ3 = 1.0 / np.sqrt(3.0)
        ISQ2 = 1.0 / np.sqrt(2.0)

        def _forward(x, edge_index, edge_feat, edge_scalars, W_ss, W_sv, W_vs, W_vv, W_rad, b_rad, L_s, L_v):
            src, dst = (edge_index[0], edge_index[1])
            n = x.shape[0]
            xs = x[:, :MUL_S]
            xv = x[:, MUL_S:].reshape(n, MUL_V, 3)
            xs_e = xs[src]
            xv_e = xv[src]
            es = edge_feat[:, 0]
            ev = edge_feat[:, 1:4]
            out_s = (jnp.einsum('eu,uo->eo', xs_e * es[:, None], W_ss) / np.sqrt(MUL_S) + jnp.einsum('eud,ed,uo->eo', xv_e, ev, W_vv) * ISQ3 / np.sqrt(MUL_V)) * ISQ2
            out_v = (jnp.einsum('eu,ed,uv->evd', xs_e, ev, W_sv) * ISQ3 / np.sqrt(MUL_S) + jnp.einsum('eud,e,uv->evd', xv_e, es, W_vs) * ISQ3 / np.sqrt(MUL_V)) * ISQ2
            messages = jnp.concatenate([out_s, out_v.reshape(-1, 3 * MUL_V)], axis=1)
            scale = jax.nn.sigmoid(edge_scalars @ W_rad.T + b_rad)
            messages = messages * scale
            agg = jax.ops.segment_sum(messages, dst, num_segments=n)
            h = x + agg
            hs = h[:, :MUL_S]
            hv = h[:, MUL_S:].reshape(n, MUL_V, 3)
            ys = hs @ L_s / np.sqrt(MUL_S)
            yv = jnp.einsum('nud,uv->nvd', hv, L_v) / np.sqrt(MUL_V)
            return jnp.concatenate([ys, yv.reshape(n, 3 * MUL_V)], axis=1)
        return _forward(x, edge_index, edge_feat, edge_scalars, W_ss, W_sv, W_vs, W_vv, W_rad, b_rad, L_s, L_v)

    def _L3_gnn_ref(node_input, node_attr, node_crystal_attr, sym_mask, edge_attr, edge_length_embedded, edge_src, edge_dst, Ws_sc_a, Wv_sc_a, Ws_sc_c, Wv_sc_c, Ws_l1_a, Wv_l1_a, Ws_l1_c, Wv_l1_c, W_fc1, W_fc2, Ws_l2_a, Wv_l2_a, Ws_l2_c, Wv_l2_c, Ws_l3, Wv_l3):
        import jax, jax.numpy as jnp
        import numpy as np
        N = 25000
        E = 6250
        S = 64
        V = 32
        NB = 10
        H = 100
        WN = 192
        MID = 96
        NUM_NEIGHBORS = 16.0
        C_S = float(np.sin(np.pi / 8.0))
        C_X = float(np.cos(np.pi / 8.0))
        SQRT3 = float(np.sqrt(3.0))

        def fctp_scalar_attr(xs, xv, attr, Ws, Wv):
            s = xs * attr @ Ws
            v = jnp.einsum('nuc,uo->noc', xv * attr[:, :, None], Wv)
            return (s, v)
        n = node_input.shape[0]
        xs = node_input[:, :S]
        xv = node_input[:, S:].reshape(n, V, 3)
        ssa, sva = fctp_scalar_attr(xs, xv, node_attr, Ws_sc_a, Wv_sc_a)
        ssc, svc = fctp_scalar_attr(xs, xv, node_crystal_attr, Ws_sc_c, Wv_sc_c)
        s_s, s_v = (ssa + ssc, sva + svc)
        l1a_s, l1a_v = fctp_scalar_attr(xs, xv, node_attr, Ws_l1_a, Wv_l1_a)
        l1c_s, l1c_v = fctp_scalar_attr(xs, xv, node_crystal_attr, Ws_l1_c, Wv_l1_c)
        x1s, x1v = (l1a_s + l1c_s, l1a_v + l1c_v)
        weight = jax.nn.silu(edge_length_embedded @ W_fc1) @ W_fc2
        w0 = weight[:, :S]
        w1 = weight[:, S:2 * S]
        w2 = weight[:, 2 * S:2 * S + V]
        w3 = weight[:, 2 * S + V:]
        gs = x1s[edge_src]
        gv = x1v[edge_src]
        e_s = edge_attr[:, :1]
        e_v = edge_attr[:, 1:]
        mid0a = w0 * gs * e_s
        mid0b = w3 * (jnp.einsum('euc,ec->eu', gv, e_v) / SQRT3)
        mid1a = w1[:, :, None] * gs[:, :, None] * e_v[:, None, :]
        mid1b = w2[:, :, None] * gv * e_s[:, :, None]
        edge_feat = jnp.concatenate([mid0a, mid0b, mid1a.reshape(-1, 3 * S), mid1b.reshape(-1, 3 * V)], axis=-1)
        agg = jax.ops.segment_sum(edge_feat, edge_dst, num_segments=n) / np.sqrt(NUM_NEIGHBORS)
        m_s = agg[:, :MID]
        m_v = agg[:, MID:].reshape(n, MID, 3)
        l2a_s, l2a_v = fctp_scalar_attr(m_s, m_v, node_attr, Ws_l2_a, Wv_l2_a)
        l2c_s, l2c_v = fctp_scalar_attr(m_s, m_v, node_crystal_attr, Ws_l2_c, Wv_l2_c)
        m_s, m_v = (l2a_s + l2c_s, l2a_v + l2c_v)
        o_s, o_v = fctp_scalar_attr(m_s, m_v, sym_mask, Ws_l3, Wv_l3)
        out_s = C_S * s_s + C_X * o_s
        out_v = C_S * s_v + C_X * o_v
        return jnp.concatenate([out_s, out_v.reshape(n, 3 * V)], axis=-1)
    edge_index = jnp.stack([src, dst])
    h = jnp.maximum(_layernorm(x, axis=-1), 0.0)
    x = x + _L0_gnn_ref(h, edge_index, edge_attr_4, node_vec1, L0_gnn_Wm_ss, L0_gnn_Wm_vv, L0_gnn_Wm_sv, L0_gnn_Wm_vs, L0_gnn_Lm_s, L0_gnn_Lm_v, L0_gnn_Wu_ss, L0_gnn_Wu_vv, L0_gnn_Wu_sv, L0_gnn_Wu_vs, L0_gnn_Lu_s, L0_gnn_Lu_v)
    h = jnp.maximum(_layernorm(x, axis=-1), 0.0)
    x = x + _L1_gnn_ref(h, edge_attr_3, edge_attr_64, L1_gnn_W_skip0, L1_gnn_W_skip1, L1_gnn_W_nl0, L1_gnn_W_nl1, L1_gnn_W_fc1, L1_gnn_W_fc2, L1_gnn_W_out_s, L1_gnn_W_out_v, edge_index)
    h = jnp.maximum(_layernorm(x, axis=-1), 0.0)
    x = x + _L2_gnn_ref(h, edge_index, edge_attr_4, edge_attr_16, L2_gnn_W_ss, L2_gnn_W_sv, L2_gnn_W_vs, L2_gnn_W_vv, L2_gnn_W_rad, L2_gnn_b_rad, L2_gnn_L_s, L2_gnn_L_v)
    h = jnp.maximum(_layernorm(x, axis=-1), 0.0)
    x = x + _L3_gnn_ref(h, node_vec1, node_vec1_n2, node_vec1_n3, edge_attr_4, edge_attr_10, src, dst, L3_gnn_Ws_sc_a, L3_gnn_Wv_sc_a, L3_gnn_Ws_sc_c, L3_gnn_Wv_sc_c, L3_gnn_Ws_l1_a, L3_gnn_Wv_l1_a, L3_gnn_Ws_l1_c, L3_gnn_Wv_l1_c, L3_gnn_W_fc1, L3_gnn_W_fc2, L3_gnn_Ws_l2_a, L3_gnn_Wv_l2_a, L3_gnn_Ws_l2_c, L3_gnn_Wv_l2_c, L3_gnn_Ws_l3, L3_gnn_Wv_l3)
    return x

_drawn_inputs = setup_inputs


def setup_inputs(seed=0):
    import zlib

    import numpy as np

    out = dict(_drawn_inputs(seed))
    spreads = {}
    factors = {'edge_attr_10': 4.395,
     'edge_attr_3': 8.0,
     'edge_attr_64': 8.0,
     'L1_gnn_W_nl0': 8.0,
     'L1_gnn_W_nl1': 8.0,
     'L1_gnn_W_fc1': 8.0,
     'L1_gnn_W_fc2': 8.0,
     'L1_gnn_W_out_s': 8.0,
     'L1_gnn_W_out_v': 8.0,
     'L2_gnn_b_rad': 200.0,
     'L3_gnn_Ws_l1_a': 3.738,
     'L3_gnn_Wv_l1_a': 5.34,
     'L3_gnn_Ws_l1_c': 3.559,
     'L3_gnn_Wv_l1_c': 4.937,
     'L3_gnn_Ws_l2_a': 4.733,
     'L3_gnn_Wv_l2_a': 13.674,
     'L3_gnn_Ws_l2_c': 4.8,
     'L3_gnn_Wv_l2_c': 13.094,
     'L3_gnn_Ws_l3': 3.383,
     'edge_attr_16': 8.0,
     'L1_gnn_W_skip0': 7.102,
     'L1_gnn_W_skip1': 22.491,
     'L2_gnn_W_ss': 8.0,
     'L2_gnn_W_sv': 8.0,
     'L2_gnn_W_vs': 8.0,
     'L2_gnn_W_vv': 8.0,
     'L2_gnn_W_rad': 8.0,
     'L2_gnn_L_s': 8.0,
     'L2_gnn_L_v': 8.0,
     'L3_gnn_Ws_sc_a': 55.753,
     'L3_gnn_Wv_sc_a': 64.0,
     'L3_gnn_Ws_sc_c': 54.744,
     'L3_gnn_Wv_sc_c': 64.0,
     'L3_gnn_Wv_l3': 2.816}
    for name, (base, spread) in spreads.items():
        noise = np.random.default_rng([zlib.crc32(name.encode()), seed]).standard_normal(out[name].shape)
        drawn = base * np.exp(spread * noise) if base else spread * noise
        out[name] = jnp.asarray(drawn.astype(out[name].dtype))
    for name, factor in factors.items():
        out[name] = (out[name] * factor).astype(out[name].dtype)
    return out
```

```python
from contextlib import ExitStack

import numpy as np

import concourse.bass as bass
from concourse import mybir

F32 = mybir.dt.float32
I32 = mybir.dt.int32
ALU = mybir.AluOpType
ACT = mybir.ActivationFunctionType
AX_X = mybir.AxisListType.X

P = 128
S, V = 64, 32
D = S + 3 * V
G = 4
NB = 6
EPS = 1e-5

EA10, EA4, EA16, EA3, EA64, EAW = 0, 10, 14, 30, 33, 97
K_IDENT, K_LOWER, K_JUNK, K_EPS, K_WIDTH = 0, P, 2 * P, 2 * P + 1, 2 * P + 2

INV_SQRT3 = 3.0 ** -0.5
INV_SQRT32 = 32.0 ** -0.5
INV_SQRT2 = 2.0 ** -0.5
C_S = float(np.sin(np.pi / 8.0))
C_X = float(np.cos(np.pi / 8.0))


def weight_blocks():
    def one(r, c, scale=1.0):
        return (r, c, [(0, r, 0, c, scale)])
    msg_v = INV_SQRT3 * INV_SQRT32
    return {
        "u_ss": one(P, 2048, 1 / 64), "u_vv": one(P, 512, INV_SQRT3 / 32),
        "u_sv": one(S, 1024, 2048.0 ** -0.5), "u_vs": one(S, 1024, 2048.0 ** -0.5),
        "m_a": one(P, S, 0.125), "m_c": one(V, S, msg_v),
        "m_b": (P, V, [(0, S, 0, V, 0.125), (S, P, 0, V, INV_SQRT32)]),
        "lu_s": one(S, S, 0.125), "lu_v": one(96, 96, INV_SQRT32),
        "skip_s": one(S, 96), "skip_v": one(96, 96), "nl_s": one(S, S), "nl_v": one(96, 96),
        "fc1": one(64, 64), "fc2": one(64, 224), "out_s": one(96, 96, 1 / 32),
        "out_v": (P, V, [(0, 96, 0, V, 1 / 32), (96, P, 0, V, INV_SQRT2 / 32)]),
        "l2_s": (96, S, [(0, S, 0, S, INV_SQRT2 / 8), (S, 96, 0, S, msg_v * INV_SQRT2)]),
        "l2_v": (96, V, [(0, S, 0, V, INV_SQRT3 / 8 * INV_SQRT2), (S, 96, 0, V, msg_v * INV_SQRT2)]),
        "rad": one(17, D), "l2l_s": one(S, S, 0.125), "l2l_v": one(96, 96, INV_SQRT32),
        "sc_s": one(S, 2 * S, C_S), "sc_v": one(96, 192, C_S), "l1_s": one(S, 2 * S), "l1_v": one(96, 192),
        "fcr1": one(10, 100), "fcr2": one(100, 192),
        "l2aT_s": (96, 96, [(0, 96, 0, 64, 1.0), (0, 96, 64, 96, INV_SQRT3)]),
        "l2cT_s": (96, 96, [(0, 96, 0, 64, 1.0), (0, 96, 64, 96, INV_SQRT3)]),
        "l2aT_v": one(96, 96), "l2cT_v": one(96, 96),
        "l3_s": one(96, S, C_X / 4), "l3_v": one(96, V, C_X / 4),
    }


def weight_columns():
    at, start = 0, {}
    for name, (_, cols, _) in weight_blocks().items():
        start[name] = at
        at += cols
    return start, at


class Tile:

    def __init__(self, n, slot, turn, rows):
        self.n, self.slot, self.turn, self.rows = n, slot, turn, rows


def sweep(eng, total, full, last_rows, deepest, step):
    def straight(k):
        def tile(lag):
            n = k - lag
            if n < 0 or n >= total:
                return None
            return Tile(n, n % NB, n // NB, P if n < full else last_rows)
        step(tile)

    first = NB * (-(-(deepest + NB) // NB))
    turns = max(0, (full - first) // NB)
    if turns < 2:
        turns = 0
    else:
        for k in range(first):
            straight(k)
        with eng.Fori(0, turns) as j:
            for u in range(NB):
                def tile(lag, k=first + u):
                    n = k - lag
                    return Tile(j * NB + n, n % NB, j + n // NB, P)
                step(tile)
    for k in range(first + turns * NB if turns else 0, total + deepest):
        straight(k)


def positive(count):
    return not isinstance(count, int) or count > 0


def repeat(ap, axis, n):
    shape = list(ap.shape)
    shape.insert(axis, n)
    return ap.unsqueeze(axis).broadcast_to(shape)


def build(nc, N, E, x, idx2, idx2T, ea, nattr, wpack, wscale, consts, out):
    NJ = N + P
    tiles, full_tiles = -(-E // P), E // P
    last_edges = E - (tiles - 1) * P
    groups, full_groups = -(-N // (P * G)), N // (P * G)
    last_parts = (N - (groups - 1) * P * G) // G
    assert N == E * G
    WCOL, WWIDTH = weight_columns()
    BLOCKS = weight_blocks()

    def table(name, cols, rows=NJ, dt=F32):
        return nc.dram_tensor(name, (rows, cols), dt, kind="Internal").ap()

    x1, p1, h2, x3, t3 = table("x1", D), table("p1", 192), table("h2", D, N), table("x3", D), table("t3", D)
    same = table("same", 2 * P, tiles * P)
    unique = table("unique", 2, tiles * P, I32)

    outer = ExitStack()
    with outer:
        def sem(name):
            return nc.alloc_semaphore(name=name)

        def ring_sems(name, n=NB):
            return [sem(f"{name}{i}") for i in range(n)]

        W = outer.enter_context(nc.sbuf_tensor("W", [P, WWIDTH], F32))
        K = outer.enter_context(nc.sbuf_tensor("K", [P, K_WIDTH], F32))
        WLs = outer.enter_context(nc.sbuf_tensor("WLs", [96, 2 * S], F32))
        WLv = outer.enter_context(nc.sbuf_tensor("WLv", [96, 2 * V], F32))
        ident = K[:, K_IDENT:K_IDENT + P]
        lower = K[:, K_LOWER:K_LOWER + P]
        junk = K[:, K_JUNK:K_JUNK + 1]
        epsilon = K[:, K_EPS:K_EPS + 1]

        def w(name):
            r, c, _ = BLOCKS[name]
            return W[0:r, WCOL[name]:WCOL[name] + c]

        with nc.cleanup_on_exit(), ExitStack() as ph:
            scale = ph.enter_context(nc.sbuf_tensor("scale", [P, WWIDTH], F32))
            zero = ph.enter_context(nc.sbuf_tensor("zero", [P, 192], F32))
            pl = ph.enter_context(nc.psum_tensor("pl", [P, 512], F32))
            weights_in, zeroed, junk_clean = sem("weights_in"), sem("zeroed"), sem("junk_clean")
            scaled, folded, folded_out, with_identity = sem("scaled"), sem("folded"), sem("folded_out"), sem("with_identity")
            block = ph.enter_context(nc.Block())

            @block.sync
            def _(sp):
                sp.dma_start(W[:, :], wpack).then_inc(weights_in, 16)
                sp.dma_start(scale[:, :], wscale).then_inc(weights_in, 16)
                sp.dma_start(K[:, :], consts).then_inc(weights_in, 16)
                sp.wait_ge(zeroed, 1)
                for t in (x1, p1, x3, t3):
                    sp.dma_start(t[N:NJ, :], zero[:, 0:t.shape[1]]).then_inc(junk_clean, 16)
                sp.wait_ge(junk_clean, 64)

            @block.vector
            def _(dve):
                nc.vector.memset(zero[:, :], 0.0).then_inc(zeroed, 1)
                dve.wait_ge(weights_in, 48)
                nc.vector.tensor_tensor(W[:, :], W[:, :], scale[:, :], ALU.mult).then_inc(scaled, 1)
                dve.wait_ge(scaled, 1)
                nc.vector.tensor_tensor(w("lu_s"), w("lu_s"), ident[0:S, 0:S], ALU.add).then_inc(with_identity, 1)
                nc.vector.tensor_tensor(w("lu_v"), w("lu_v"), ident[0:96, 0:96], ALU.add).then_inc(with_identity, 1)
                dve.wait_ge(folded, 1)
                nc.vector.tensor_copy(WLs[:, :], pl[0:96, 0:2 * S]).then_inc(folded_out, 1)
                nc.vector.tensor_copy(WLv[:, :], pl[0:96, 2 * S:2 * S + 2 * V]).then_inc(folded_out, 1)
                dve.wait_ge(folded_out, 2)
                dve.wait_ge(with_identity, 2)

            @block.tensor
            def _(pe):
                pe.wait_ge(scaled, 1)
                for n, (a, b, at, m) in enumerate((("l2aT_s", "l3_s", 0, S), ("l2cT_s", "l3_s", S, S),
                                                   ("l2aT_v", "l3_v", 2 * S, V), ("l2cT_v", "l3_v", 2 * S + V, V))):
                    mm = nc.tensor.matmul(pl[0:96, at:at + m], w(a), w(b), start=True, stop=True)
                mm.then_inc(folded, 1)

        NEWTON = 10

        def inverse_root(dve, t, steps, v, bits, tmp, y, at):
            if at:
                if positive(t.n * (NEWTON + 1) + at):
                    dve.wait_ge(steps, t.n * (NEWTON + 1) + at)
            if at == 0:
                ins = nc.vector.tensor_scalar(bits, v.bitcast(I32), 1, None, ALU.logical_shift_right)
            elif at == 1:
                ins = nc.vector.tensor_scalar(y.bitcast(I32), bits, -1.0, float(0x5F3759DF), ALU.mult, ALU.add)
            elif at % 3 == 2:
                ins = nc.vector.scalar_tensor_tensor(tmp, y, -0.5, y, ALU.mult, ALU.mult)
            elif at % 3 == 0:
                ins = nc.vector.tensor_tensor(tmp, tmp, v, ALU.mult)
            else:
                ins = nc.vector.scalar_tensor_tensor(y, tmp, 1.5, y, ALU.add, ALU.mult)
            ins.then_inc(steps, 1)

        class Norm:

            def __init__(self, ph, tag, parts, newton=False):
                def sb(name, shape, dt=F32):
                    return ph.enter_context(nc.sbuf_tensor(f"{tag}_{name}", shape, dt))
                self.parts = parts
                self.bn, self.mv = sb("bn", [P, 2, parts, 6]), sb("mv", [P, NB, parts, 2])
                self.var, self.tmp, self.bits = sb("var", [P, NB, parts]), sb("tmp", [P, parts]), sb("bits", [P, parts], I32)
                self.rstd, self.shift = sb("rstd", [P, NB, parts]), sb("shift", [P, NB, parts])
                self.stats, self.moments = sem(f"{tag}_stats"), sem(f"{tag}_moments")
                self.widened, self.steps, self.inverted = sem(f"{tag}_widened"), sem(f"{tag}_steps"), sem(f"{tag}_inverted")
                self.passed = sem(f"{tag}_dve_passed")
                self.ready, self.done = sem(f"{tag}_norm_ready"), sem(f"{tag}_norm_done")

            def statistics(self, dve, t, views):
                n, b = t.rows, t.slot
                if positive(t.n - (NB - 1)):
                    dve.wait_ge(self.done, t.n - (NB - 1))
                for q, v in enumerate(views):
                    ins = nc.vector.bn_stats(self.bn[0:n, b % 2, q, :], v)
                ins.then_inc(self.stats, 1)
                dve.wait_ge(self.stats, t.n + 1)
                dve.sem_inc(self.passed, 1)
                for q in range(self.parts):
                    ins = nc.vector.bn_aggr(self.mv[0:n, b, q, :], self.bn[0:n, b % 2, q, :])
                ins.then_inc(self.moments, 1)

            def root(self, act, t):
                n, b = t.rows, t.slot
                act.wait_ge(self.moments, t.n + 1)
                nc.scalar.activation(self.var[0:n, b, :], self.mv[0:n, b, :, 1], ACT.Sqrt, bias=epsilon[0:n, :])\
                    .then_inc(self.widened, 1)

            def scales(self, dve, t):
                n, b = t.rows, t.slot
                dve.wait_ge(self.widened, t.n + 1)
                nc.vector.reciprocal(self.rstd[0:n, b, :], self.var[0:n, b, :]).then_inc(self.inverted, 1)
                dve.wait_ge(self.inverted, t.n + 1)
                self.shifts(dve, t)

            def widen(self, dve, t):
                n, b = t.rows, t.slot
                dve.wait_ge(self.moments, t.n + 1)
                nc.vector.tensor_scalar(self.var[0:n, b, :], self.mv[0:n, b, :, 1], EPS, None, ALU.add).then_inc(self.widened, 1)
                dve.wait_ge(self.widened, t.n + 1)

            def newton(self, dve, t, at):
                n, b = t.rows, t.slot
                inverse_root(dve, t, self.steps, self.var[0:n, b, :], self.bits[0:n], self.tmp[0:n], self.rstd[0:n, b, :], at)

            def on_vector(self, dve, t, views):
                self.statistics(dve, t, views)
                self.widen(dve, t)
                for at in range(NEWTON + 1):
                    self.newton(dve, t, at)
                self.newton_shifts(dve, t)

            def newton_shifts(self, dve, t):
                if positive((t.n + 1) * (NEWTON + 1)):
                    dve.wait_ge(self.steps, (t.n + 1) * (NEWTON + 1))
                self.shifts(dve, t)

            def shifts(self, dve, t):
                n, b = t.rows, t.slot
                nc.vector.scalar_tensor_tensor(self.shift[0:n, b, :], self.mv[0:n, b, :, 0], -1.0, self.rstd[0:n, b, :],
                                               ALU.mult, ALU.mult).then_inc(self.ready, 1)

            def map(self, t, out_ap, in_ap, q):
                n, b = t.rows, t.slot
                return nc.scalar.activation(out_ap, in_ap, ACT.Relu, bias=self.shift[0:n, b, q:q + 1],
                                            scale=self.rstd[0:n, b, q:q + 1])

        def rows_of(tab, t):
            return tab[bass.ds(t.n * (P * G), t.rows * G), :].rearrange("(p g) c -> p g c", g=G)

        def dense_phase(tag, kind):
            newton = kind == 2
            STATS = 3 if kind == 2 else 1
            MAP = STATS + (1 if newton else 2)
            TURN, MUL, STORE = MAP + 1, MAP + 2, MAP + 3
            source = (x, x1, x1, x3)[kind]
            width = (D, 192, D, 2 * D)[kind]
            banks = 4 if kind == 3 else 2
            per_bank = G // banks
            weights = (("lu_s", "lu_v"), ("skip_s", "skip_v"), ("l2l_s", "l2l_v"), ("sc_s", "sc_v"))[kind]
            sums = 1 if kind == 3 else 2
            loads = (1, 1, 2, 3)[kind]
            with nc.cleanup_on_exit(), ExitStack() as ph:
                def sb(name, shape, dt=F32):
                    return ph.enter_context(nc.sbuf_tensor(f"{tag}_{name}", shape, dt))
                X, H = sb("X", [P, NB, G, D]), sb("H", [P, NB, G, D])
                HsT, HvT = sb("HsT", [S, 2, 512]), sb("HvT", [96, 2, 512])
                Y = sb("Y", [P, NB, G, 192 if kind == 1 else D])
                if kind == 0:
                    col, row = sb("col", [P, NB, 2], I32), sb("row", [P, NB, 2, P], I32)
                    eq, early = sb("eq", [P, NB, 2, P]), sb("early", [P, 2, 2, P])
                    off, rep, moved = sb("off", [P, 2]), sb("rep", [P, 2]), sb("moved", [P, 2])
                    uniq = sb("uniq", [P, NB, 2], I32)
                    index_in, index_stored = ring_sems("ix_in"), ring_sems("ix_stored")
                    ix = {n: sem("ix_" + n) for n in ("compared", "masked", "counted", "offset", "moved", "ready")}
                if kind == 2:
                    Pt, Gt, X2 = sb("Pt", [P, NB, G, 192]), sb("Gt", [P, 2, G, 96]), sb("X2", [P, NB, G, D])
                if kind == 3:
                    T3, NA, XT = sb("T3", [P, NB, G, D]), sb("NA", [P, NB, G, 3]), sb("XT", [P, NB, G, D])
                    A1 = sb("A1", [P, 2, G, D])
                psS = ph.enter_context(nc.psum_tensor(f"{tag}_psS", [P, 2, 512], F32))
                psV = ph.enter_context(nc.psum_tensor(f"{tag}_psV", [P, 2, 512], F32))
                psO = ph.enter_context(nc.psum_tensor(f"{tag}_psO", [P, sums, banks, 512], F32))
                norm = Norm(ph, tag, G)
                loaded, stored = ring_sems(f"{tag}_loaded"), ring_sems(f"{tag}_stored")
                turned, s_out, v_out = sem(f"{tag}_turned"), sem(f"{tag}_s_out"), sem(f"{tag}_v_out")
                product, summed = sem(f"{tag}_product"), sem(f"{tag}_summed")
                if kind >= 2:
                    gates, gated, residual_ready, part_a = (sem(f"{tag}_{n}") for n in ("gates", "gated", "residual_ready", "part_a"))
                block = ph.enter_context(nc.Block())

                @block.sync
                def _(sp):
                    def step(tile):
                        t = tile(0)
                        if t:
                            n, b = t.rows, t.slot
                            if kind == 1:
                                if positive(t.n - (NB - 1)):
                                    sp.wait_ge(norm.done, t.n - (NB - 1))
                            if kind >= 2:
                                if positive(t.n - (NB - 1)):
                                    sp.wait_ge(residual_ready, t.n - (NB - 1))
                            if kind == 3:
                                if positive(t.n - (NB - 1)):
                                    sp.wait_ge(norm.done, t.n - (NB - 1))
                            if kind in (0, 3):
                                if positive(t.n - (NB - 1)):
                                    sp.wait_ge(summed, t.n - (NB - 1))
                            sp.dma_start(X[0:n, b, :, :], rows_of(source, t)).then_inc(loaded[b], 16)
                            if kind == 2:
                                sp.dma_start(Pt[0:n, b, :, :], rows_of(p1, t)).then_inc(loaded[b], 16)
                            if kind == 3:
                                sp.dma_start(T3[0:n, b, :, :], rows_of(t3, t)).then_inc(loaded[b], 16)
                                sp.dma_start(NA[0:n, b, :, :], rows_of(nattr, t)).then_inc(loaded[b], 16)
                        t = tile(STORE)
                        if t:
                            n, b = t.rows, t.slot
                            sp.wait_ge(summed, t.n + 1)
                            target = (x1, p1, x3, out)[kind]
                            sp.dma_start(rows_of(target, t), Y[0:n, b, :, :]).then_inc(stored[b], 16)
                            if kind == 2:
                                sp.dma_start(rows_of(h2, t), H[0:n, b, :, :]).then_inc(stored[b], 16)
                        if kind == 0:
                            index_step(tile)

                    def index_step(tile):
                        t = tile(0)
                        if t:
                            n, b = t.rows, t.slot
                            if positive(t.n - (NB - 1)):
                                sp.wait_ge(ix["ready"], t.n - (NB - 1))
                            sp.dma_start(col[0:n, b, :], idx2[bass.ds(t.n * P, n), :]).then_inc(index_in[b], 16)
                            for a in range(2):
                                sp.dma_start(row[0:n, b, a, 0:n], idx2T[a:a + 1, bass.ds(t.n * P, n)].broadcast_to([n, n]))\
                                  .then_inc(index_in[b], 16)
                        t = tile(5)
                        if t:
                            n, b = t.rows, t.slot
                            sp.wait_ge(ix["ready"], t.n + 1)
                            sp.dma_start(unique[bass.ds(t.n * P, n), :], uniq[0:n, b, :]).then_inc(index_stored[b], 16)
                            sp.dma_start(same[bass.ds(t.n * P, n), :].rearrange("p (a q) -> p a q", a=2)[:, :, 0:n],
                                         eq[0:n, b, :, 0:n]).then_inc(index_stored[b], 16)
                    sweep(sp, groups, full_groups, last_parts, STORE, step)
                    for b in range(NB):
                        sp.wait_ge(stored[b], (32 if kind == 2 else 16) * ((groups - 1 - b) // NB + 1))
                        if kind == 0:
                            sp.wait_ge(index_stored[b], 32 * ((tiles - 1 - b) // NB + 1))

                @block.scalar
                def _(act):
                    def step(tile):
                        t = tile(MAP)
                        if t:
                            n, b = t.rows, t.slot
                            act.wait_ge(norm.ready, t.n + 1)
                            if kind == 2:
                                if positive(t.turn):
                                    act.wait_ge(stored[t.slot], t.turn * 32)
                            else:
                                if positive(t.n - (NB - 1)):
                                    act.wait_ge(turned, t.n - (NB - 1))
                            src = X2 if kind == 2 else X
                            for q in range(G):
                                ins = norm.map(t, H[0:n, b, q, :], src[0:n, b, q, :], q)
                            ins.then_inc(norm.done, 1)
                        t = tile(STATS + 1)
                        if t and not newton:
                            norm.root(act, t)
                        t = tile(1)
                        if t and kind == 2:
                            n, b = t.rows, t.slot
                            act.wait_ge(loaded[t.slot], (t.turn + 1) * (16 * (loads)))
                            if positive(t.n - 1):
                                act.wait_ge(gated, t.n - 1)
                            nc.scalar.activation(Gt[0:n, b % 2, :, :], Pt[0:n, b, :, 0:96], ACT.Sigmoid)\
                                .then_inc(gates, 1)
                        t = tile(TURN)
                        if t:
                            b = t.slot % 2
                            act.wait_ge(turned, t.n + 1)
                            if positive(t.n - 1):
                                act.wait_ge(product, t.n - 1)
                            nc.scalar.copy(HvT[:, b, 0:G * t.rows], psV[0:96, b, 0:G * t.rows]).then_inc(v_out, 1)
                            nc.scalar.copy(HsT[:, b, 0:G * t.rows], psS[0:S, b, 0:G * t.rows]).then_inc(s_out, 1)
                    sweep(act, groups, full_groups, last_parts, STORE, step)

                @block.tensor
                def _(pe):
                    ws, wv = w(weights[0]), w(weights[1])
                    if kind == 3:
                        ws, wv = ws.rearrange("p (k c) -> p k c", k=2), wv.rearrange("p (k c) -> p k c", k=2)

                    def step(tile):
                        t = tile(TURN)
                        if t:
                            n, b = t.rows, t.slot
                            pe.wait_ge(norm.done, t.n + 1)
                            if positive(t.n - 1):
                                pe.wait_ge(s_out, t.n - 1)
                            if positive(t.n - 1):
                                pe.wait_ge(v_out, t.n - 1)
                            for q in range(G):
                                nc.tensor.transpose(psV[0:96, b % 2, q * n:(q + 1) * n], H[0:n, b, q, S:D], ident[0:n, 0:n])
                                tr = nc.tensor.transpose(psS[0:S, b % 2, q * n:(q + 1) * n], H[0:n, b, q, 0:S], ident[0:n, 0:n])
                            tr.then_inc(turned, 1)
                        t = tile(MUL)
                        if t:
                            n, b = t.rows, t.slot
                            pe.wait_ge(s_out, t.n + 1)
                            pe.wait_ge(v_out, t.n + 1)
                            if positive(t.n - (sums - 1)):
                                pe.wait_ge(summed, t.n - (sums - 1))
                            for q in range(G):
                                o = psO[0:n, b % sums, q // per_bank, (q % per_bank) * width:(q % per_bank + 1) * width]
                                if kind == 3:
                                    o = o.rearrange("p (k c) -> p k c", k=2)
                                    os_, ov = o[:, :, 0:S], o[:, :, S:D]
                                else:
                                    ns = 96 if kind == 1 else S
                                    os_, ov = o[:, 0:ns], o[:, ns:width]
                                nc.tensor.matmul(os_, HsT[:, b % 2, q * n:(q + 1) * n], ws, start=True, stop=True)
                                mm = nc.tensor.matmul(ov, HvT[:, b % 2, q * n:(q + 1) * n], wv, start=True, stop=True)
                            mm.then_inc(product, 1)
                    sweep(pe, groups, full_groups, last_parts, STORE, step)

                if kind == 0:
                    @block.gpsimd
                    def _(pool):
                        def step(tile):
                            t = tile(3)
                            if t:
                                n, b = t.rows, t.slot
                                pool.wait_ge(ix["compared"], t.n + 1)
                                if positive(t.n - 1):
                                    pool.wait_ge(ix["counted"], t.n - 1)
                                nc.gpsimd.tensor_tensor(early[0:n, b % 2, :, 0:n], eq[0:n, b, :, 0:n],
                                                        repeat(lower[0:n, 0:n], 1, 2), ALU.mult).then_inc(ix["masked"], 1)
                        sweep(pool, groups, full_groups, last_parts, STORE, step)

                if kind >= 2:
                    @block.gpsimd
                    def _(pool):
                        def step(tile):
                            t = tile(2 if kind == 2 else 1)
                            if not t:
                                return
                            n, b = t.rows, t.slot
                            if kind == 2:
                                pool.wait_ge(gates, t.n + 1)
                                g = Gt[0:n, b % 2, :, :]
                                pv = Pt[0:n, b, :, 96:192].rearrange("p g (k i) -> p g k i", i=3)
                                nc.gpsimd.tensor_tensor(Pt[0:n, b, :, 0:S], Pt[0:n, b, :, 0:S], g[:, :, 0:S], ALU.mult)
                                for q in range(G):
                                    ins = nc.gpsimd.tensor_tensor(pv[:, q], pv[:, q], repeat(g[:, q, S:96], 2, 3), ALU.mult)
                                ins.then_inc(gated, 1)
                                pool.wait_ge(gated, t.n + 1)
                                if positive(t.n - (NB - 1)):
                                    pool.wait_ge(summed, t.n - (NB - 1))
                                nc.gpsimd.tensor_tensor(X2[0:n, b, :, 0:S], Pt[0:n, b, :, 0:S], X[0:n, b, :, 0:S], ALU.add)
                                nc.gpsimd.tensor_tensor(X2[0:n, b, :, S:D], Pt[0:n, b, :, 96:192], X[0:n, b, :, S:D], ALU.add)\
                                    .then_inc(residual_ready, 1)
                            else:
                                pool.wait_ge(loaded[t.slot], (t.turn + 1) * (16 * (loads)))
                                if positive(t.n - (NB - 1)):
                                    pool.wait_ge(summed, t.n - (NB - 1))
                                nc.gpsimd.tensor_tensor(XT[0:n, b, :, :], X[0:n, b, :, :], T3[0:n, b, :, :], ALU.add)\
                                    .then_inc(residual_ready, 1)
                        sweep(pool, groups, full_groups, last_parts, STORE, step)

                @block.vector
                def _(dve):
                    def add_half(t):
                        n, b = t.rows, t.slot
                        dve.wait_ge(product, t.n + 1)
                        if positive(t.turn):
                            dve.wait_ge(stored[t.slot], t.turn * (16 * (2 if kind == 2 else 1)))
                        ps = psO[0:n, b % sums]
                        if kind == 3:
                            dve.wait_ge(residual_ready, t.n + 1)
                            if positive(t.n - 1):
                                dve.wait_ge(summed, t.n - 1)
                            for q in range(G):
                                ins = nc.vector.scalar_tensor_tensor(A1[0:n, b % 2, q, :], ps[:, q, 0:D], NA[0:n, b, q, 0:1],
                                                                     XT[0:n, b, q, :], ALU.mult, ALU.add)
                            ins.then_inc(part_a, 1)
                            dve.wait_ge(part_a, t.n + 1)
                            for q in range(G):
                                ins = nc.vector.scalar_tensor_tensor(Y[0:n, b, q, :], ps[:, q, D:2 * D], NA[0:n, b, q, 1:2],
                                                                     A1[0:n, b % 2, q, :], ALU.mult, ALU.add)
                        else:
                            pairs = ps[:, :, 0:2 * width]
                            yv = Y[0:n, b, :, :].rearrange("p (k g) c -> p k (g c)", k=2)
                            if kind == 1:
                                ins = nc.vector.tensor_copy(yv, pairs)
                            else:
                                xv = (X if kind == 0 else X2)[0:n, b, :, :].rearrange("p (k g) c -> p k (g c)", k=2)
                                ins = nc.vector.tensor_tensor(yv, xv, pairs, ALU.add)
                        ins.then_inc(summed, 1)

                    def index_step(tile):
                        t = tile(4)
                        if t:
                            n, b = t.rows, t.slot
                            dve.wait_ge(ix["masked"], t.n + 1)
                            if positive(t.n):
                                dve.wait_ge(ix["moved"], t.n)
                            nc.vector.tensor_reduce(rep[0:n, :], early[0:n, b % 2, :, 0:n], AX_X, ALU.max)\
                                .then_inc(ix["counted"], 1)
                            nc.vector.tensor_scalar(off[0:n, :], col[0:n, b, :], -1.0, junk[0:n, :], ALU.mult, ALU.add)\
                                .then_inc(ix["offset"], 1)
                        t_ = tile(2)
                        if t_:
                            n, b = t_.rows, t_.slot
                            dve.wait_ge(index_in[t_.slot], (t_.turn + 1) * 48)
                            if positive(t_.turn):
                                dve.wait_ge(index_stored[t_.slot], t_.turn * 32)
                            if positive(t_.n - (NB - 1)):
                                dve.wait_ge(ix["masked"], t_.n - (NB - 1))
                            nc.vector.tensor_tensor(eq[0:n, b, :, 0:n], row[0:n, b, :, 0:n], repeat(col[0:n, b, :], 2, n),
                                                    ALU.is_equal).then_inc(ix["compared"], 1)
                        if t:
                            n, b = t.rows, t.slot
                            dve.wait_ge(ix["counted"], t.n + 1)
                            dve.wait_ge(ix["offset"], t.n + 1)
                            if positive(t.n):
                                dve.wait_ge(ix["ready"], t.n)
                            nc.vector.tensor_tensor(moved[0:n, :], off[0:n, :], rep[0:n, :], ALU.mult)\
                                .then_inc(ix["moved"], 1)
                            dve.wait_ge(ix["moved"], t.n + 1)
                            nc.vector.tensor_tensor(uniq[0:n, b, :], moved[0:n, :], col[0:n, b, :], ALU.add)\
                                .then_inc(ix["ready"], 1)

                    def step(tile):
                        if kind == 0:
                            index_step(tile)
                        t = tile(STATS)
                        if t:
                            n, b = t.rows, t.slot
                            if kind == 2:
                                dve.wait_ge(residual_ready, t.n + 1)
                            else:
                                dve.wait_ge(loaded[t.slot], (t.turn + 1) * (16 * (loads)))
                            src = X2 if kind == 2 else X
                            norm.statistics(dve, t, [src[0:n, b, q, :] for q in range(G)])
                        tm = tile(MUL)
                        if newton:
                            if t:
                                norm.widen(dve, t)
                                for at in range(5):
                                    norm.newton(dve, t, at)
                            if tm:
                                add_half(tm)
                            if t:
                                for at in range(5, NEWTON + 1):
                                    norm.newton(dve, t, at)
                                norm.newton_shifts(dve, t)
                        else:
                            if tm:
                                add_half(tm)
                            t = tile(STATS + 1)
                            if t:
                                norm.scales(dve, t)
                    sweep(dve, groups, full_groups, last_parts, STORE, step)

        def gather(pool, out_ap, tab, index):
            return pool.indirect_dma_start(out=out_ap, out_offset=None, in_=tab,
                                           in_offset=bass.IndirectOffsetOnAxis(ap=index, axis=0))

        def scatter_add(pool, tab, index, in_ap):
            return pool.indirect_dma_start(out=tab, out_offset=bass.IndirectOffsetOnAxis(ap=index, axis=0),
                                           in_=in_ap, in_offset=None, compute_op=ALU.add)

        SRC, DST = 0, 1

        class EdgePhase:

            def __init__(self, ph, tag, table_in, at, to, table_out, width, ea_cols, lags, gathers=1):
                self.tag, self.table_in, self.at, self.to, self.table_out = tag, table_in, at, to, table_out
                self.width, self.ea_cols, self.gathers, self.row_dmas = width, ea_cols, gathers, gathers
                self.ea_lag, self.eq_lag, self.uq_lag, self.last = lags

                def sb(name, shape, dt=F32):
                    return ph.enter_context(nc.sbuf_tensor(f"{tag}_{name}", shape, dt))
                self.index, self.uniq = sb("index", [P, NB, 2], I32), sb("uniq", [P, NB, 2], I32)
                self.X = sb("X", [P, NB, gathers, D])
                self.EA = sb("EA", [P, NB, ea_cols[1] - ea_cols[0]])
                self.EQ, self.R = sb("EQ", [P, NB, P]), sb("R", [P, NB, width])
                self.index_in, self.ea_in = ring_sems(f"{tag}_index_in"), ring_sems(f"{tag}_ea_in")
                self.eq_in, self.uniq_in = ring_sems(f"{tag}_eq_in"), ring_sems(f"{tag}_uniq_in")
                self.rows_in = ring_sems(f"{tag}_rows_in")
                self.added, self.passed = sem(f"{tag}_added"), sem(f"{tag}_pool_passed")

            def loads(self, sp, tile, index_used, ea_used, eq_used):
                t = tile(0)
                if t:
                    n, b = t.rows, t.slot
                    index_used(sp, t)
                    sp.dma_start(self.index[0:n, b, :], idx2[bass.ds(t.n * P, n), :]).then_inc(self.index_in[b], 16)
                t = tile(self.ea_lag)
                if t:
                    n, b = t.rows, t.slot
                    if positive(t.n - (NB - 1)):
                        sp.wait_ge(ea_used, t.n - (NB - 1))
                    sp.dma_start(self.EA[0:n, b, :], ea[bass.ds(t.n * P, n), self.ea_cols[0]:self.ea_cols[1]])\
                      .then_inc(self.ea_in[b], 16)
                t = tile(self.eq_lag)
                if t:
                    n, b = t.rows, t.slot
                    if positive(t.n - (NB - 1)):
                        sp.wait_ge(eq_used, t.n - (NB - 1))
                    sp.dma_start(self.EQ[0:n, b, 0:n], same[bass.ds(t.n * P, n), self.to * P:self.to * P + n])\
                      .then_inc(self.eq_in[b], 16)
                t = tile(self.uq_lag)
                if t:
                    n, b = t.rows, t.slot
                    if positive((t.n - (NB - 1)) * 16):
                        sp.wait_ge(self.added, (t.n - (NB - 1)) * 16)
                    sp.dma_start(self.uniq[0:n, b, :], unique[bass.ds(t.n * P, n), :]).then_inc(self.uniq_in[b], 16)

            def gather_rows(self, pool, t, rows_free):
                n, b = t.rows, t.slot
                pool.wait_ge(self.index_in[t.slot], (t.turn + 1) * 16)
                if positive(t.n - (NB - 1)):
                    pool.wait_ge(rows_free, t.n - (NB - 1))
                pool.sem_inc(self.passed, 1)
                for g in range(self.gathers):
                    a = self.at if self.gathers == 1 else (DST, SRC)[g]
                    gather(pool, self.X[0:n, b, g, :], self.table_in, self.index[0:n, b, a:a + 1])\
                        .then_inc(self.rows_in[b], 16)

            def add_rows(self, pool, t, result, per=1):
                n, b = t.rows, t.slot
                pool.wait_ge(self.uniq_in[t.slot], (t.turn + 1) * 16)
                pool.wait_ge(result, (t.n + 1) * per)
                if positive(t.n * 16):
                    pool.wait_ge(self.added, t.n * 16)
                pool.sem_inc(self.passed, 1)
                scatter_add(pool, self.table_out, self.uniq[0:n, b, self.to:self.to + 1], self.R[0:n, b, :])\
                    .then_inc(self.added, 16)

        def rows_used(e):
            def wait(sp, t):
                if positive(t.turn):
                    sp.wait_ge(e.rows_in[t.slot], t.turn * (16 * (e.row_dmas)))
            return wait

        def layer1_edges():
            with nc.cleanup_on_exit(), ExitStack() as ph:
                tag, LAST = "e1", 7

                def sb(name, shape, dt=F32):
                    return ph.enter_context(nc.sbuf_tensor(f"{tag}_{name}", shape, dt))

                def pb(name, shape):
                    return ph.enter_context(nc.psum_tensor(f"{tag}_{name}", shape, F32))
                e = EdgePhase(ph, tag, x1, DST, SRC, p1, 192, (EA3, EAW), (1, 3, 4, LAST))
                norm = Norm(ph, tag, 1)
                H, XT, VT, hidT = sb("H", [P, NB, D]), sb("XT", [S, NB, 2, P]), sb("VT", [96, NB, P]), sb("hidT", [64, NB, P])
                XS, XV = sb("XS", [P, NB, S]), sb("XV", [P, NB, 5, V])
                half, rtmp = sb("n2_bits", [P, NB], I32), sb("rtmp", [P, 1])
                n2, rn, rhat, sh = sb("n2", [P, NB]), sb("rn", [P, NB]), sb("rhat", [P, NB, 3]), sb("sh", [P, NB, 5])
                sq, w1x, Wt = sb("sq", [P, 3]), sb("w1x", [P, S]), sb("Wt", [P, NB, 224])
                ca, cb, dp, ds_ = sb("ca", [P, 3, V]), sb("cb", [P, 3, V]), sb("dp", [P, 3, V]), sb("ds", [P, V])
                CR, DT = sb("CR", [P, 2, 3, V]), sb("DT", [P, 2, V])
                Z, ZT = sb("Z", [P, NB, 480]), sb("ZT", [P, NB, 4, P])
                psT, psM, psW, psZ, psO = pb("psT", [P, 2, 512]), pb("psM", [P, 2, 512]), pb("psW", [P, 512]), pb("psZ", [P, 2, 512]), pb("psO", [P, 512])
                q = {m: sem(f"{tag}_{m}") for m in (
                    "turned", "xt_out", "vt_out", "mixed", "hid_out", "xv_out", "filter", "filter_out",
                    "squared", "n2", "n2_half", "rn", "rhat", "sh", "pool_products", "cross", "dot1", "dot", "w1x", "z_ready",
                    "z_turned", "z_out_a", "z_out_b", "linear", "result")}
                block = ph.enter_context(nc.Block())

                @block.sync
                def _(sp):
                    def step(tile):
                        e.loads(sp, tile, rows_used(e), q["z_ready"], q["z_turned"])
                    sweep(sp, tiles, full_tiles, last_edges, LAST, step)

                @block.gpsimd
                def _(pool):
                    def step(tile):
                        t = tile(6)
                        if t:
                            e.add_rows(pool, t, q["result"])
                        t = tile(1)
                        if t:
                            e.gather_rows(pool, t, norm.done)
                        t = tile(4)
                        if t:
                            n, b = t.rows, t.slot
                            pool.wait_ge(q["xv_out"], t.n + 1)
                            pool.wait_ge(q["sh"], t.n + 1)
                            if positive(t.n - 1):
                                pool.wait_ge(q["z_ready"], t.n - 1)
                            if positive(t.n):
                                pool.wait_ge(q["dot"], t.n)
                            v = XV[0:n, b, :, :]
                            nc.gpsimd.tensor_tensor(ca[0:n], v[:, 1:4, :], repeat(sh[0:n, b, 2:5], 2, V), ALU.mult)
                            nc.gpsimd.tensor_tensor(cb[0:n], v[:, 2:5, :], repeat(sh[0:n, b, 1:4], 2, V), ALU.mult)
                            nc.gpsimd.tensor_tensor(dp[0:n], v[:, 0:3, :], repeat(rhat[0:n, b, :], 2, V), ALU.mult)\
                                .then_inc(q["pool_products"], 1)
                            pool.wait_ge(q["pool_products"], t.n + 1)
                            nc.gpsimd.tensor_tensor(CR[0:n, b % 2], ca[0:n], cb[0:n], ALU.subtract).then_inc(q["cross"], 1)
                            nc.gpsimd.tensor_tensor(ds_[0:n], dp[0:n, 0], dp[0:n, 1], ALU.add).then_inc(q["dot1"], 1)
                            pool.wait_ge(q["dot1"], t.n + 1)
                            nc.gpsimd.tensor_tensor(DT[0:n, b % 2], ds_[0:n], dp[0:n, 2], ALU.add).then_inc(q["dot"], 1)
                    sweep(pool, tiles, full_tiles, last_edges, LAST, step)
                    pool.wait_ge(e.added, 16 * tiles)

                @block.scalar
                def _(act):
                    def step(tile):
                        t = tile(5)
                        if t:
                            n, b = t.rows, t.slot
                            act.wait_ge(q["z_turned"], t.n + 1)
                            if positive(t.n - (NB - 1)):
                                act.wait_ge(q["linear"], t.n - (NB - 1))
                            nc.scalar.copy(ZT[0:P, b, 1:4, 0:n], psZ[:, b % 2, P:512].rearrange("p (c q) -> p c q", c=3)[:, :, 0:n])\
                                .then_inc(q["z_out_a"], 1)
                            nc.scalar.copy(ZT[0:96, b, 0, 0:n], psZ[0:96, b % 2, 0:n]).then_inc(q["z_out_b"], 1)
                        t = tile(3)
                        if t:
                            n, b = t.rows, t.slot
                        t = tile(5)
                        if t:
                            n, b = t.rows, t.slot
                            act.wait_ge(q["linear"], t.n + 1)
                            if positive((t.n - (NB - 1)) * 16):
                                act.wait_ge(e.added, (t.n - (NB - 1)) * 16)
                            nc.scalar.copy(e.R[0:n, b, :], psO[0:n, 0:192]).then_inc(q["result"], 1)
                        t = tile(3)
                        if t:
                            n, b = t.rows, t.slot
                            act.wait_ge(q["mixed"], t.n + 1)
                            if positive(t.n - (NB - 1)):
                                act.wait_ge(q["filter"], t.n - (NB - 1))
                            nc.scalar.activation(hidT[:, b, 0:n], psM[0:64, b % 2, D:D + n], ACT.Relu).then_inc(q["hid_out"], 1)
                            if positive(t.n - (NB - 1)):
                                act.wait_ge(q["z_ready"], t.n - (NB - 1))
                            nc.scalar.copy(XS[0:n, b, :], psM[0:n, b % 2, 0:S])
                            v = psM[0:n, b % 2, S:D].rearrange("p (i u) -> p i u", i=3)
                            nc.scalar.copy(XV[0:n, b, 0:3, :], v)
                            nc.scalar.copy(XV[0:n, b, 3:5, :], v[:, 0:2, :]).then_inc(q["xv_out"], 1)
                        t = tile(2)
                        if t:
                            n, b = t.rows, t.slot
                            act.wait_ge(norm.ready, t.n + 1)
                            if positive(t.n - (NB - 1)):
                                act.wait_ge(q["turned"], t.n - (NB - 1))
                            norm.map(t, H[0:n, b, :], e.X[0:n, b, 0, :], 0).then_inc(norm.done, 1)
                    sweep(act, tiles, full_tiles, last_edges, LAST, step)

                @block.tensor
                def _(pe):
                    def step(tile):
                        t = tile(5)
                        if t:
                            n, b = t.rows, t.slot
                            pe.wait_ge(q["z_ready"], t.n + 1)
                            pe.wait_ge(e.eq_in[t.slot], (t.turn + 1) * 16)
                            if positive(t.n - 1):
                                pe.wait_ge(q["z_out_a"], t.n - 1)
                            if positive(t.n - 1):
                                pe.wait_ge(q["z_out_b"], t.n - 1)
                            nc.tensor.matmul(psZ[0:96, b % 2, 0:n], Z[0:n, b, 0:96], e.EQ[0:n, b, 0:n], start=True, stop=True)
                            for i in range(3):
                                mm = nc.tensor.matmul(psZ[:, b % 2, P * (i + 1):P * (i + 1) + n], Z[0:n, b, 96 + P * i:96 + P * (i + 1)],
                                                      e.EQ[0:n, b, 0:n], start=True, stop=True)
                            mm.then_inc(q["z_turned"], 1)
                        t = tile(3)
                        if t:
                            n, b = t.rows, t.slot
                            pe.wait_ge(norm.done, t.n + 1)
                            pe.wait_ge(e.ea_in[t.slot], (t.turn + 1) * 16)
                            if positive(t.n - 1):
                                pe.wait_ge(q["xt_out"], t.n - 1)
                            if positive(t.n - 1):
                                pe.wait_ge(q["vt_out"], t.n - 1)
                            nc.tensor.transpose(psT[0:96, b % 2, 2 * P:2 * P + n], H[0:n, b, S:D], ident[0:n, 0:n])
                            nc.tensor.transpose(psT[0:S, b % 2, 0:n], H[0:n, b, 0:S], ident[0:n, 0:n])
                            nc.tensor.transpose(psT[0:S, b % 2, P:P + n], e.EA[0:n, b, 3:67], ident[0:n, 0:n])\
                                .then_inc(q["turned"], 1)
                        t = tile(5)
                        if t:
                            n, b = t.rows, t.slot
                            pe.wait_ge(q["z_out_a"], t.n + 1)
                            pe.wait_ge(q["z_out_b"], t.n + 1)
                            if positive(t.n):
                                pe.wait_ge(q["result"], t.n)
                            nc.tensor.matmul(psO[0:n, 0:96], ZT[0:96, b, 0, 0:n], w("out_s"), start=True, stop=True)
                            for i in range(3):
                                mm = nc.tensor.matmul(psO[0:n, 96 + i:192:3], ZT[:, b, 1 + i, 0:n], w("out_v"), start=True, stop=True)
                            mm.then_inc(q["linear"], 1)
                        t = tile(3)
                        if t:
                            n, b = t.rows, t.slot
                            pe.wait_ge(q["xt_out"], t.n + 1)
                            pe.wait_ge(q["vt_out"], t.n + 1)
                            if positive(t.n - 1):
                                pe.wait_ge(q["xv_out"], t.n - 1)
                            nc.tensor.matmul(psM[0:n, b % 2, 0:S], XT[0:S, b, 0, 0:n], w("nl_s"), start=True, stop=True)
                            nc.tensor.matmul(psM[0:n, b % 2, S:D], VT[0:96, b, 0:n], w("nl_v"), start=True, stop=True)
                            nc.tensor.matmul(psM[0:64, b % 2, D:D + n], w("fc1"), XT[0:64, b, 1, 0:n], start=True, stop=True)\
                                .then_inc(q["mixed"], 1)
                        t = tile(3)
                        if t:
                            n, b = t.rows, t.slot
                            pe.wait_ge(q["hid_out"], t.n + 1)
                            if positive(t.n):
                                pe.wait_ge(q["filter_out"], t.n)
                            nc.tensor.matmul(psW[0:n, 0:224], hidT[:, b, 0:n], w("fc2"), start=True, stop=True)\
                                .then_inc(q["filter"], 1)
                    sweep(pe, tiles, full_tiles, last_edges, LAST, step)

                @block.vector
                def _(dve):
                    def step(tile):
                        t = tile(3)
                        if t:
                            n, b = t.rows, t.slot
                            dve.wait_ge(q["turned"], t.n + 1)
                            if positive(t.n - (NB - 1)):
                                dve.wait_ge(q["mixed"], t.n - (NB - 1))
                            nc.vector.tensor_copy(XT[0:S, b, :, 0:n], psT[0:S, b % 2, 0:2 * P].rearrange("p (c q) -> p c q", c=2)[:, :, 0:n])\
                                .then_inc(q["xt_out"], 1)
                            nc.vector.tensor_copy(VT[:, b, 0:n], psT[0:96, b % 2, 2 * P:2 * P + n]).then_inc(q["vt_out"], 1)
                            dve.wait_ge(e.ea_in[t.slot], (t.turn + 1) * 16)
                            a = e.EA[0:n, b, 0:3]
                            if positive(t.n):
                                dve.wait_ge(q["n2"], t.n)
                            nc.vector.tensor_tensor(sq[0:n], a, a, ALU.mult).then_inc(q["squared"], 1)
                            dve.wait_ge(q["squared"], t.n + 1)
                            nc.vector.tensor_reduce(n2[0:n, b:b + 1], sq[0:n], AX_X, ALU.add).then_inc(q["n2"], 1)
                            dve.wait_ge(q["n2"], t.n + 1)
                            for at in range(NEWTON + 1):
                                inverse_root(dve, t, q["rn"], n2[0:n, b:b + 1], half[0:n, b:b + 1], rtmp[0:n], rn[0:n, b:b + 1], at)
                            if positive((t.n + 1) * (NEWTON + 1)):
                                dve.wait_ge(q["rn"], (t.n + 1) * (NEWTON + 1))
                            if positive(t.n - (NB - 1)):
                                dve.wait_ge(q["dot"], t.n - (NB - 1))
                            nc.vector.tensor_scalar(rhat[0:n, b, :], a, rn[0:n, b:b + 1], None, ALU.mult).then_inc(q["rhat"], 1)
                            nc.vector.tensor_scalar(sh[0:n, b, 0:3], a, rn[0:n, b:b + 1], 3.0 ** 0.5, ALU.mult, ALU.mult)
                            nc.vector.tensor_scalar(sh[0:n, b, 3:5], a[:, 0:2], rn[0:n, b:b + 1], 3.0 ** 0.5, ALU.mult, ALU.mult)\
                                .then_inc(q["sh"], 1)
                        t = tile(2)
                        if t:
                            n, b = t.rows, t.slot
                            dve.wait_ge(e.rows_in[t.slot], (t.turn + 1) * 16)
                            norm.on_vector(dve, t, [e.X[0:n, b, 0, :]])
                        t = tile(3)
                        if t:
                            n, b = t.rows, t.slot
                            dve.wait_ge(q["filter"], t.n + 1)
                            nc.vector.tensor_copy(Wt[0:n, b, :], psW[0:n, 0:224]).then_inc(q["filter_out"], 1)
                        t = tile(4)
                        if t:
                            n, b = t.rows, t.slot
                            dve.wait_ge(q["xv_out"], t.n + 1)
                            dve.wait_ge(q["filter_out"], t.n + 1)
                            if positive(t.n - (NB - 1)):
                                dve.wait_ge(q["z_turned"], t.n - (NB - 1))
                            z, wt = Z[0:n, b, :], Wt[0:n, b, :]
                            zv = z[:, 96:480].rearrange("p (i c) -> p i c", i=3)
                            if positive(t.n):
                                dve.wait_ge(q["z_ready"], t.n)
                            nc.vector.tensor_tensor(w1x[0:n], wt[:, 64:128], XS[0:n, b, :], ALU.mult).then_inc(q["w1x"], 1)
                            nc.vector.tensor_tensor(z[:, 0:S], wt[:, 0:64], XS[0:n, b, :], ALU.mult)
                            nc.vector.tensor_tensor(zv[:, :, S:96], XV[0:n, b, 0:3, :], repeat(wt[:, 128:160], 1, 3), ALU.mult)
                            dve.wait_ge(q["w1x"], t.n + 1)
                            dve.wait_ge(q["sh"], t.n + 1)
                            nc.vector.tensor_tensor(zv[:, :, 0:S], repeat(w1x[0:n], 1, 3), repeat(sh[0:n, b, 0:3], 2, S), ALU.mult)
                            dve.wait_ge(q["cross"], t.n + 1)
                            nc.vector.tensor_tensor(zv[:, :, 96:P], CR[0:n, b % 2], repeat(wt[:, 192:224], 1, 3), ALU.mult)
                            dve.wait_ge(q["dot"], t.n + 1)
                            nc.vector.tensor_tensor(z[:, S:96], DT[0:n, b % 2], wt[:, 160:192], ALU.mult).then_inc(q["z_ready"], 1)
                    sweep(dve, tiles, full_tiles, last_edges, LAST, step)

        def layer2_edges():
            with nc.cleanup_on_exit(), ExitStack() as ph:
                tag, LAST = "e2", 5

                def sb(name, shape, dt=F32):
                    return ph.enter_context(nc.sbuf_tensor(f"{tag}_{name}", shape, dt))

                def pb(name, shape):
                    return ph.enter_context(nc.psum_tensor(f"{tag}_{name}", shape, F32))
                e = EdgePhase(ph, tag, h2, SRC, DST, x3, D, (EA4, EA3), (1, 2, 3, LAST))
                VE, VD = sb("VE", [P, 3, V]), sb("VD", [P, V])
                Z, ZT, RT = sb("Z", [P, NB, 4, 96]), sb("ZT", [96, NB, 4, P]), sb("RT", [17, NB, P])
                gate, M = sb("gate", [P, NB, D]), sb("M", [P, NB, D])
                MsT, MvT = sb("MsT", [S, NB, P]), sb("MvT", [96, NB, P])
                psZ, psR, psM = pb("psZ", [P, 2, 512]), pb("psR", [P, 512]), pb("psM", [P, 2, 512])
                psA, psO = pb("psA", [P, 2, 512]), pb("psO", [P, 512])
                q = {m: sem(f"{tag}_{m}") for m in (
                    "ones", "ve", "ve1", "z_pool", "z_ready", "turned", "rad_turned", "rt_out", "zt_out", "message",
                    "gate", "m_ready", "m_turned", "ms_out", "mv_out", "linear", "result")}
                block = ph.enter_context(nc.Block())

                @block.sync
                def _(sp):
                    def step(tile):
                        e.loads(sp, tile, rows_used(e), q["turned"], q["m_turned"])
                    sweep(sp, tiles, full_tiles, last_edges, LAST, step)

                @block.gpsimd
                def _(pool):
                    nc.gpsimd.memset(RT[:, :, :], 1.0).then_inc(q["ones"], 1)

                    def step(tile):
                        t = tile(5)
                        if t:
                            e.add_rows(pool, t, q["result"])
                        t = tile(1)
                        if t:
                            e.gather_rows(pool, t, q["z_ready"])
                        t = tile(2)
                        if t:
                            n, b = t.rows, t.slot
                            pool.wait_ge(e.rows_in[t.slot], (t.turn + 1) * 16)
                            pool.wait_ge(e.ea_in[t.slot], (t.turn + 1) * 16)
                            if positive(t.n - (NB - 1)):
                                pool.wait_ge(q["turned"], t.n - (NB - 1))
                            if positive(t.n):
                                pool.wait_ge(q["z_pool"], t.n)
                            xv = e.X[0:n, b, 0, S:D].rearrange("p (u i) -> p i u", i=3)
                            ev = e.EA[0:n, b, 1:4]
                            nc.gpsimd.tensor_tensor(VE[0:n], xv, repeat(ev, 2, V), ALU.mult).then_inc(q["ve"], 1)
                            pool.wait_ge(q["ve"], t.n + 1)
                            nc.gpsimd.tensor_tensor(VD[0:n], VE[0:n, 0], VE[0:n, 1], ALU.add).then_inc(q["ve1"], 1)
                            pool.wait_ge(q["ve1"], t.n + 1)
                            nc.gpsimd.tensor_tensor(Z[0:n, b, 0, S:96], VD[0:n], VE[0:n, 2], ALU.add).then_inc(q["z_pool"], 1)
                    sweep(pool, tiles, full_tiles, last_edges, LAST, step)
                    pool.wait_ge(e.added, 16 * tiles)

                @block.vector
                def _(dve):
                    def step(tile):
                        t = tile(4)
                        if t:
                            n, b = t.rows, t.slot
                            dve.wait_ge(q["m_turned"], t.n + 1)
                            if positive(t.n - (NB - 1)):
                                dve.wait_ge(q["linear"], t.n - (NB - 1))
                            nc.vector.tensor_copy(MsT[:, b, 0:n], psA[0:S, b % 2, 0:n]).then_inc(q["ms_out"], 1)
                            nc.vector.tensor_copy(MvT[:, b, 0:n], psA[0:96, b % 2, P:P + n]).then_inc(q["mv_out"], 1)
                        t = tile(2)
                        if t:
                            n, b = t.rows, t.slot
                            dve.wait_ge(e.rows_in[t.slot], (t.turn + 1) * 16)
                            dve.wait_ge(e.ea_in[t.slot], (t.turn + 1) * 16)
                            if positive(t.n - (NB - 1)):
                                dve.wait_ge(q["turned"], t.n - (NB - 1))
                            xs = e.X[0:n, b, 0, 0:S]
                            xv = e.X[0:n, b, 0, S:D].rearrange("p (u i) -> p i u", i=3)
                            es, ev = e.EA[0:n, b, 0:1], e.EA[0:n, b, 1:4]
                            nc.vector.tensor_scalar(Z[0:n, b, 0, 0:S], xs, es, None, ALU.mult)
                            nc.vector.tensor_scalar(Z[0:n, b, 1:4, S:96], xv, es, None, ALU.mult)
                            nc.vector.tensor_tensor(Z[0:n, b, 1:4, 0:S], repeat(xs, 1, 3), repeat(ev, 2, S), ALU.mult)\
                                .then_inc(q["z_ready"], 1)
                        t = tile(3)
                        if t:
                            n, b = t.rows, t.slot
                            dve.wait_ge(q["message"], t.n + 1)
                            dve.wait_ge(q["gate"], t.n + 1)
                            if positive(t.n - (NB - 1)):
                                dve.wait_ge(q["m_turned"], t.n - (NB - 1))
                            nc.vector.tensor_tensor(M[0:n, b, :], psM[0:n, b % 2, 0:D], gate[0:n, b, :], ALU.mult)\
                                .then_inc(q["m_ready"], 1)
                    sweep(dve, tiles, full_tiles, last_edges, LAST, step)

                @block.scalar
                def _(act):
                    act.wait_ge(q["ones"], 1)

                    def step(tile):
                        t = tile(3)
                        if t:
                            n, b = t.rows, t.slot
                            act.wait_ge(q["turned"], t.n + 1)
                            if positive(t.n - (NB - 1)):
                                act.wait_ge(q["message"], t.n - (NB - 1))
                            nc.scalar.copy(RT[0:16, b, 0:n], psR[0:16, 0:n]).then_inc(q["rt_out"], 1)
                            nc.scalar.copy(ZT[:, b, :, 0:n], psZ[0:96, b % 2, :].rearrange("p (c q) -> p c q", c=4)[:, :, 0:n])\
                                .then_inc(q["zt_out"], 1)
                            act.wait_ge(q["message"], t.n + 1)
                            if positive(t.n - (NB - 1)):
                                act.wait_ge(q["m_ready"], t.n - (NB - 1))
                            nc.scalar.activation(gate[0:n, b, :], psM[0:n, b % 2, D:2 * D], ACT.Sigmoid).then_inc(q["gate"], 1)
                        t = tile(4)
                        if t:
                            n, b = t.rows, t.slot
                            act.wait_ge(q["linear"], t.n + 1)
                            if positive((t.n - (NB - 1)) * 16):
                                act.wait_ge(e.added, (t.n - (NB - 1)) * 16)
                            nc.scalar.copy(e.R[0:n, b, :], psO[0:n, 0:D]).then_inc(q["result"], 1)
                    sweep(act, tiles, full_tiles, last_edges, LAST, step)

                @block.tensor
                def _(pe):
                    def step(tile):
                        t = tile(4)
                        if t:
                            n, b = t.rows, t.slot
                            pe.wait_ge(q["m_ready"], t.n + 1)
                            pe.wait_ge(e.eq_in[t.slot], (t.turn + 1) * 16)
                            if positive(t.n - 1):
                                pe.wait_ge(q["ms_out"], t.n - 1)
                            if positive(t.n - 1):
                                pe.wait_ge(q["mv_out"], t.n - 1)
                            nc.tensor.matmul(psA[0:S, b % 2, 0:n], M[0:n, b, 0:S], e.EQ[0:n, b, 0:n], start=True, stop=True)
                            nc.tensor.matmul(psA[0:96, b % 2, P:P + n], M[0:n, b, S:D], e.EQ[0:n, b, 0:n], start=True, stop=True)\
                                .then_inc(q["m_turned"], 1)
                        t = tile(3)
                        if t:
                            n, b = t.rows, t.slot
                            pe.wait_ge(q["z_ready"], t.n + 1)
                            pe.wait_ge(q["z_pool"], t.n + 1)
                            if positive(t.n - 1):
                                pe.wait_ge(q["zt_out"], t.n - 1)
                            if positive(t.n):
                                pe.wait_ge(q["rt_out"], t.n)
                            nc.tensor.transpose(psR[0:16, 0:n], e.EA[0:n, b, 4:20], ident[0:n, 0:n])
                            for c in range(4):
                                tr = nc.tensor.transpose(psZ[0:96, b % 2, P * c:P * c + n], Z[0:n, b, c, :], ident[0:n, 0:n])
                            tr.then_inc(q["turned"], 1)
                            pe.wait_ge(q["rt_out"], t.n + 1)
                            pe.wait_ge(q["zt_out"], t.n + 1)
                            if positive(t.n - 1):
                                pe.wait_ge(q["m_ready"], t.n - 1)
                            nc.tensor.matmul(psM[0:n, b % 2, D:2 * D], RT[:, b, 0:n], w("rad"), start=True, stop=True)
                            nc.tensor.matmul(psM[0:n, b % 2, 0:S], ZT[:, b, 0, 0:n], w("l2_s"), start=True, stop=True)
                            for i in range(3):
                                mm = nc.tensor.matmul(psM[0:n, b % 2, S + i:D:3], ZT[:, b, 1 + i, 0:n], w("l2_v"), start=True, stop=True)
                            mm.then_inc(q["message"], 1)
                        t = tile(4)
                        if t:
                            n, b = t.rows, t.slot
                            pe.wait_ge(q["ms_out"], t.n + 1)
                            pe.wait_ge(q["mv_out"], t.n + 1)
                            if positive(t.n):
                                pe.wait_ge(q["result"], t.n)
                            nc.tensor.matmul(psO[0:n, 0:S], MsT[:, b, 0:n], w("l2l_s"), start=True, stop=True)
                            nc.tensor.matmul(psO[0:n, S:D], MvT[:, b, 0:n], w("l2l_v"), start=True, stop=True).then_inc(q["linear"], 1)
                    sweep(pe, tiles, full_tiles, last_edges, LAST, step)

        def layer3_edges():
            with nc.cleanup_on_exit(), ExitStack() as ph:
                tag, LAST = "e3", 7

                def sb(name, shape, dt=F32):
                    return ph.enter_context(nc.sbuf_tensor(f"{tag}_{name}", shape, dt))

                def pb(name, shape):
                    return ph.enter_context(nc.psum_tensor(f"{tag}_{name}", shape, F32))
                e = EdgePhase(ph, tag, x3, SRC, DST, t3, D, (EA10, EA16), (1, 3, 4, LAST))
                e.row_dmas = 3
                norm = Norm(ph, tag, 1)
                NA, ND, AM = sb("NA", [P, NB, 3]), sb("ND", [P, NB, 3]), sb("AM", [P, NB, 2])
                nd_in = ring_sems(f"{tag}_nd_in")
                H, HT, VT, LT = sb("H", [P, NB, D]), sb("HT", [S, NB, P]), sb("VT", [96, NB, P]), sb("LT", [10, NB, P])
                sg, hidT, A1, XM, Wt = sb("sg", [100, P]), sb("hidT", [100, NB, P]), sb("A1", [P, D]), sb("XM", [P, NB, D]), sb("Wt", [P, NB, 192])
                w1x, VE, VD, DT, W2 = sb("w1x", [P, S]), sb("VE", [P, 3, V]), sb("VD", [P, V]), sb("DT", [P, 2, V]), sb("W2", [P, V])
                Z, ZT, TA = sb("Z", [P, NB, 4, 96]), sb("ZT", [96, NB, 4, P]), sb("TA", [P, D])
                psT, psL, psM, psW = pb("psT", [P, 512]), pb("psL", [P, 512]), pb("psM", [P, 2, 512]), pb("psW", [P, 512])
                psZ, psO = pb("psZ", [P, 2, 512]), pb("psO", [P, 512])
                q = {m: sem(f"{tag}_{m}") for m in (
                    "turned", "ht_out", "vt_out", "lt_out", "hidden", "sig", "hid_out", "mixed", "part_a", "mix_out", "filter",
                    "filter_out", "ve", "ve1", "dot", "w1x", "w2e", "z_ready", "z_turned", "z_out", "linear", "am", "part_r", "result")}
                block = ph.enter_context(nc.Block())

                @block.sync
                def _(sp):
                    def step(tile):
                        e.loads(sp, tile, rows_used(e), q["z_ready"], q["z_turned"])
                    sweep(sp, tiles, full_tiles, last_edges, LAST, step)

                @block.gpsimd
                def _(pool):
                    def step(tile):
                        t = tile(6)
                        if t:
                            e.add_rows(pool, t, q["result"])
                        t = tile(1)
                        if t:
                            n, b = t.rows, t.slot
                            e.gather_rows(pool, t, norm.done)
                            if positive(t.n - (NB - 1)):
                                pool.wait_ge(q["mix_out"], t.n - (NB - 1))
                            pool.sem_inc(e.passed, 1)
                            gather(pool, NA[0:n, b, :], nattr, e.index[0:n, b, SRC:SRC + 1]).then_inc(e.rows_in[b], 16)
                            if positive(t.n - (NB - 1)):
                                pool.wait_ge(q["am"], t.n - (NB - 1))
                            pool.sem_inc(e.passed, 1)
                            gather(pool, ND[0:n, b, :], nattr, e.index[0:n, b, DST:DST + 1]).then_inc(e.rows_in[b], 16)
                        t = tile(4)
                        if t:
                            n, b = t.rows, t.slot
                            pool.wait_ge(q["mix_out"], t.n + 1)
                            if positive(t.n - 1):
                                pool.wait_ge(q["z_ready"], t.n - 1)
                            if positive(t.n):
                                pool.wait_ge(q["dot"], t.n)
                            xv = XM[0:n, b, S:D].rearrange("p (i u) -> p i u", i=3)
                            nc.gpsimd.tensor_tensor(VE[0:n], xv, repeat(e.EA[0:n, b, 11:14], 2, V), ALU.mult).then_inc(q["ve"], 1)
                            pool.wait_ge(q["ve"], t.n + 1)
                            nc.gpsimd.tensor_tensor(VD[0:n], VE[0:n, 0], VE[0:n, 1], ALU.add).then_inc(q["ve1"], 1)
                            pool.wait_ge(q["ve1"], t.n + 1)
                            nc.gpsimd.tensor_tensor(DT[0:n, b % 2], VD[0:n], VE[0:n, 2], ALU.add).then_inc(q["dot"], 1)
                    sweep(pool, tiles, full_tiles, last_edges, LAST, step)
                    pool.wait_ge(e.added, 16 * tiles)

                @block.vector
                def _(dve):
                    def step(tile):
                        t = tile(5)
                        if t:
                            n, b = t.rows, t.slot
                            if positive(t.n - (NB - 1)):
                                dve.wait_ge(q["result"], t.n - (NB - 1))
                            nc.vector.tensor_scalar(AM[0:n, b, :], ND[0:n, b, 0:2], ND[0:n, b, 2:3], None, ALU.mult)\
                                .then_inc(q["am"], 1)
                        t = tile(3)
                        if t:
                            n, b = t.rows, t.slot
                            dve.wait_ge(q["turned"], t.n + 1)
                            if positive(t.n - (NB - 1)):
                                dve.wait_ge(q["mixed"], t.n - (NB - 1))
                            nc.vector.tensor_copy(HT[:, b, 0:n], psT[0:S, 0:n]).then_inc(q["ht_out"], 1)
                            nc.vector.tensor_copy(VT[:, b, 0:n], psT[0:96, P:P + n]).then_inc(q["vt_out"], 1)
                        t = tile(2)
                        if t:
                            n, b = t.rows, t.slot
                            dve.wait_ge(e.rows_in[t.slot], (t.turn + 1) * 48)
                            norm.on_vector(dve, t, [e.X[0:n, b, 0, :]])
                        t = tile(3)
                        if t:
                            n, b = t.rows, t.slot
                            dve.wait_ge(q["sig"], t.n + 1)
                            if positive(t.n - (NB - 1)):
                                dve.wait_ge(q["filter"], t.n - (NB - 1))
                            nc.vector.tensor_tensor(hidT[:, b, 0:n], psL[0:100, P:P + n], sg[:, 0:n], ALU.mult).then_inc(q["hid_out"], 1)
                            dve.wait_ge(q["mixed"], t.n + 1)
                            if positive(t.n):
                                dve.wait_ge(q["mix_out"], t.n)
                            nc.vector.tensor_scalar(A1[0:n], psM[0:n, b % 2, 0:D], NA[0:n, b, 0:1], None, ALU.mult)\
                                .then_inc(q["part_a"], 1)
                            dve.wait_ge(q["part_a"], t.n + 1)
                            if positive(t.n - (NB - 1)):
                                dve.wait_ge(q["z_ready"], t.n - (NB - 1))
                            if positive(t.n - (NB - 1)):
                                dve.wait_ge(q["dot"], t.n - (NB - 1))
                            nc.vector.scalar_tensor_tensor(XM[0:n, b, :], psM[0:n, b % 2, D:2 * D], NA[0:n, b, 1:2], A1[0:n],
                                                           ALU.mult, ALU.add).then_inc(q["mix_out"], 1)
                        t = tile(5)
                        if t:
                            n, b = t.rows, t.slot
                            dve.wait_ge(q["linear"], t.n + 1)
                            dve.wait_ge(q["am"], t.n + 1)
                            if positive((t.n - (NB - 1)) * 16):
                                dve.wait_ge(e.added, (t.n - (NB - 1)) * 16)
                            if positive(t.n):
                                dve.wait_ge(q["result"], t.n)
                            nc.vector.tensor_scalar(TA[0:n], psO[0:n, 0:D], AM[0:n, b, 0:1], None, ALU.mult).then_inc(q["part_r"], 1)
                            dve.wait_ge(q["part_r"], t.n + 1)
                            nc.vector.scalar_tensor_tensor(e.R[0:n, b, :], psO[0:n, D:2 * D], AM[0:n, b, 1:2], TA[0:n],
                                                           ALU.mult, ALU.add).then_inc(q["result"], 1)
                        t = tile(4)
                        if t:
                            n, b = t.rows, t.slot
                            dve.wait_ge(q["filter_out"], t.n + 1)
                            dve.wait_ge(q["mix_out"], t.n + 1)
                            if positive(t.n - (NB - 1)):
                                dve.wait_ge(q["z_turned"], t.n - (NB - 1))
                            z, wt, xs = Z[0:n, b, :, :], Wt[0:n, b, :], XM[0:n, b, 0:S]
                            xv = XM[0:n, b, S:D].rearrange("p (i u) -> p i u", i=3)
                            es, ev = e.EA[0:n, b, 10:11], e.EA[0:n, b, 11:14]
                            if positive(t.n):
                                dve.wait_ge(q["z_ready"], t.n)
                            nc.vector.tensor_tensor(w1x[0:n], wt[:, 64:128], xs, ALU.mult).then_inc(q["w1x"], 1)
                            nc.vector.tensor_scalar(W2[0:n], wt[:, 128:160], es, None, ALU.mult).then_inc(q["w2e"], 1)
                            nc.vector.scalar_tensor_tensor(z[:, 0, 0:S], wt[:, 0:64], es, xs, ALU.mult, ALU.mult)
                            dve.wait_ge(q["w1x"], t.n + 1)
                            nc.vector.tensor_tensor(z[:, 1:4, 0:S], repeat(w1x[0:n], 1, 3), repeat(ev, 2, S), ALU.mult)
                            dve.wait_ge(q["w2e"], t.n + 1)
                            nc.vector.tensor_tensor(z[:, 1:4, S:96], xv, repeat(W2[0:n], 1, 3), ALU.mult)
                            dve.wait_ge(q["dot"], t.n + 1)
                            nc.vector.tensor_tensor(z[:, 0, S:96], DT[0:n, b % 2], wt[:, 160:192], ALU.mult).then_inc(q["z_ready"], 1)
                    sweep(dve, tiles, full_tiles, last_edges, LAST, step)

                @block.scalar
                def _(act):
                    def step(tile):
                        t = tile(5)
                        if t:
                            n, b = t.rows, t.slot
                            act.wait_ge(q["z_turned"], t.n + 1)
                            if positive(t.n - (NB - 1)):
                                act.wait_ge(q["linear"], t.n - (NB - 1))
                            nc.scalar.copy(ZT[:, b, :, 0:n], psZ[0:96, b % 2, :].rearrange("p (c q) -> p c q", c=4)[:, :, 0:n])\
                                .then_inc(q["z_out"], 1)
                        t = tile(3)
                        if t:
                            n, b = t.rows, t.slot
                            act.wait_ge(q["turned"], t.n + 1)
                            if positive(t.n - (NB - 1)):
                                act.wait_ge(q["hidden"], t.n - (NB - 1))
                            nc.scalar.copy(LT[:, b, 0:n], psL[0:10, 0:n]).then_inc(q["lt_out"], 1)
                            act.wait_ge(q["hidden"], t.n + 1)
                            if positive(t.n):
                                act.wait_ge(q["hid_out"], t.n)
                            nc.scalar.activation(sg[:, 0:n], psL[0:100, P:P + n], ACT.Sigmoid).then_inc(q["sig"], 1)
                        t = tile(2)
                        if t:
                            n, b = t.rows, t.slot
                            act.wait_ge(norm.ready, t.n + 1)
                            if positive(t.n - (NB - 1)):
                                act.wait_ge(q["turned"], t.n - (NB - 1))
                            norm.map(t, H[0:n, b, :], e.X[0:n, b, 0, :], 0).then_inc(norm.done, 1)
                        t = tile(3)
                        if t:
                            n, b = t.rows, t.slot
                            act.wait_ge(q["filter"], t.n + 1)
                            if positive(t.n - (NB - 1)):
                                act.wait_ge(q["z_ready"], t.n - (NB - 1))
                            nc.scalar.copy(Wt[0:n, b, :], psW[0:n, 0:192]).then_inc(q["filter_out"], 1)
                    sweep(act, tiles, full_tiles, last_edges, LAST, step)

                @block.tensor
                def _(pe):
                    def step(tile):
                        t = tile(5)
                        if t:
                            n, b = t.rows, t.slot
                            pe.wait_ge(q["z_ready"], t.n + 1)
                            pe.wait_ge(e.eq_in[t.slot], (t.turn + 1) * 16)
                            if positive(t.n - 1):
                                pe.wait_ge(q["z_out"], t.n - 1)
                            for c in range(4):
                                mm = nc.tensor.matmul(psZ[0:96, b % 2, P * c:P * c + n], Z[0:n, b, c, :], e.EQ[0:n, b, 0:n],
                                                      start=True, stop=True)
                            mm.then_inc(q["z_turned"], 1)
                        t = tile(3)
                        if t:
                            n, b = t.rows, t.slot
                            pe.wait_ge(norm.done, t.n + 1)
                            pe.wait_ge(e.ea_in[t.slot], (t.turn + 1) * 16)
                            if positive(t.n):
                                pe.wait_ge(q["hid_out"], t.n)
                            if positive(t.n):
                                pe.wait_ge(q["ht_out"], t.n)
                            if positive(t.n):
                                pe.wait_ge(q["vt_out"], t.n)
                            nc.tensor.transpose(psL[0:10, 0:n], e.EA[0:n, b, 0:10], ident[0:n, 0:n])
                            nc.tensor.transpose(psT[0:S, 0:n], H[0:n, b, 0:S], ident[0:n, 0:n])
                            nc.tensor.transpose(psT[0:96, P:P + n], H[0:n, b, S:D], ident[0:n, 0:n]).then_inc(q["turned"], 1)
                            pe.wait_ge(q["lt_out"], t.n + 1)
                            nc.tensor.matmul(psL[0:100, P:P + n], w("fcr1"), LT[:, b, 0:n], start=True, stop=True)\
                                .then_inc(q["hidden"], 1)
                            pe.wait_ge(q["ht_out"], t.n + 1)
                            pe.wait_ge(q["vt_out"], t.n + 1)
                            if positive(t.n - 1):
                                pe.wait_ge(q["mix_out"], t.n - 1)
                            o = psM[0:n, b % 2, 0:2 * D].rearrange("p (k c) -> p k c", k=2)
                            nc.tensor.matmul(o[:, :, 0:S], HT[:, b, 0:n], w("l1_s").rearrange("p (k c) -> p k c", k=2), start=True, stop=True)
                            nc.tensor.matmul(o[:, :, S:D], VT[:, b, 0:n], w("l1_v").rearrange("p (k c) -> p k c", k=2), start=True, stop=True).then_inc(q["mixed"], 1)
                            pe.wait_ge(q["hid_out"], t.n + 1)
                            if positive(t.n):
                                pe.wait_ge(q["filter_out"], t.n)
                            nc.tensor.matmul(psW[0:n, 0:192], hidT[:, b, 0:n], w("fcr2"), start=True, stop=True).then_inc(q["filter"], 1)
                        t = tile(5)
                        if t:
                            n, b = t.rows, t.slot
                            pe.wait_ge(q["z_out"], t.n + 1)
                            if positive(t.n):
                                pe.wait_ge(q["result"], t.n)
                            o = psO[0:n, 0:2 * D].rearrange("p (k c) -> p k c", k=2)
                            nc.tensor.matmul(o[:, :, 0:S], ZT[:, b, 0, 0:n], WLs[:, :].rearrange("p (k c) -> p k c", k=2), start=True, stop=True)
                            for i in range(3):
                                mm = nc.tensor.matmul(o[:, :, S + i:D:3], ZT[:, b, 1 + i, 0:n], WLv[:, :].rearrange("p (k c) -> p k c", k=2), start=True, stop=True)
                            mm.then_inc(q["linear"], 1)
                    sweep(pe, tiles, full_tiles, last_edges, LAST, step)

        def layer0_edges():
            with nc.cleanup_on_exit(), ExitStack() as ph:
                tag, LAST = "e0", 6
                HALVES = 10

                def sb(name, shape, dt=F32):
                    return ph.enter_context(nc.sbuf_tensor(f"{tag}_{name}", shape, dt))

                def pb(name, shape):
                    return ph.enter_context(nc.psum_tensor(f"{tag}_{name}", shape, F32))
                e = EdgePhase(ph, tag, x, DST, SRC, x1, D, (EA4, EA16), (1, 2, 3, LAST), gathers=2)
                norm = Norm(ph, tag, 2)
                zero = sb("zero", [P, G * D])
                Zm, ZmT, CT = sb("Zm", [P, 2, 544]), sb("ZmT", [P, 2, 4, P]), sb("CT", [V, P])
                VR, VD = sb("VR", [P, 3, V]), sb("VD", [P, V])
                xs, a0, xsT, a0T = sb("xs", [P, NB, S]), sb("a0", [P, NB, S]), sb("xsT", [S, 2, P]), sb("a0T", [S, 2, P])
                ak = sb("ak", [P, NB, 3, S])
                outer_p, outer_t = sb("outer_p", [P, 2, 1024]), sb("outer_t", [P, 2, 512])
                o1, o2 = sb("o1", [P, 1024]), sb("o2", [P, 1024])
                prod = sb("prod", [P, 3, 2048])
                T4 = pb("T4", [P, 2048])
                psZ, psU, psM = pb("psZ", [P, 2, 512]), pb("psU", [P, 512]), pb("psM", [P, 512])
                q = {m: sem(f"{tag}_{m}") for m in (
                    "zero_set", "zm_pool", "vr", "vr1", "zm_turned", "c_turned", "zmt_out", "ct_out", "xs_out", "message", "a_out",
                    "a_turned", "a0t_out", "maps", "products", "u1", "piece", "o1", "o2", "o12", "half_turned", "half_out", "half_used",
                    "u0")}
                t3_zero, pe_passed = sem("t3_zero"), sem("e0_pe_passed")
                block = ph.enter_context(nc.Block())

                @block.sync
                def _(sp):
                    def step(tile):
                        e.loads(sp, tile, rows_used(e), q["zm_pool"], q["c_turned"])
                        t = tile(0)
                        if t:
                            if isinstance(t.n, int) and t.n == 0:
                                sp.wait_ge(q["zero_set"], 1)
                            t3_piece(sp, t)

                    def t3_piece(sp, t):
                        if isinstance(t.n, int) and t.n >= full_groups:
                            return
                        sp.dma_start(t3[bass.ds(t.n * (P * G), P * G), :].rearrange("(p g) c -> p (g c)", g=G), zero[:, :])\
                            .then_inc(t3_zero, 16)
                    sweep(sp, tiles, full_tiles, last_edges, LAST, step)
                    for g in range(min(tiles, full_groups), full_groups):
                        t3_piece(sp, Tile(g, 0, 0, P))
                    if groups > full_groups:
                        sp.dma_start(t3[full_groups * P * G:N, :].rearrange("(p g) c -> p (g c)", g=G), zero[0:last_parts, :])\
                            .then_inc(t3_zero, 16)
                    sp.wait_ge(t3_zero, 16 * groups)

                @block.gpsimd
                def _(pool):
                    nc.gpsimd.memset(zero[:, :], 0.0).then_inc(q["zero_set"], 1)

                    def piece(t, j):
                        n, b, buf = t.rows, t.slot, (5 * t.slot + j) % 2
                        if positive(t.n * HALVES + (2 * j - 2)):
                            pool.wait_ge(q["half_turned"], t.n * HALVES + (2 * j - 2))
                        if j < 4:
                            nc.gpsimd.tensor_tensor(outer_p[0:n, buf, :].rearrange("p (u v) -> p u v", v=S),
                                                    repeat(xs[0:n, b, 16 * j:16 * j + 16], 2, S), repeat(a0[0:n, b, :], 1, 16),
                                                    ALU.mult).then_inc(q["piece"], 1)
                            return
                        if positive(t.n * 5 + 4 - 4):
                            pool.wait_ge(q["piece"], t.n * 5 + 4 - 4)
                        for i, (o, s_) in enumerate(((outer_p[0:n, buf, :], None), (o1[0:n, :], q["o1"]), (o2[0:n, :], q["o2"]))):
                            ins = nc.gpsimd.tensor_tensor(o.rearrange("p (u v) -> p u v", v=V), repeat(ak[0:n, b, i, V:S], 2, V),
                                                          repeat(ak[0:n, b, i, 0:V], 1, V), ALU.mult)
                            if s_ is not None:
                                ins.then_inc(s_, 1)
                        pool.wait_ge(q["o2"], t.n + 1)
                        nc.gpsimd.tensor_tensor(o1[0:n, :], o1[0:n, :], o2[0:n, :], ALU.add).then_inc(q["o12"], 1)
                        pool.wait_ge(q["o12"], t.n + 1)
                        nc.gpsimd.tensor_tensor(outer_p[0:n, buf, :], outer_p[0:n, buf, :], o1[0:n, :], ALU.add).then_inc(q["piece"], 1)

                    def step(tile):
                        t = tile(5)
                        if t:
                            pool.wait_ge(q["u1"], (t.n + 1) * 3)
                            e.add_rows(pool, t, q["u0"])
                        t = tile(1)
                        if t:
                            if positive(t.n - (NB - 1)):
                                pool.wait_ge(q["zm_pool"], t.n - (NB - 1))
                            e.gather_rows(pool, t, norm.done)
                        t = tile(4)
                        if t:
                            pool.wait_ge(q["a_out"], t.n + 1)
                            for j in range(3):
                                piece(t, j)
                        t = tile(2)
                        if t:
                            n, b = t.rows, t.slot
                            pool.wait_ge(norm.done, t.n + 1)
                            pool.wait_ge(e.ea_in[t.slot], (t.turn + 1) * 16)
                            if positive(t.n):
                                pool.wait_ge(q["zm_pool"], t.n)
                            z = Zm[0:n, b % 2, :]
                            zi = z[:, P:512].rearrange("p (i c) -> p i c", i=3)
                            r, dist = e.EA[0:n, b, 0:3], e.EA[0:n, b, 3:4]
                            nc.gpsimd.tensor_tensor(VR[0:n], zi[:, :, 96:P], repeat(r, 2, V), ALU.mult).then_inc(q["vr"], 1)
                            nc.gpsimd.tensor_scalar(z[:, 0:S], z[:, S:P], dist, None, ALU.mult)
                            nc.gpsimd.tensor_tensor(zi[:, :, 0:S], repeat(z[:, S:P], 1, 3), repeat(r, 2, S), ALU.mult)
                            nc.gpsimd.tensor_scalar(zi[:, :, S:96], zi[:, :, 96:P], dist, None, ALU.mult)
                            pool.wait_ge(q["vr"], t.n + 1)
                            nc.gpsimd.tensor_tensor(VD[0:n], VR[0:n, 0], VR[0:n, 1], ALU.add).then_inc(q["vr1"], 1)
                            pool.wait_ge(q["vr1"], t.n + 1)
                            nc.gpsimd.tensor_tensor(z[:, 512:544], VD[0:n], VR[0:n, 2], ALU.add).then_inc(q["zm_pool"], 1)
                        t = tile(4)
                        if t:
                            for j in range(3, 5):
                                piece(t, j)
                    sweep(pool, tiles, full_tiles, last_edges, LAST, step)
                    pool.wait_ge(e.added, 16 * tiles)

                @block.scalar
                def _(act):
                    def half(t, h):
                        n = t.rows
                        act.wait_ge(q["half_turned"], t.n * HALVES + (h + 1))
                        if positive(t.n * HALVES + (h - 1)):
                            act.wait_ge(q["half_used"], t.n * HALVES + (h - 1))
                        nc.scalar.copy(outer_t[:, h % 2, :].rearrange("p (c q) -> p c q", c=4)[:, :, 0:n],
                                       psZ[:, (h + 1) % 2, :].rearrange("p (c q) -> p c q", c=4)[:, :, 0:n]).then_inc(q["half_out"], 1)

                    def step(tile):
                        t3_, t4_ = tile(3), tile(4)
                        if t3_:
                            n, b = t3_.rows, t3_.slot % 2
                            act.wait_ge(q["zm_turned"], t3_.n + 1)
                            if positive(t3_.n - 1):
                                act.wait_ge(q["message"], t3_.n - 1)
                            nc.scalar.copy(ZmT[:, b, :, 0:n], psZ[:, 0, :].rearrange("p (c q) -> p c q", c=4)[:, :, 0:n])\
                                .then_inc(q["zmt_out"], 1)
                            act.wait_ge(q["c_turned"], t3_.n + 1)
                            nc.scalar.copy(CT[:, 0:n], psM[0:V, 0:n]).then_inc(q["ct_out"], 1)
                            if positive(t3_.n - 1):
                                act.wait_ge(q["maps"], t3_.n - 1)
                            nc.scalar.copy(xsT[:, b, 0:n], psM[0:S, P:P + n]).then_inc(q["xs_out"], 1)
                        if t4_:
                            half(t4_, 0)
                            half(t4_, 1)
                        if t3_:
                            n, b = t3_.rows, t3_.slot
                            act.wait_ge(q["message"], t3_.n + 1)
                            if positive((t3_.n - (NB - 1)) * 5):
                                act.wait_ge(q["piece"], (t3_.n - (NB - 1)) * 5)
                            if positive((t3_.n - (NB - 1)) * 3):
                                act.wait_ge(q["products"], (t3_.n - (NB - 1)) * 3)
                            nc.scalar.copy(a0[0:n, b, :], psM[0:n, 2 * P:2 * P + S])
                            nc.scalar.copy(ak[0:n, b, :, 0:V], psM[0:n, 2 * P + S:2 * P + D].rearrange("p (i v) -> p i v", i=3))\
                                .then_inc(q["a_out"], 1)
                        if t4_:
                            half(t4_, 2)
                            half(t4_, 3)
                        if t3_:
                            n, b = t3_.rows, t3_.slot % 2
                            act.wait_ge(q["a_turned"], t3_.n + 1)
                            nc.scalar.copy(a0T[:, b, 0:n], psM[0:S, 0:n]).then_inc(q["a0t_out"], 1)
                        if t4_:
                            half(t4_, 4)
                            half(t4_, 5)
                        t = tile(2)
                        if t:
                            n, b = t.rows, t.slot
                            act.wait_ge(norm.ready, t.n + 1)
                            if positive(t.n - 1):
                                act.wait_ge(q["c_turned"], t.n - 1)
                            if positive(t.n - (NB - 1)):
                                act.wait_ge(q["a_turned"], t.n - (NB - 1))
                            z = Zm[0:n, b % 2, :]
                            zi = z[:, P:512].rearrange("p (i c) -> p i c", i=3)
                            norm.map(t, z[:, S:P], e.X[0:n, b, 0, 0:S], 0)
                            norm.map(t, zi[:, :, 96:P], e.X[0:n, b, 0, S:D].rearrange("p (u i) -> p i u", i=3), 0)
                            norm.map(t, xs[0:n, b, :], e.X[0:n, b, 1, 0:S], 1)
                            norm.map(t, ak[0:n, b, :, V:S], e.X[0:n, b, 1, S:D].rearrange("p (u i) -> p i u", i=3), 1)\
                                .then_inc(norm.done, 1)
                        if t4_:
                            for h in range(6, HALVES):
                                half(t4_, h)
                            n, b = t4_.rows, t4_.slot
                            act.wait_ge(q["half_used"], (t4_.n + 1) * HALVES)
                            if positive((t4_.n - (NB - 1)) * 16):
                                act.wait_ge(e.added, (t4_.n - (NB - 1)) * 16)
                            nc.scalar.copy(e.R[0:n, b, 0:S], psU[0:n, 0:S]).then_inc(q["u0"], 1)
                    sweep(act, tiles, full_tiles, last_edges, LAST, step)

                @block.tensor
                def _(pe):
                    wss = w("u_ss").rearrange("p (c n) -> p c n", n=S)
                    wvv = w("u_vv").rearrange("p (c n) -> p c n", n=S)

                    def turn(t, h):
                        n, buf = t.rows, (5 * t.slot + h // 2) % 2
                        pe.wait_ge(q["piece"], t.n * 5 + (h // 2 + 1))
                        if positive(t.n * HALVES + (h - 1)):
                            pe.wait_ge(q["half_out"], t.n * HALVES + (h - 1))
                        for c in range(4):
                            at = (h % 2) * 512 + c * P
                            tr = nc.tensor.transpose(psZ[:, (h + 1) % 2, c * P:c * P + n], outer_p[0:n, buf, at:at + P], ident[0:n, 0:n])
                        tr.then_inc(q["half_turned"], 1)

                    def use(t, h):
                        n = t.rows
                        pe.wait_ge(q["half_out"], t.n * HALVES + (h + 1))
                        if h == 0:
                            if positive(t.n):
                                pe.wait_ge(q["u0"], t.n)
                        for c in range(4):
                            k = 4 * h + c
                            mm = nc.tensor.matmul(psU[0:n, 0:S], outer_t[:, h % 2, c * P:c * P + n], wss[:, k, :] if k < 32 else wvv[:, k - 32, :],
                                                  start=(k == 0), stop=(k == 39))
                        mm.then_inc(q["half_used"], 1)

                    def step(tile):
                        t3_, t4_ = tile(3), tile(4)
                        if t3_:
                            n, b = t3_.rows, t3_.slot
                            pe.wait_ge(q["zm_pool"], t3_.n + 1)
                            pe.wait_ge(e.eq_in[t3_.slot], (t3_.turn + 1) * 16)
                            if positive((t3_.n - 1) * HALVES):
                                pe.wait_ge(q["half_out"], (t3_.n - 1) * HALVES)
                            z, eq = Zm[0:n, b % 2, :], e.EQ[0:n, b, 0:n]
                            for c in range(4):
                                mm = nc.tensor.matmul(psZ[:, 0, c * P:c * P + n], z[:, c * P:(c + 1) * P], eq, start=True, stop=True)
                            mm.then_inc(q["zm_turned"], 1)
                            if positive(t3_.n):
                                pe.wait_ge(q["a0t_out"], t3_.n)
                            nc.tensor.matmul(psM[0:V, 0:n], z[:, 512:544], eq, start=True, stop=True)
                            nc.tensor.transpose(psM[0:S, P:P + n], xs[0:n, b, :], ident[0:n, 0:n]).then_inc(q["c_turned"], 1)
                        if t4_:
                            turn(t4_, 0)
                            if t3_:
                                pe.wait_ge(q["zmt_out"], t3_.n + 1)
                            turn(t4_, 1)
                            use(t4_, 0)
                        if t3_:
                            n, b = t3_.rows, t3_.slot
                            pe.wait_ge(q["zmt_out"], t3_.n + 1)
                            pe.wait_ge(q["ct_out"], t3_.n + 1)
                            pe.wait_ge(q["xs_out"], t3_.n + 1)
                            if positive(t3_.n):
                                pe.wait_ge(q["a_out"], t3_.n)
                            nc.tensor.matmul(psM[0:n, 2 * P:2 * P + S], ZmT[:, b % 2, 0, 0:n], w("m_a"), start=True, stop=False)
                            nc.tensor.matmul(psM[0:n, 2 * P:2 * P + S], CT[:, 0:n], w("m_c"), start=False, stop=True)
                            for i in range(3):
                                at = 2 * P + S + V * i
                                mm = nc.tensor.matmul(psM[0:n, at:at + V], ZmT[:, b % 2, 1 + i, 0:n], w("m_b"), start=True, stop=True)
                            mm.then_inc(q["message"], 1)
                        if t4_:
                            turn(t4_, 2)
                            use(t4_, 1)
                            turn(t4_, 3)
                            use(t4_, 2)
                        if t3_:
                            n, b = t3_.rows, t3_.slot
                            pe.wait_ge(q["a_out"], t3_.n + 1)
                            pe.sem_inc(pe_passed, 1)
                            nc.tensor.transpose(psM[0:S, 0:n], a0[0:n, b, :], ident[0:n, 0:n]).then_inc(q["a_turned"], 1)
                        if t4_:
                            turn(t4_, 4)
                            use(t4_, 3)
                            turn(t4_, 5)
                            use(t4_, 4)
                        if t3_:
                            n, b = t3_.rows, t3_.slot % 2
                            pe.wait_ge(q["xs_out"], t3_.n + 1)
                            pe.wait_ge(q["a0t_out"], t3_.n + 1)
                            if positive(t3_.n * 3):
                                pe.wait_ge(q["products"], t3_.n * 3)
                            for c in range(2):
                                nc.tensor.matmul(T4[0:n, 512 * c:512 * c + 512], xsT[:, b, 0:n], w("u_sv")[:, 512 * c:512 * c + 512],
                                                 start=True, stop=True)
                            for c in range(2):
                                mm = nc.tensor.matmul(T4[0:n, 1024 + 512 * c:1536 + 512 * c], a0T[:, b, 0:n],
                                                      w("u_vs")[:, 512 * c:512 * c + 512], start=True, stop=True)
                            mm.then_inc(q["maps"], 1)
                        if t4_:
                            for h in range(6, HALVES):
                                turn(t4_, h)
                                use(t4_, h - 1)
                            use(t4_, HALVES - 1)
                    sweep(pe, tiles, full_tiles, last_edges, LAST, step)

                @block.vector
                def _(dve):
                    def step(tile):
                        t = tile(4)
                        if t:
                            n, b = t.rows, t.slot
                            dve.wait_ge(q["maps"], t.n + 1)
                            dve.wait_ge(q["a_out"], t.n + 1)
                            t4 = T4[0:n, :].rearrange("p (k w) -> p k w", w=V)
                            for i in range(3):
                                if positive((t.n - 1) * 3 + (i + 1)):
                                    dve.wait_ge(q["u1"], (t.n - 1) * 3 + (i + 1))
                                nc.vector.tensor_tensor(prod[0:n, i, :].rearrange("p (k w) -> p k w", w=V), t4,
                                                        repeat(ak[0:n, b, i, :], 2, V), ALU.mult).then_inc(q["products"], 1)
                        t2 = tile(2)
                        if t2:
                            dve.wait_ge(e.rows_in[t2.slot], (t2.turn + 1) * 32)
                            norm.on_vector(dve, t2, [e.X[0:t2.rows, t2.slot, g, :] for g in range(2)])
                        if t:
                            if positive((t.n - (NB - 1)) * 16):
                                dve.wait_ge(e.added, (t.n - (NB - 1)) * 16)
                            for i in range(3):
                                dve.wait_ge(q["products"], t.n * 3 + (i + 1))
                                nc.vector.tensor_reduce(e.R[0:n, b, S + i:D:3], prod[0:n, i, :].rearrange("p (k w) -> p w k", w=V),
                                                        AX_X, ALU.add).then_inc(q["u1"], 1)
                    sweep(dve, tiles, full_tiles, last_edges, LAST, step)

        dense_phase("d0", 0)
        layer0_edges()
        dense_phase("d1", 1)
        layer1_edges()
        dense_phase("d2", 2)
        layer2_edges()
        layer3_edges()
        dense_phase("d3", 3)


def kernel(**inputs):
    import numpy as _np
    import concourse.bacc as _bacc
    from concourse.bass_utils import run_bass_kernel_spmd as _run

    a = {k: _np.asarray(v) for k, v in inputs.items()}
    N, E = a["x"].shape[0], a["src"].shape[0]

    def kron(m):
        o = _np.zeros((3 * m.shape[0], 3 * m.shape[1]), m.dtype)
        for i in range(3):
            o[i::3, i::3] = m
        return o

    def apart(m):
        r, c = m.shape
        o = _np.zeros((3 * r, 3 * c), m.dtype)
        for i in range(3):
            o[i::3, i * c:(i + 1) * c] = m
        return o

    def chunks(m):
        return m.reshape(-1, P, m.shape[-1]).transpose(1, 0, 2).reshape(P, -1)

    rows, cols = (lambda *m: _np.concatenate(m, 0)), (lambda *m: _np.concatenate(m, 1))
    l0, l1, l2, l3 = (lambda k, g=g: a[f"L{g}_gnn_{k}"] for g in range(4))
    blocks = {
        "u_ss": chunks(l0("Wu_ss").reshape(S * S, S)), "u_vv": chunks(l0("Wu_vv").reshape(V * V, S)),
        "u_sv": l0("Wu_sv").reshape(S, V * V), "u_vs": l0("Wu_vs").transpose(1, 0, 2).reshape(S, V * V),
        "m_a": rows(l0("Wm_ss"), l0("Lm_s")), "m_c": l0("Wm_vv"), "m_b": rows(l0("Wm_sv"), l0("Wm_vs"), l0("Lm_v")),
        "lu_s": l0("Lu_s"), "lu_v": kron(l0("Lu_v")),
        "skip_s": l1("W_skip0"), "skip_v": kron(l1("W_skip1")), "nl_s": l1("W_nl0"), "nl_v": apart(l1("W_nl1")),
        "fc1": l1("W_fc1"), "fc2": l1("W_fc2"), "out_s": l1("W_out_s"), "out_v": l1("W_out_v"),
        "l2_s": rows(l2("W_ss"), l2("W_vv")), "l2_v": rows(l2("W_sv"), l2("W_vs")),
        "rad": rows(l2("W_rad").T, l2("b_rad").reshape(1, -1)), "l2l_s": l2("L_s"), "l2l_v": kron(l2("L_v")),
        "sc_s": cols(l3("Ws_sc_a"), l3("Ws_sc_c")), "sc_v": cols(kron(l3("Wv_sc_a")), kron(l3("Wv_sc_c"))),
        "l1_s": cols(l3("Ws_l1_a"), l3("Ws_l1_c")), "l1_v": cols(apart(l3("Wv_l1_a")), apart(l3("Wv_l1_c"))),
        "fcr1": l3("W_fc1"), "fcr2": l3("W_fc2"),
        "l2aT_s": l3("Ws_l2_a").T, "l2cT_s": l3("Ws_l2_c").T, "l2aT_v": l3("Wv_l2_a").T, "l2cT_v": l3("Wv_l2_c").T,
        "l3_s": l3("Ws_l3"), "l3_v": l3("Wv_l3"),
    }
    start, width = weight_columns()
    wpack, wscale = _np.zeros((P, width), _np.float32), _np.zeros((P, width), _np.float32)
    for name, (r, c, scales) in weight_blocks().items():
        assert blocks[name].shape == (r, c), name
        wpack[0:r, start[name]:start[name] + c] = blocks[name]
        for r0, r1, c0, c1, s in scales:
            wscale[r0:r1, start[name] + c0:start[name] + c1] = s
    consts = _np.zeros((P, K_WIDTH), _np.float32)
    consts[:, K_IDENT:K_IDENT + P] = _np.eye(P)
    consts[:, K_LOWER:K_LOWER + P] = _np.tril(_np.ones((P, P)), -1)
    consts[:, K_JUNK] = N + _np.arange(P)
    consts[:, K_EPS] = EPS
    idx2 = _np.ascontiguousarray(_np.stack([a["src"], a["dst"]], 1))
    arrays = {
        "x": a["x"], "idx2": idx2, "idx2T": _np.ascontiguousarray(idx2.T),
        "ea": _np.ascontiguousarray(cols(a["edge_attr_10"], a["edge_attr_4"], a["edge_attr_16"], a["edge_attr_3"], a["edge_attr_64"])),
        "nattr": _np.pad(cols(a["node_vec1"], a["node_vec1_n2"], a["node_vec1_n3"]), ((0, P), (0, 0))),
        "wpack": wpack, "wscale": wscale, "consts": consts,
    }
    nc = _bacc.Bacc("TRN2", target_bir_lowering=False, num_devices=1)
    args = {k: nc.dram_tensor(k, v.shape, mybir.dt.from_np(v.dtype), kind="ExternalInput").ap() for k, v in arrays.items()}
    out = nc.dram_tensor("out", (N, D), F32, kind="ExternalOutput").ap()
    build(nc, N, E, out=out, **args)
    r = _run(nc, [arrays], core_ids=[0])
    return r.results[0]["out"]
```

```python
from contextlib import ExitStack

import numpy as np

import concourse.bass as bass
from concourse import mybir

F32 = mybir.dt.float32
I32 = mybir.dt.int32
ALU = mybir.AluOpType
ACT = mybir.ActivationFunctionType
AX_X = mybir.AxisListType.X

P = 128
S, V = 64, 32
D = S + 3 * V
G = 4
NB = 6
EPS = 1e-5

EA10, EA4, EA16, EA3, EA64, EAW = 0, 10, 14, 30, 33, 97
K_IDENT, K_LOWER, K_JUNK, K_EPS, K_WIDTH = 0, P, 2 * P, 2 * P + 1, 2 * P + 2

INV_SQRT3 = 3.0 ** -0.5
INV_SQRT32 = 32.0 ** -0.5
INV_SQRT2 = 2.0 ** -0.5
C_S = float(np.sin(np.pi / 8.0))
C_X = float(np.cos(np.pi / 8.0))


def weight_blocks():
    def one(r, c, scale=1.0):
        return (r, c, [(0, r, 0, c, scale)])
    msg_v = INV_SQRT3 * INV_SQRT32
    return {
        "u_ss": one(P, 2048, 1 / 64), "u_vv": one(P, 512, INV_SQRT3 / 32),
        "u_sv": one(S, 1024, 2048.0 ** -0.5), "u_vs": one(S, 1024, 2048.0 ** -0.5),
        "m_a": one(P, S, 0.125), "m_c": one(V, S, msg_v),
        "m_b": (P, V, [(0, S, 0, V, 0.125), (S, P, 0, V, INV_SQRT32)]),
        "lu_s": one(S, S, 0.125), "lu_v": one(96, 96, INV_SQRT32),
        "skip_s": one(S, 96), "skip_v": one(96, 96), "nl_s": one(S, S), "nl_v": one(96, 96),
        "fc1": one(64, 64), "fc2": one(64, 224), "out_s": one(96, 96, 1 / 32),
        "out_v": (P, V, [(0, 96, 0, V, 1 / 32), (96, P, 0, V, INV_SQRT2 / 32)]),
        "l2_s": (96, S, [(0, S, 0, S, INV_SQRT2 / 8), (S, 96, 0, S, msg_v * INV_SQRT2)]),
        "l2_v": (96, V, [(0, S, 0, V, INV_SQRT3 / 8 * INV_SQRT2), (S, 96, 0, V, msg_v * INV_SQRT2)]),
        "rad": one(17, D), "l2l_s": one(S, S, 0.125), "l2l_v": one(96, 96, INV_SQRT32),
        "sc_s": one(S, 2 * S, C_S), "sc_v": one(96, 192, C_S), "l1_s": one(S, 2 * S), "l1_v": one(96, 192),
        "fcr1": one(10, 100), "fcr2": one(100, 192),
        "l2aT_s": (96, 96, [(0, 96, 0, 64, 1.0), (0, 96, 64, 96, INV_SQRT3)]),
        "l2cT_s": (96, 96, [(0, 96, 0, 64, 1.0), (0, 96, 64, 96, INV_SQRT3)]),
        "l2aT_v": one(96, 96), "l2cT_v": one(96, 96),
        "l3_s": one(96, S, C_X / 4), "l3_v": one(96, V, C_X / 4),
    }


def weight_columns():
    at, start = 0, {}
    for name, (_, cols, _) in weight_blocks().items():
        start[name] = at
        at += cols
    return start, at


class Tile:

    def __init__(self, n, slot, turn, rows):
        self.n, self.slot, self.turn, self.rows = n, slot, turn, rows


def sweep(eng, total, full, last_rows, deepest, step):
    def straight(k):
        def tile(lag):
            n = k - lag
            if n < 0 or n >= total:
                return None
            return Tile(n, n % NB, n // NB, P if n < full else last_rows)
        step(tile)

    first = NB * (-(-(deepest + NB) // NB))
    turns = max(0, (full - first) // NB)
    if turns < 2:
        turns = 0
    else:
        for k in range(first):
            straight(k)
        with eng.Fori(0, turns) as j:
            for u in range(NB):
                def tile(lag, k=first + u):
                    n = k - lag
                    return Tile(j * NB + n, n % NB, j + n // NB, P)
                step(tile)
    for k in range(first + turns * NB if turns else 0, total + deepest):
        straight(k)


def positive(count):
    return not isinstance(count, int) or count > 0


def repeat(ap, axis, n):
    shape = list(ap.shape)
    shape.insert(axis, n)
    return ap.unsqueeze(axis).broadcast_to(shape)


def build(nc, N, E, x, idx2, idx2T, ea, nattr, wpack, wscale, consts, out):
    NJ = N + P
    tiles, full_tiles = -(-E // P), E // P
    last_edges = E - (tiles - 1) * P
    groups, full_groups = -(-N // (P * G)), N // (P * G)
    last_parts = (N - (groups - 1) * P * G) // G
    assert N == E * G
    WCOL, WWIDTH = weight_columns()
    BLOCKS = weight_blocks()

    def table(name, cols, rows=NJ, dt=F32):
        return nc.dram_tensor(name, (rows, cols), dt, kind="Internal").ap()

    x1, p1, h2, x3, t3 = table("x1", D), table("p1", 192), table("h2", D, N), table("x3", D), table("t3", D)
    same = table("same", 2 * P, tiles * P)
    unique = table("unique", 2, tiles * P, I32)

    outer = ExitStack()
    with outer:
        def sem(name):
            return nc.alloc_semaphore(name=name)

        def ring_sems(name, n=NB):
            return [sem(f"{name}{i}") for i in range(n)]

        W = outer.enter_context(nc.sbuf_tensor("W", [P, WWIDTH], F32))
        K = outer.enter_context(nc.sbuf_tensor("K", [P, K_WIDTH], F32))
        WLs = outer.enter_context(nc.sbuf_tensor("WLs", [96, 2 * S], F32))
        WLv = outer.enter_context(nc.sbuf_tensor("WLv", [96, 2 * V], F32))
        ident = K[:, K_IDENT:K_IDENT + P]
        lower = K[:, K_LOWER:K_LOWER + P]
        junk = K[:, K_JUNK:K_JUNK + 1]
        epsilon = K[:, K_EPS:K_EPS + 1]

        def w(name):
            r, c, _ = BLOCKS[name]
            return W[0:r, WCOL[name]:WCOL[name] + c]

        with nc.cleanup_on_exit(), ExitStack() as ph:
            scale = ph.enter_context(nc.sbuf_tensor("scale", [P, WWIDTH], F32))
            zero = ph.enter_context(nc.sbuf_tensor("zero", [P, 192], F32))
            pl = ph.enter_context(nc.psum_tensor("pl", [P, 512], F32))
            weights_in, zeroed, junk_clean = sem("weights_in"), sem("zeroed"), sem("junk_clean")
            scaled, folded, folded_out, with_identity = sem("scaled"), sem("folded"), sem("folded_out"), sem("with_identity")
            block = ph.enter_context(nc.Block())

            @block.sync
            def _(sp):
                sp.dma_start(W[:, :], wpack).then_inc(weights_in, 16)
                sp.dma_start(scale[:, :], wscale).then_inc(weights_in, 16)
                sp.dma_start(K[:, :], consts).then_inc(weights_in, 16)
                sp.wait_ge(zeroed, 1)
                for t in (x1, p1, x3, t3):
                    sp.dma_start(t[N:NJ, :], zero[:, 0:t.shape[1]]).then_inc(junk_clean, 16)
                sp.wait_ge(junk_clean, 64)

            @block.vector
            def _(dve):
                nc.vector.memset(zero[:, :], 0.0).then_inc(zeroed, 1)
                dve.wait_ge(weights_in, 48)
                nc.vector.tensor_tensor(W[:, :], W[:, :], scale[:, :], ALU.mult).then_inc(scaled, 1)
                dve.wait_ge(scaled, 1)
                nc.vector.tensor_tensor(w("lu_s"), w("lu_s"), ident[0:S, 0:S], ALU.add).then_inc(with_identity, 1)
                nc.vector.tensor_tensor(w("lu_v"), w("lu_v"), ident[0:96, 0:96], ALU.add).then_inc(with_identity, 1)
                dve.wait_ge(folded, 1)
                nc.vector.tensor_copy(WLs[:, :], pl[0:96, 0:2 * S]).then_inc(folded_out, 1)
                nc.vector.tensor_copy(WLv[:, :], pl[0:96, 2 * S:2 * S + 2 * V]).then_inc(folded_out, 1)
                dve.wait_ge(folded_out, 2)
                dve.wait_ge(with_identity, 2)

            @block.tensor
            def _(pe):
                pe.wait_ge(scaled, 1)
                for n, (a, b, at, m) in enumerate((("l2aT_s", "l3_s", 0, S), ("l2cT_s", "l3_s", S, S),
                                                   ("l2aT_v", "l3_v", 2 * S, V), ("l2cT_v", "l3_v", 2 * S + V, V))):
                    mm = nc.tensor.matmul(pl[0:96, at:at + m], w(a), w(b), start=True, stop=True)
                mm.then_inc(folded, 1)

        NEWTON = 10

        def inverse_root(dve, t, steps, v, bits, tmp, y, at):
            if at:
                if positive(t.n * (NEWTON + 1) + at):
                    dve.wait_ge(steps, t.n * (NEWTON + 1) + at)
            if at == 0:
                ins = nc.vector.tensor_scalar(bits, v.bitcast(I32), 1, None, ALU.logical_shift_right)
            elif at == 1:
                ins = nc.vector.tensor_scalar(y.bitcast(I32), bits, -1.0, float(0x5F3759DF), ALU.mult, ALU.add)
            elif at % 3 == 2:
                ins = nc.vector.scalar_tensor_tensor(tmp, y, -0.5, y, ALU.mult, ALU.mult)
            elif at % 3 == 0:
                ins = nc.vector.tensor_tensor(tmp, tmp, v, ALU.mult)
            else:
                ins = nc.vector.scalar_tensor_tensor(y, tmp, 1.5, y, ALU.add, ALU.mult)
            ins.then_inc(steps, 1)

        class Norm:

            def __init__(self, ph, tag, parts, newton=False):
                def sb(name, shape, dt=F32):
                    return ph.enter_context(nc.sbuf_tensor(f"{tag}_{name}", shape, dt))
                self.parts = parts
                self.bn, self.mv = sb("bn", [P, 2, parts, 6]), sb("mv", [P, NB, parts, 2])
                self.var, self.tmp, self.bits = sb("var", [P, NB, parts]), sb("tmp", [P, parts]), sb("bits", [P, parts], I32)
                self.rstd, self.shift = sb("rstd", [P, NB, parts]), sb("shift", [P, NB, parts])
                self.stats, self.moments = sem(f"{tag}_stats"), sem(f"{tag}_moments")
                self.widened, self.steps, self.inverted = sem(f"{tag}_widened"), sem(f"{tag}_steps"), sem(f"{tag}_inverted")
                self.passed = sem(f"{tag}_dve_passed")
                self.ready, self.done = sem(f"{tag}_norm_ready"), sem(f"{tag}_norm_done")

            def statistics(self, dve, t, views):
                n, b = t.rows, t.slot
                if positive(t.n - (NB - 1)):
                    dve.wait_ge(self.done, t.n - (NB - 1))
                for q, v in enumerate(views):
                    ins = nc.vector.bn_stats(self.bn[0:n, b % 2, q, :], v)
                ins.then_inc(self.stats, 1)
                dve.wait_ge(self.stats, t.n + 1)
                dve.sem_inc(self.passed, 1)
                for q in range(self.parts):
                    ins = nc.vector.bn_aggr(self.mv[0:n, b, q, :], self.bn[0:n, b % 2, q, :])
                ins.then_inc(self.moments, 1)

            def root(self, act, t):
                n, b = t.rows, t.slot
                act.wait_ge(self.moments, t.n + 1)
                nc.scalar.activation(self.var[0:n, b, :], self.mv[0:n, b, :, 1], ACT.Sqrt, bias=epsilon[0:n, :])\
                    .then_inc(self.widened, 1)

            def scales(self, dve, t):
                n, b = t.rows, t.slot
                dve.wait_ge(self.widened, t.n + 1)
                nc.vector.reciprocal(self.rstd[0:n, b, :], self.var[0:n, b, :]).then_inc(self.inverted, 1)
                dve.wait_ge(self.inverted, t.n + 1)
                self.shifts(dve, t)

            def widen(self, dve, t):
                n, b = t.rows, t.slot
                dve.wait_ge(self.moments, t.n + 1)
                nc.vector.tensor_scalar(self.var[0:n, b, :], self.mv[0:n, b, :, 1], EPS, None, ALU.add).then_inc(self.widened, 1)
                dve.wait_ge(self.widened, t.n + 1)

            def newton(self, dve, t, at):
                n, b = t.rows, t.slot
                inverse_root(dve, t, self.steps, self.var[0:n, b, :], self.bits[0:n], self.tmp[0:n], self.rstd[0:n, b, :], at)

            def on_vector(self, dve, t, views):
                self.statistics(dve, t, views)
                self.widen(dve, t)
                for at in range(NEWTON + 1):
                    self.newton(dve, t, at)
                self.newton_shifts(dve, t)

            def newton_shifts(self, dve, t):
                if positive((t.n + 1) * (NEWTON + 1)):
                    dve.wait_ge(self.steps, (t.n + 1) * (NEWTON + 1))
                self.shifts(dve, t)

            def shifts(self, dve, t):
                n, b = t.rows, t.slot
                nc.vector.scalar_tensor_tensor(self.shift[0:n, b, :], self.mv[0:n, b, :, 0], -1.0, self.rstd[0:n, b, :],
                                               ALU.mult, ALU.mult).then_inc(self.ready, 1)

            def map(self, t, out_ap, in_ap, q):
                n, b = t.rows, t.slot
                return nc.scalar.activation(out_ap, in_ap, ACT.Relu, bias=self.shift[0:n, b, q:q + 1],
                                            scale=self.rstd[0:n, b, q:q + 1])

        def rows_of(tab, t):
            return tab[bass.ds(t.n * (P * G), t.rows * G), :].rearrange("(p g) c -> p g c", g=G)

        def dense_phase(tag, kind):
            newton = kind == 2
            STATS = 3 if kind == 2 else 1
            MAP = STATS + (1 if newton else 2)
            TURN, MUL, STORE = MAP + 1, MAP + 2, MAP + 3
            source = (x, x1, x1, x3)[kind]
            width = (D, 192, D, 2 * D)[kind]
            banks = 4 if kind == 3 else 2
            per_bank = G // banks
            weights = (("lu_s", "lu_v"), ("skip_s", "skip_v"), ("l2l_s", "l2l_v"), ("sc_s", "sc_v"))[kind]
            sums = 1 if kind == 3 else 2
            loads = (1, 1, 2, 3)[kind]
            with nc.cleanup_on_exit(), ExitStack() as ph:
                def sb(name, shape, dt=F32):
                    return ph.enter_context(nc.sbuf_tensor(f"{tag}_{name}", shape, dt))
                X, H = sb("X", [P, NB, G, D]), sb("H", [P, NB, G, D])
                HsT, HvT = sb("HsT", [S, 2, 512]), sb("HvT", [96, 2, 512])
                Y = sb("Y", [P, NB, G, 192 if kind == 1 else D])
                if kind == 0:
                    col, row = sb("col", [P, NB, 2], I32), sb("row", [P, NB, 2, P], I32)
                    eq, early = sb("eq", [P, NB, 2, P]), sb("early", [P, 2, 2, P])
                    off, rep, moved = sb("off", [P, 2]), sb("rep", [P, 2]), sb("moved", [P, 2])
                    uniq = sb("uniq", [P, NB, 2], I32)
                    index_in, index_stored = ring_sems("ix_in"), ring_sems("ix_stored")
                    ix = {n: sem("ix_" + n) for n in ("compared", "masked", "counted", "offset", "moved", "ready")}
                if kind == 2:
                    Pt, Gt, X2 = sb("Pt", [P, NB, G, 192]), sb("Gt", [P, 2, G, 96]), sb("X2", [P, NB, G, D])
                if kind == 3:
                    T3, NA, XT = sb("T3", [P, NB, G, D]), sb("NA", [P, NB, G, 3]), sb("XT", [P, NB, G, D])
                    A1 = sb("A1", [P, 2, G, D])
                psS = ph.enter_context(nc.psum_tensor(f"{tag}_psS", [P, 2, 512], F32))
                psV = ph.enter_context(nc.psum_tensor(f"{tag}_psV", [P, 2, 512], F32))
                psO = ph.enter_context(nc.psum_tensor(f"{tag}_psO", [P, sums, banks, 512], F32))
                norm = Norm(ph, tag, G)
                loaded, stored = ring_sems(f"{tag}_loaded"), ring_sems(f"{tag}_stored")
                turned, s_out, v_out = sem(f"{tag}_turned"), sem(f"{tag}_s_out"), sem(f"{tag}_v_out")
                product, summed = sem(f"{tag}_product"), sem(f"{tag}_summed")
                if kind >= 2:
                    gates, gated, residual_ready, part_a = (sem(f"{tag}_{n}") for n in ("gates", "gated", "residual_ready", "part_a"))
                block = ph.enter_context(nc.Block())

                @block.sync
                def _(sp):
                    def step(tile):
                        t = tile(0)
                        if t:
                            n, b = t.rows, t.slot
                            if kind == 1:
                                if positive(t.n - (NB - 1)):
                                    sp.wait_ge(norm.done, t.n - (NB - 1))
                            if kind >= 2:
                                if positive(t.n - (NB - 1)):
                                    sp.wait_ge(residual_ready, t.n - (NB - 1))
                            if kind == 3:
                                if positive(t.n - (NB - 1)):
                                    sp.wait_ge(norm.done, t.n - (NB - 1))
                            if kind in (0, 3):
                                if positive(t.n - (NB - 1)):
                                    sp.wait_ge(summed, t.n - (NB - 1))
                            sp.dma_start(X[0:n, b, :, :], rows_of(source, t)).then_inc(loaded[b], 16)
                            if kind == 2:
                                sp.dma_start(Pt[0:n, b, :, :], rows_of(p1, t)).then_inc(loaded[b], 16)
                            if kind == 3:
                                sp.dma_start(T3[0:n, b, :, :], rows_of(t3, t)).then_inc(loaded[b], 16)
                                sp.dma_start(NA[0:n, b, :, :], rows_of(nattr, t)).then_inc(loaded[b], 16)
                        t = tile(STORE)
                        if t:
                            n, b = t.rows, t.slot
                            sp.wait_ge(summed, t.n + 1)
                            target = (x1, p1, x3, out)[kind]
                            sp.dma_start(rows_of(target, t), Y[0:n, b, :, :]).then_inc(stored[b], 16)
                            if kind == 2:
                                sp.dma_start(rows_of(h2, t), H[0:n, b, :, :]).then_inc(stored[b], 16)
                        if kind == 0:
                            index_step(tile)

                    def index_step(tile):
                        t = tile(0)
                        if t:
                            n, b = t.rows, t.slot
                            if positive(t.n - (NB - 1)):
                                sp.wait_ge(ix["ready"], t.n - (NB - 1))
                            sp.dma_start(col[0:n, b, :], idx2[bass.ds(t.n * P, n), :]).then_inc(index_in[b], 16)
                            for a in range(2):
                                sp.dma_start(row[0:n, b, a, 0:n], idx2T[a:a + 1, bass.ds(t.n * P, n)].broadcast_to([n, n]))\
                                  .then_inc(index_in[b], 16)
                        t = tile(5)
                        if t:
                            n, b = t.rows, t.slot
                            sp.wait_ge(ix["ready"], t.n + 1)
                            sp.dma_start(unique[bass.ds(t.n * P, n), :], uniq[0:n, b, :]).then_inc(index_stored[b], 16)
                            sp.dma_start(same[bass.ds(t.n * P, n), :].rearrange("p (a q) -> p a q", a=2)[:, :, 0:n],
                                         eq[0:n, b, :, 0:n]).then_inc(index_stored[b], 16)
                    sweep(sp, groups, full_groups, last_parts, STORE, step)
                    for b in range(NB):
                        sp.wait_ge(stored[b], (32 if kind == 2 else 16) * ((groups - 1 - b) // NB + 1))
                        if kind == 0:
                            sp.wait_ge(index_stored[b], 32 * ((tiles - 1 - b) // NB + 1))

                @block.scalar
                def _(act):
                    def step(tile):
                        t = tile(MAP)
                        if t:
                            n, b = t.rows, t.slot
                            act.wait_ge(norm.ready, t.n + 1)
                            if kind == 2:
                                if positive(t.turn):
                                    act.wait_ge(stored[t.slot], t.turn * 32)
                            else:
                                if positive(t.n - (NB - 1)):
                                    act.wait_ge(turned, t.n - (NB - 1))
                            src = X2 if kind == 2 else X
                            for q in range(G):
                                ins = norm.map(t, H[0:n, b, q, :], src[0:n, b, q, :], q)
                            ins.then_inc(norm.done, 1)
                        t = tile(STATS + 1)
                        if t and not newton:
                            norm.root(act, t)
                        t = tile(1)
                        if t and kind == 2:
                            n, b = t.rows, t.slot
                            act.wait_ge(loaded[t.slot], (t.turn + 1) * (16 * (loads)))
                            if positive(t.n - 1):
                                act.wait_ge(gated, t.n - 1)
                            nc.scalar.activation(Gt[0:n, b % 2, :, :], Pt[0:n, b, :, 0:96], ACT.Sigmoid)\
                                .then_inc(gates, 1)
                        t = tile(TURN)
                        if t:
                            b = t.slot % 2
                            act.wait_ge(turned, t.n + 1)
                            if positive(t.n - 1):
                                act.wait_ge(product, t.n - 1)
                            nc.scalar.copy(HvT[:, b, 0:G * t.rows], psV[0:96, b, 0:G * t.rows]).then_inc(v_out, 1)
                            nc.scalar.copy(HsT[:, b, 0:G * t.rows], psS[0:S, b, 0:G * t.rows]).then_inc(s_out, 1)
                    sweep(act, groups, full_groups, last_parts, STORE, step)

                @block.tensor
                def _(pe):
                    ws, wv = w(weights[0]), w(weights[1])
                    if kind == 3:
                        ws, wv = ws.rearrange("p (k c) -> p k c", k=2), wv.rearrange("p (k c) -> p k c", k=2)

                    def step(tile):
                        t = tile(TURN)
                        if t:
                            n, b = t.rows, t.slot
                            pe.wait_ge(norm.done, t.n + 1)
                            if positive(t.n - 1):
                                pe.wait_ge(s_out, t.n - 1)
                            if positive(t.n - 1):
                                pe.wait_ge(v_out, t.n - 1)
                            for q in range(G):
                                nc.tensor.transpose(psV[0:96, b % 2, q * n:(q + 1) * n], H[0:n, b, q, S:D], ident[0:n, 0:n])
                                tr = nc.tensor.transpose(psS[0:S, b % 2, q * n:(q + 1) * n], H[0:n, b, q, 0:S], ident[0:n, 0:n])
                            tr.then_inc(turned, 1)
                        t = tile(MUL)
                        if t:
                            n, b = t.rows, t.slot
                            pe.wait_ge(s_out, t.n + 1)
                            pe.wait_ge(v_out, t.n + 1)
                            if positive(t.n - (sums - 1)):
                                pe.wait_ge(summed, t.n - (sums - 1))
                            for q in range(G):
                                o = psO[0:n, b % sums, q // per_bank, (q % per_bank) * width:(q % per_bank + 1) * width]
                                if kind == 3:
                                    o = o.rearrange("p (k c) -> p k c", k=2)
                                    os_, ov = o[:, :, 0:S], o[:, :, S:D]
                                else:
                                    ns = 96 if kind == 1 else S
                                    os_, ov = o[:, 0:ns], o[:, ns:width]
                                nc.tensor.matmul(os_, HsT[:, b % 2, q * n:(q + 1) * n], ws, start=True, stop=True)
                                mm = nc.tensor.matmul(ov, HvT[:, b % 2, q * n:(q + 1) * n], wv, start=True, stop=True)
                            mm.then_inc(product, 1)
                    sweep(pe, groups, full_groups, last_parts, STORE, step)

                if kind == 0:
                    @block.gpsimd
                    def _(pool):
                        def step(tile):
                            t = tile(3)
                            if t:
                                n, b = t.rows, t.slot
                                pool.wait_ge(ix["compared"], t.n + 1)
                                if positive(t.n - 1):
                                    pool.wait_ge(ix["counted"], t.n - 1)
                                nc.gpsimd.tensor_tensor(early[0:n, b % 2, :, 0:n], eq[0:n, b, :, 0:n],
                                                        repeat(lower[0:n, 0:n], 1, 2), ALU.mult).then_inc(ix["masked"], 1)
                        sweep(pool, groups, full_groups, last_parts, STORE, step)

                if kind >= 2:
                    @block.gpsimd
                    def _(pool):
                        def step(tile):
                            t = tile(2 if kind == 2 else 1)
                            if not t:
                                return
                            n, b = t.rows, t.slot
                            if kind == 2:
                                pool.wait_ge(gates, t.n + 1)
                                g = Gt[0:n, b % 2, :, :]
                                pv = Pt[0:n, b, :, 96:192].rearrange("p g (k i) -> p g k i", i=3)
                                nc.gpsimd.tensor_tensor(Pt[0:n, b, :, 0:S], Pt[0:n, b, :, 0:S], g[:, :, 0:S], ALU.mult)
                                for q in range(G):
                                    ins = nc.gpsimd.tensor_tensor(pv[:, q], pv[:, q], repeat(g[:, q, S:96], 2, 3), ALU.mult)
                                ins.then_inc(gated, 1)
                                pool.wait_ge(gated, t.n + 1)
                                if positive(t.n - (NB - 1)):
                                    pool.wait_ge(summed, t.n - (NB - 1))
                                nc.gpsimd.tensor_tensor(X2[0:n, b, :, 0:S], Pt[0:n, b, :, 0:S], X[0:n, b, :, 0:S], ALU.add)
                                nc.gpsimd.tensor_tensor(X2[0:n, b, :, S:D], Pt[0:n, b, :, 96:192], X[0:n, b, :, S:D], ALU.add)\
                                    .then_inc(residual_ready, 1)
                            else:
                                pool.wait_ge(loaded[t.slot], (t.turn + 1) * (16 * (loads)))
                                if positive(t.n - (NB - 1)):
                                    pool.wait_ge(summed, t.n - (NB - 1))
                                nc.gpsimd.tensor_tensor(XT[0:n, b, :, :], X[0:n, b, :, :], T3[0:n, b, :, :], ALU.add)\
                                    .then_inc(residual_ready, 1)
                        sweep(pool, groups, full_groups, last_parts, STORE, step)

                @block.vector
                def _(dve):
                    def add_half(t):
                        n, b = t.rows, t.slot
                        dve.wait_ge(product, t.n + 1)
                        if positive(t.turn):
                            dve.wait_ge(stored[t.slot], t.turn * (16 * (2 if kind == 2 else 1)))
                        ps = psO[0:n, b % sums]
                        if kind == 3:
                            dve.wait_ge(residual_ready, t.n + 1)
                            if positive(t.n - 1):
                                dve.wait_ge(summed, t.n - 1)
                            for q in range(G):
                                ins = nc.vector.scalar_tensor_tensor(A1[0:n, b % 2, q, :], ps[:, q, 0:D], NA[0:n, b, q, 0:1],
                                                                     XT[0:n, b, q, :], ALU.mult, ALU.add)
                            ins.then_inc(part_a, 1)
                            dve.wait_ge(part_a, t.n + 1)
                            for q in range(G):
                                ins = nc.vector.scalar_tensor_tensor(Y[0:n, b, q, :], ps[:, q, D:2 * D], NA[0:n, b, q, 1:2],
                                                                     A1[0:n, b % 2, q, :], ALU.mult, ALU.add)
                        else:
                            pairs = ps[:, :, 0:2 * width]
                            yv = Y[0:n, b, :, :].rearrange("p (k g) c -> p k (g c)", k=2)
                            if kind == 1:
                                ins = nc.vector.tensor_copy(yv, pairs)
                            else:
                                xv = (X if kind == 0 else X2)[0:n, b, :, :].rearrange("p (k g) c -> p k (g c)", k=2)
                                ins = nc.vector.tensor_tensor(yv, xv, pairs, ALU.add)
                        ins.then_inc(summed, 1)

                    def index_step(tile):
                        t = tile(4)
                        if t:
                            n, b = t.rows, t.slot
                            dve.wait_ge(ix["masked"], t.n + 1)
                            if positive(t.n):
                                dve.wait_ge(ix["moved"], t.n)
                            nc.vector.tensor_reduce(rep[0:n, :], early[0:n, b % 2, :, 0:n], AX_X, ALU.max)\
                                .then_inc(ix["counted"], 1)
                            nc.vector.tensor_scalar(off[0:n, :], col[0:n, b, :], -1.0, junk[0:n, :], ALU.mult, ALU.add)\
                                .then_inc(ix["offset"], 1)
                        t_ = tile(2)
                        if t_:
                            n, b = t_.rows, t_.slot
                            dve.wait_ge(index_in[t_.slot], (t_.turn + 1) * 48)
                            if positive(t_.turn):
                                dve.wait_ge(index_stored[t_.slot], t_.turn * 32)
                            if positive(t_.n - (NB - 1)):
                                dve.wait_ge(ix["masked"], t_.n - (NB - 1))
                            nc.vector.tensor_tensor(eq[0:n, b, :, 0:n], row[0:n, b, :, 0:n], repeat(col[0:n, b, :], 2, n),
                                                    ALU.is_equal).then_inc(ix["compared"], 1)
                        if t:
                            n, b = t.rows, t.slot
                            dve.wait_ge(ix["counted"], t.n + 1)
                            dve.wait_ge(ix["offset"], t.n + 1)
                            if positive(t.n):
                                dve.wait_ge(ix["ready"], t.n)
                            nc.vector.tensor_tensor(moved[0:n, :], off[0:n, :], rep[0:n, :], ALU.mult)\
                                .then_inc(ix["moved"], 1)
                            dve.wait_ge(ix["moved"], t.n + 1)
                            nc.vector.tensor_tensor(uniq[0:n, b, :], moved[0:n, :], col[0:n, b, :], ALU.add)\
                                .then_inc(ix["ready"], 1)

                    def step(tile):
                        if kind == 0:
                            index_step(tile)
                        t = tile(STATS)
                        if t:
                            n, b = t.rows, t.slot
                            if kind == 2:
                                dve.wait_ge(residual_ready, t.n + 1)
                            else:
                                dve.wait_ge(loaded[t.slot], (t.turn + 1) * (16 * (loads)))
                            src = X2 if kind == 2 else X
                            norm.statistics(dve, t, [src[0:n, b, q, :] for q in range(G)])
                        tm = tile(MUL)
                        if newton:
                            if t:
                                norm.widen(dve, t)
                                for at in range(5):
                                    norm.newton(dve, t, at)
                            if tm:
                                add_half(tm)
                            if t:
                                for at in range(5, NEWTON + 1):
                                    norm.newton(dve, t, at)
                                norm.newton_shifts(dve, t)
                        else:
                            if tm:
                                add_half(tm)
                            t = tile(STATS + 1)
                            if t:
                                norm.scales(dve, t)
                    sweep(dve, groups, full_groups, last_parts, STORE, step)

        def gather(pool, out_ap, tab, index):
            return pool.indirect_dma_start(out=out_ap, out_offset=None, in_=tab,
                                           in_offset=bass.IndirectOffsetOnAxis(ap=index, axis=0))

        def scatter_add(pool, tab, index, in_ap):
            return pool.indirect_dma_start(out=tab, out_offset=bass.IndirectOffsetOnAxis(ap=index, axis=0),
                                           in_=in_ap, in_offset=None, compute_op=ALU.add)

        SRC, DST = 0, 1

        class EdgePhase:

            def __init__(self, ph, tag, table_in, at, to, table_out, width, ea_cols, lags, gathers=1):
                self.tag, self.table_in, self.at, self.to, self.table_out = tag, table_in, at, to, table_out
                self.width, self.ea_cols, self.gathers, self.row_dmas = width, ea_cols, gathers, gathers
                self.ea_lag, self.eq_lag, self.uq_lag, self.last = lags

                def sb(name, shape, dt=F32):
                    return ph.enter_context(nc.sbuf_tensor(f"{tag}_{name}", shape, dt))
                self.index, self.uniq = sb("index", [P, NB, 2], I32), sb("uniq", [P, NB, 2], I32)
                self.X = sb("X", [P, NB, gathers, D])
                self.EA = sb("EA", [P, NB, ea_cols[1] - ea_cols[0]])
                self.EQ, self.R = sb("EQ", [P, NB, P]), sb("R", [P, NB, width])
                self.index_in, self.ea_in = ring_sems(f"{tag}_index_in"), ring_sems(f"{tag}_ea_in")
                self.eq_in, self.uniq_in = ring_sems(f"{tag}_eq_in"), ring_sems(f"{tag}_uniq_in")
                self.rows_in = ring_sems(f"{tag}_rows_in")
                self.added, self.passed = sem(f"{tag}_added"), sem(f"{tag}_pool_passed")

            def loads(self, sp, tile, index_used, ea_used, eq_used):
                t = tile(0)
                if t:
                    n, b = t.rows, t.slot
                    index_used(sp, t)
                    sp.dma_start(self.index[0:n, b, :], idx2[bass.ds(t.n * P, n), :]).then_inc(self.index_in[b], 16)
                t = tile(self.ea_lag)
                if t:
                    n, b = t.rows, t.slot
                    for read in ea_used:
                        if positive(t.n - (NB - 1)):
                            sp.wait_ge(read, t.n - (NB - 1))
                    sp.dma_start(self.EA[0:n, b, :], ea[bass.ds(t.n * P, n), self.ea_cols[0]:self.ea_cols[1]])\
                      .then_inc(self.ea_in[b], 16)
                t = tile(self.eq_lag)
                if t:
                    n, b = t.rows, t.slot
                    if positive(t.n - (NB - 1)):
                        sp.wait_ge(eq_used, t.n - (NB - 1))
                    sp.dma_start(self.EQ[0:n, b, 0:n], same[bass.ds(t.n * P, n), self.to * P:self.to * P + n])\
                      .then_inc(self.eq_in[b], 16)
                t = tile(self.uq_lag)
                if t:
                    n, b = t.rows, t.slot
                    if positive((t.n - (NB - 1)) * 16):
                        sp.wait_ge(self.added, (t.n - (NB - 1)) * 16)
                    sp.dma_start(self.uniq[0:n, b, :], unique[bass.ds(t.n * P, n), :]).then_inc(self.uniq_in[b], 16)

            def gather_rows(self, pool, t, rows_free):
                n, b = t.rows, t.slot
                pool.wait_ge(self.index_in[t.slot], (t.turn + 1) * 16)
                if positive(t.n - (NB - 1)):
                    pool.wait_ge(rows_free, t.n - (NB - 1))
                pool.sem_inc(self.passed, 1)
                for g in range(self.gathers):
                    a = self.at if self.gathers == 1 else (DST, SRC)[g]
                    gather(pool, self.X[0:n, b, g, :], self.table_in, self.index[0:n, b, a:a + 1])\
                        .then_inc(self.rows_in[b], 16)

            def add_rows(self, pool, t, result, per=1):
                n, b = t.rows, t.slot
                pool.wait_ge(self.uniq_in[t.slot], (t.turn + 1) * 16)
                pool.wait_ge(result, (t.n + 1) * per)
                if positive(t.n * 16):
                    pool.wait_ge(self.added, t.n * 16)
                pool.sem_inc(self.passed, 1)
                scatter_add(pool, self.table_out, self.uniq[0:n, b, self.to:self.to + 1], self.R[0:n, b, :])\
                    .then_inc(self.added, 16)

        def rows_used(e):
            def wait(sp, t):
                if positive(t.turn):
                    sp.wait_ge(e.rows_in[t.slot], t.turn * (16 * (e.row_dmas)))
            return wait

        def layer1_edges():
            with nc.cleanup_on_exit(), ExitStack() as ph:
                tag = "e1"
                GATHER, STATS, ROOT, SCALES, MAP, TURN, MIX, SH, SPREAD, FILTER, FOLD, Z_AT, SUM, Z_OUT, LINEAR, RESULT, ADD = \
                    1, 3, 4, 5, 6, 7, 9, 9, 10, 11, 12, 13, 14, 15, 16, 17, 18

                def sb(name, shape, dt=F32):
                    return ph.enter_context(nc.sbuf_tensor(f"{tag}_{name}", shape, dt))

                def pb(name, shape):
                    return ph.enter_context(nc.psum_tensor(f"{tag}_{name}", shape, F32))
                e = EdgePhase(ph, tag, x1, DST, SRC, p1, 192, (EA3, EAW), (TURN - 2, SUM - 2, ADD - 2, ADD))
                norm = Norm(ph, tag, 1)
                H, XT, VT, hidT = sb("H", [P, NB, D]), sb("XT", [S, NB, 2, P]), sb("VT", [96, NB, P]), sb("hidT", [64, NB, P])
                XS, XV = sb("XS", [P, NB, S]), sb("XV", [P, NB, 5, V])
                n2, root, rn = sb("n2", [P, NB]), sb("root", [P, NB]), sb("rn", [P, NB])
                rhat, sh = sb("rhat", [P, NB, 3]), sb("sh", [P, NB, 5])
                sq, w1x, Wt = sb("sq", [P, 3]), sb("w1x", [P, S]), sb("Wt", [P, NB, 224])
                ca, cb, dp, ds_ = sb("ca", [P, 3, V]), sb("cb", [P, 3, V]), sb("dp", [P, 3, V]), sb("ds", [P, V])
                CR, DT = sb("CR", [P, NB, 3, V]), sb("DT", [P, NB, V])
                Z, ZT = sb("Z", [P, NB, 480]), sb("ZT", [P, NB, 4, P])
                psT, psM, psW, psZ, psO = pb("psT", [P, 2, 512]), pb("psM", [P, 2, 512]), pb("psW", [P, 512]), pb("psZ", [P, 2, 512]), pb("psO", [P, 512])
                q = {m: sem(f"{tag}_{m}") for m in (
                    "turned", "xt_out", "vt_out", "mixed", "hid_out", "xv_out", "filter", "filter_out",
                    "squared", "n2", "root", "rn", "rhat", "sh", "pool_products", "cross", "dot1", "dot", "w1x", "z_ready",
                    "z_turned", "z_out", "linear", "result")}
                block = ph.enter_context(nc.Block())

                @block.sync
                def _(sp):
                    def step(tile):
                        e.loads(sp, tile, rows_used(e), (q["turned"], q["sh"]), q["z_turned"])
                    sweep(sp, tiles, full_tiles, last_edges, ADD, step)

                @block.gpsimd
                def _(pool):
                    def step(tile):
                        t = tile(ADD)
                        if t:
                            e.add_rows(pool, t, q["result"])
                        t = tile(GATHER)
                        if t:
                            e.gather_rows(pool, t, norm.done)
                        t = tile(FILTER)
                        if t:
                            n, b = t.rows, t.slot
                            pool.wait_ge(q["xv_out"], t.n + 1)
                            pool.wait_ge(q["sh"], t.n + 1)
                            if positive(t.n - (NB - 1)):
                                pool.wait_ge(q["z_ready"], t.n - (NB - 1))
                            if positive(t.n):
                                pool.wait_ge(q["dot"], t.n)
                            v = XV[0:n, b, :, :]
                            nc.gpsimd.tensor_tensor(ca[0:n], v[:, 1:4, :], repeat(sh[0:n, b, 2:5], 2, V), ALU.mult)
                            nc.gpsimd.tensor_tensor(cb[0:n], v[:, 2:5, :], repeat(sh[0:n, b, 1:4], 2, V), ALU.mult)
                            nc.gpsimd.tensor_tensor(dp[0:n], v[:, 0:3, :], repeat(rhat[0:n, b, :], 2, V), ALU.mult)\
                                .then_inc(q["pool_products"], 1)
                            pool.wait_ge(q["pool_products"], t.n + 1)
                            nc.gpsimd.tensor_tensor(CR[0:n, b], ca[0:n], cb[0:n], ALU.subtract).then_inc(q["cross"], 1)
                            nc.gpsimd.tensor_tensor(ds_[0:n], dp[0:n, 0], dp[0:n, 1], ALU.add).then_inc(q["dot1"], 1)
                            pool.wait_ge(q["dot1"], t.n + 1)
                            nc.gpsimd.tensor_tensor(DT[0:n, b], ds_[0:n], dp[0:n, 2], ALU.add).then_inc(q["dot"], 1)
                    sweep(pool, tiles, full_tiles, last_edges, ADD, step)
                    pool.wait_ge(e.added, 16 * tiles)

                @block.scalar
                def _(act):
                    def step(tile):
                        t = tile(RESULT)
                        if t:
                            n, b = t.rows, t.slot
                            act.wait_ge(q["linear"], t.n + 1)
                            if positive((t.n - (NB - 1)) * 16):
                                act.wait_ge(e.added, (t.n - (NB - 1)) * 16)
                            nc.scalar.copy(e.R[0:n, b, :], psO[0:n, 0:192]).then_inc(q["result"], 1)
                        t = tile(FOLD)
                        if t:
                            n, b = t.rows, t.slot
                            act.wait_ge(q["filter"], t.n + 1)
                            if positive(t.n - (NB - 1)):
                                act.wait_ge(q["z_ready"], t.n - (NB - 1))
                            nc.scalar.copy(Wt[0:n, b, :], psW[0:n, 0:224]).then_inc(q["filter_out"], 1)
                        t = tile(Z_OUT)
                        if t:
                            n, b = t.rows, t.slot
                            act.wait_ge(q["z_turned"], t.n + 1)
                            if positive(t.n - (NB - 1)):
                                act.wait_ge(q["linear"], t.n - (NB - 1))
                            nc.scalar.copy(ZT[0:P, b, 1:4, 0:n], psZ[:, b % 2, P:512].rearrange("p (c q) -> p c q", c=3)[:, :, 0:n])
                            nc.scalar.copy(ZT[0:96, b, 0, 0:n], psZ[0:96, b % 2, 0:n]).then_inc(q["z_out"], 1)
                        t = tile(SPREAD)
                        if t:
                            n, b = t.rows, t.slot
                            act.wait_ge(q["mixed"], t.n + 1)
                            if positive(t.n - (NB - 1)):
                                act.wait_ge(q["filter"], t.n - (NB - 1))
                            nc.scalar.activation(hidT[:, b, 0:n], psM[0:64, b % 2, D:D + n], ACT.Relu).then_inc(q["hid_out"], 1)
                            if positive(t.n - (NB - 1)):
                                act.wait_ge(q["z_ready"], t.n - (NB - 1))
                            nc.scalar.copy(XS[0:n, b, :], psM[0:n, b % 2, 0:S])
                            v = psM[0:n, b % 2, S:D].rearrange("p (i u) -> p i u", i=3)
                            nc.scalar.copy(XV[0:n, b, 0:3, :], v)
                            nc.scalar.copy(XV[0:n, b, 3:5, :], v[:, 0:2, :]).then_inc(q["xv_out"], 1)
                        t = tile(TURN + 1)
                        if t:
                            n, b = t.rows, t.slot
                            act.wait_ge(q["n2"], t.n + 1)
                            nc.scalar.activation(root[0:n, b:b + 1], n2[0:n, b:b + 1], ACT.Sqrt).then_inc(q["root"], 1)
                        t = tile(MAP)
                        if t:
                            n, b = t.rows, t.slot
                            act.wait_ge(norm.ready, t.n + 1)
                            if positive(t.n - (NB - 1)):
                                act.wait_ge(q["turned"], t.n - (NB - 1))
                            norm.map(t, H[0:n, b, :], e.X[0:n, b, 0, :], 0).then_inc(norm.done, 1)
                        t = tile(ROOT)
                        if t:
                            norm.root(act, t)
                    sweep(act, tiles, full_tiles, last_edges, ADD, step)

                @block.tensor
                def _(pe):
                    def step(tile):
                        t = tile(SUM)
                        if t:
                            n, b = t.rows, t.slot
                            pe.wait_ge(q["z_ready"], t.n + 1)
                            pe.wait_ge(e.eq_in[t.slot], (t.turn + 1) * 16)
                            if positive(t.n - 1):
                                pe.wait_ge(q["z_out"], t.n - 1)
                            nc.tensor.matmul(psZ[0:96, b % 2, 0:n], Z[0:n, b, 0:96], e.EQ[0:n, b, 0:n], start=True, stop=True)
                            for i in range(3):
                                mm = nc.tensor.matmul(psZ[:, b % 2, P * (i + 1):P * (i + 1) + n], Z[0:n, b, 96 + P * i:96 + P * (i + 1)],
                                                      e.EQ[0:n, b, 0:n], start=True, stop=True)
                            mm.then_inc(q["z_turned"], 1)
                        t = tile(TURN)
                        if t:
                            n, b = t.rows, t.slot
                            pe.wait_ge(norm.done, t.n + 1)
                            pe.wait_ge(e.ea_in[t.slot], (t.turn + 1) * 16)
                            if positive(t.n - 1):
                                pe.wait_ge(q["xt_out"], t.n - 1)
                            if positive(t.n - 1):
                                pe.wait_ge(q["vt_out"], t.n - 1)
                            nc.tensor.transpose(psT[0:96, b % 2, 2 * P:2 * P + n], H[0:n, b, S:D], ident[0:n, 0:n])
                            nc.tensor.transpose(psT[0:S, b % 2, 0:n], H[0:n, b, 0:S], ident[0:n, 0:n])
                            nc.tensor.transpose(psT[0:S, b % 2, P:P + n], e.EA[0:n, b, 3:67], ident[0:n, 0:n])\
                                .then_inc(q["turned"], 1)
                        t = tile(MIX)
                        if t:
                            n, b = t.rows, t.slot
                            pe.wait_ge(q["xt_out"], t.n + 1)
                            pe.wait_ge(q["vt_out"], t.n + 1)
                            if positive(t.n - 1):
                                pe.wait_ge(q["xv_out"], t.n - 1)
                            nc.tensor.matmul(psM[0:n, b % 2, 0:S], XT[0:S, b, 0, 0:n], w("nl_s"), start=True, stop=True)
                            nc.tensor.matmul(psM[0:n, b % 2, S:D], VT[0:96, b, 0:n], w("nl_v"), start=True, stop=True)
                            nc.tensor.matmul(psM[0:64, b % 2, D:D + n], w("fc1"), XT[0:64, b, 1, 0:n], start=True, stop=True)\
                                .then_inc(q["mixed"], 1)
                        t = tile(FILTER)
                        if t:
                            n, b = t.rows, t.slot
                            pe.wait_ge(q["hid_out"], t.n + 1)
                            if positive(t.n):
                                pe.wait_ge(q["filter_out"], t.n)
                            nc.tensor.matmul(psW[0:n, 0:224], hidT[:, b, 0:n], w("fc2"), start=True, stop=True)\
                                .then_inc(q["filter"], 1)
                        t = tile(LINEAR)
                        if t:
                            n, b = t.rows, t.slot
                            pe.wait_ge(q["z_out"], t.n + 1)
                            if positive(t.n):
                                pe.wait_ge(q["result"], t.n)
                            nc.tensor.matmul(psO[0:n, 0:96], ZT[0:96, b, 0, 0:n], w("out_s"), start=True, stop=True)
                            for i in range(3):
                                mm = nc.tensor.matmul(psO[0:n, 96 + i:192:3], ZT[:, b, 1 + i, 0:n], w("out_v"), start=True, stop=True)
                            mm.then_inc(q["linear"], 1)
                    sweep(pe, tiles, full_tiles, last_edges, ADD, step)

                @block.vector
                def _(dve):
                    def step(tile):
                        t = tile(Z_AT)
                        if t:
                            n, b = t.rows, t.slot
                            dve.wait_ge(q["xv_out"], t.n + 1)
                            dve.wait_ge(q["filter_out"], t.n + 1)
                            if positive(t.n - (NB - 1)):
                                dve.wait_ge(q["z_turned"], t.n - (NB - 1))
                            z, wt = Z[0:n, b, :], Wt[0:n, b, :]
                            zv = z[:, 96:480].rearrange("p (i c) -> p i c", i=3)
                            if positive(t.n):
                                dve.wait_ge(q["z_ready"], t.n)
                            nc.vector.tensor_tensor(w1x[0:n], wt[:, 64:128], XS[0:n, b, :], ALU.mult).then_inc(q["w1x"], 1)
                            nc.vector.tensor_tensor(z[:, 0:S], wt[:, 0:64], XS[0:n, b, :], ALU.mult)
                            nc.vector.tensor_tensor(zv[:, :, S:96], XV[0:n, b, 0:3, :], repeat(wt[:, 128:160], 1, 3), ALU.mult)
                            dve.wait_ge(q["w1x"], t.n + 1)
                            dve.wait_ge(q["sh"], t.n + 1)
                            nc.vector.tensor_tensor(zv[:, :, 0:S], repeat(w1x[0:n], 1, 3), repeat(sh[0:n, b, 0:3], 2, S), ALU.mult)
                            dve.wait_ge(q["cross"], t.n + 1)
                            nc.vector.tensor_tensor(zv[:, :, 96:P], CR[0:n, b], repeat(wt[:, 192:224], 1, 3), ALU.mult)
                            dve.wait_ge(q["dot"], t.n + 1)
                            nc.vector.tensor_tensor(z[:, S:96], DT[0:n, b], wt[:, 160:192], ALU.mult).then_inc(q["z_ready"], 1)
                        t = tile(TURN + 1)
                        if t:
                            n, b = t.rows, t.slot
                            dve.wait_ge(q["turned"], t.n + 1)
                            if positive(t.n - (NB - 1)):
                                dve.wait_ge(q["mixed"], t.n - (NB - 1))
                            nc.vector.tensor_copy(XT[0:S, b, :, 0:n], psT[0:S, b % 2, 0:2 * P].rearrange("p (c q) -> p c q", c=2)[:, :, 0:n])\
                                .then_inc(q["xt_out"], 1)
                            nc.vector.tensor_copy(VT[:, b, 0:n], psT[0:96, b % 2, 2 * P:2 * P + n]).then_inc(q["vt_out"], 1)
                        tr, ts = tile(SH), tile(TURN)
                        if tr:
                            n, b = tr.rows, tr.slot
                            dve.wait_ge(q["root"], tr.n + 1)
                            nc.vector.reciprocal(rn[0:n, b:b + 1], root[0:n, b:b + 1]).then_inc(q["rn"], 1)
                        if ts:
                            n, b = ts.rows, ts.slot
                            dve.wait_ge(e.ea_in[ts.slot], (ts.turn + 1) * 16)
                            if positive(ts.n):
                                dve.wait_ge(q["n2"], ts.n)
                            if positive(ts.n - (NB - 1)):
                                dve.wait_ge(q["root"], ts.n - (NB - 1))
                            nc.vector.tensor_tensor(sq[0:n], e.EA[0:n, b, 0:3], e.EA[0:n, b, 0:3], ALU.mult).then_inc(q["squared"], 1)
                        if tr:
                            n, b = tr.rows, tr.slot
                            a = e.EA[0:n, b, 0:3]
                            dve.wait_ge(q["rn"], tr.n + 1)
                            if positive(tr.n - (NB - 1)):
                                dve.wait_ge(q["dot"], tr.n - (NB - 1))
                            nc.vector.tensor_scalar(rhat[0:n, b, :], a, rn[0:n, b:b + 1], None, ALU.mult).then_inc(q["rhat"], 1)
                            nc.vector.tensor_scalar(sh[0:n, b, 0:3], a, rn[0:n, b:b + 1], 3.0 ** 0.5, ALU.mult, ALU.mult)
                            nc.vector.tensor_scalar(sh[0:n, b, 3:5], a[:, 0:2], rn[0:n, b:b + 1], 3.0 ** 0.5, ALU.mult, ALU.mult)\
                                .then_inc(q["sh"], 1)
                        if ts:
                            n, b = ts.rows, ts.slot
                            dve.wait_ge(q["squared"], ts.n + 1)
                            nc.vector.tensor_reduce(n2[0:n, b:b + 1], sq[0:n], AX_X, ALU.add).then_inc(q["n2"], 1)
                        t = tile(STATS)
                        if t:
                            n, b = t.rows, t.slot
                            dve.wait_ge(e.rows_in[t.slot], (t.turn + 1) * 16)
                            norm.statistics(dve, t, [e.X[0:n, b, 0, :]])
                        t = tile(SCALES)
                        if t:
                            norm.scales(dve, t)
                    sweep(dve, tiles, full_tiles, last_edges, ADD, step)

        def layer2_edges():
            with nc.cleanup_on_exit(), ExitStack() as ph:
                tag = "e2"
                GATHER, Z_AT, TURN, Z_OUT, MESSAGE, GATE, M_AT, SUM, M_OUT, LINEAR, RESULT, ADD = 1, 3, 4, 5, 6, 7, 8, 9, 10, 11, 12, 13

                def sb(name, shape, dt=F32):
                    return ph.enter_context(nc.sbuf_tensor(f"{tag}_{name}", shape, dt))

                def pb(name, shape):
                    return ph.enter_context(nc.psum_tensor(f"{tag}_{name}", shape, F32))
                e = EdgePhase(ph, tag, h2, SRC, DST, x3, D, (EA4, EA3), (1, SUM - 2, ADD - 2, ADD))
                VE, VD = sb("VE", [P, 3, V]), sb("VD", [P, V])
                Z, ZT, RT = sb("Z", [P, NB, 4, 96]), sb("ZT", [96, NB, 4, P]), sb("RT", [17, NB, P])
                gate, M = sb("gate", [P, NB, D]), sb("M", [P, NB, D])
                MsT, MvT = sb("MsT", [S, NB, P]), sb("MvT", [96, NB, P])
                psZ, psR, psM = pb("psZ", [P, 2, 512]), pb("psR", [P, 512]), pb("psM", [P, 2, 512])
                psA, psO = pb("psA", [P, 2, 512]), pb("psO", [P, 512])
                q = {m: sem(f"{tag}_{m}") for m in (
                    "ones", "ve", "ve1", "z_pool", "z_ready", "turned", "rad_turned", "rt_out", "zt_out", "message",
                    "gate", "m_ready", "m_turned", "ms_out", "mv_out", "linear", "result")}
                block = ph.enter_context(nc.Block())

                @block.sync
                def _(sp):
                    def step(tile):
                        e.loads(sp, tile, rows_used(e), (q["turned"],), q["m_turned"])
                    sweep(sp, tiles, full_tiles, last_edges, ADD, step)

                @block.gpsimd
                def _(pool):
                    nc.gpsimd.memset(RT[:, :, :], 1.0).then_inc(q["ones"], 1)

                    def step(tile):
                        t = tile(ADD)
                        if t:
                            e.add_rows(pool, t, q["result"])
                        t = tile(GATHER)
                        if t:
                            e.gather_rows(pool, t, q["z_ready"])
                        t = tile(Z_AT)
                        if t:
                            n, b = t.rows, t.slot
                            pool.wait_ge(e.rows_in[t.slot], (t.turn + 1) * 16)
                            pool.wait_ge(e.ea_in[t.slot], (t.turn + 1) * 16)
                            if positive(t.n - (NB - 1)):
                                pool.wait_ge(q["turned"], t.n - (NB - 1))
                            if positive(t.n):
                                pool.wait_ge(q["z_pool"], t.n)
                            xv = e.X[0:n, b, 0, S:D].rearrange("p (u i) -> p i u", i=3)
                            ev = e.EA[0:n, b, 1:4]
                            nc.gpsimd.tensor_tensor(VE[0:n], xv, repeat(ev, 2, V), ALU.mult).then_inc(q["ve"], 1)
                            pool.wait_ge(q["ve"], t.n + 1)
                            nc.gpsimd.tensor_tensor(VD[0:n], VE[0:n, 0], VE[0:n, 1], ALU.add).then_inc(q["ve1"], 1)
                            pool.wait_ge(q["ve1"], t.n + 1)
                            nc.gpsimd.tensor_tensor(Z[0:n, b, 0, S:96], VD[0:n], VE[0:n, 2], ALU.add).then_inc(q["z_pool"], 1)
                    sweep(pool, tiles, full_tiles, last_edges, ADD, step)
                    pool.wait_ge(e.added, 16 * tiles)

                @block.vector
                def _(dve):
                    def step(tile):
                        t = tile(M_AT)
                        if t:
                            n, b = t.rows, t.slot
                            dve.wait_ge(q["message"], t.n + 1)
                            dve.wait_ge(q["gate"], t.n + 1)
                            if positive(t.n - (NB - 1)):
                                dve.wait_ge(q["m_turned"], t.n - (NB - 1))
                            nc.vector.tensor_tensor(M[0:n, b, :], psM[0:n, b % 2, 0:D], gate[0:n, b, :], ALU.mult)\
                                .then_inc(q["m_ready"], 1)
                        t = tile(M_OUT)
                        if t:
                            n, b = t.rows, t.slot
                            dve.wait_ge(q["m_turned"], t.n + 1)
                            if positive(t.n - (NB - 1)):
                                dve.wait_ge(q["linear"], t.n - (NB - 1))
                            nc.vector.tensor_copy(MsT[:, b, 0:n], psA[0:S, b % 2, 0:n]).then_inc(q["ms_out"], 1)
                            nc.vector.tensor_copy(MvT[:, b, 0:n], psA[0:96, b % 2, P:P + n]).then_inc(q["mv_out"], 1)
                        t = tile(Z_AT)
                        if t:
                            n, b = t.rows, t.slot
                            dve.wait_ge(e.rows_in[t.slot], (t.turn + 1) * 16)
                            dve.wait_ge(e.ea_in[t.slot], (t.turn + 1) * 16)
                            if positive(t.n - (NB - 1)):
                                dve.wait_ge(q["turned"], t.n - (NB - 1))
                            xs = e.X[0:n, b, 0, 0:S]
                            xv = e.X[0:n, b, 0, S:D].rearrange("p (u i) -> p i u", i=3)
                            es, ev = e.EA[0:n, b, 0:1], e.EA[0:n, b, 1:4]
                            nc.vector.tensor_scalar(Z[0:n, b, 0, 0:S], xs, es, None, ALU.mult)
                            nc.vector.tensor_scalar(Z[0:n, b, 1:4, S:96], xv, es, None, ALU.mult)
                            nc.vector.tensor_tensor(Z[0:n, b, 1:4, 0:S], repeat(xs, 1, 3), repeat(ev, 2, S), ALU.mult)\
                                .then_inc(q["z_ready"], 1)
                    sweep(dve, tiles, full_tiles, last_edges, ADD, step)

                @block.scalar
                def _(act):
                    act.wait_ge(q["ones"], 1)

                    def step(tile):
                        t = tile(RESULT)
                        if t:
                            n, b = t.rows, t.slot
                            act.wait_ge(q["linear"], t.n + 1)
                            if positive((t.n - (NB - 1)) * 16):
                                act.wait_ge(e.added, (t.n - (NB - 1)) * 16)
                            nc.scalar.copy(e.R[0:n, b, :], psO[0:n, 0:D]).then_inc(q["result"], 1)
                        t = tile(Z_OUT)
                        if t:
                            n, b = t.rows, t.slot
                            act.wait_ge(q["turned"], t.n + 1)
                            if positive(t.n - (NB - 1)):
                                act.wait_ge(q["message"], t.n - (NB - 1))
                            nc.scalar.copy(RT[0:16, b, 0:n], psR[0:16, 0:n]).then_inc(q["rt_out"], 1)
                            nc.scalar.copy(ZT[:, b, :, 0:n], psZ[0:96, b % 2, :].rearrange("p (c q) -> p c q", c=4)[:, :, 0:n])\
                                .then_inc(q["zt_out"], 1)
                        t = tile(GATE)
                        if t:
                            n, b = t.rows, t.slot
                            act.wait_ge(q["message"], t.n + 1)
                            if positive(t.n - (NB - 1)):
                                act.wait_ge(q["m_ready"], t.n - (NB - 1))
                            nc.scalar.activation(gate[0:n, b, :], psM[0:n, b % 2, D:2 * D], ACT.Sigmoid).then_inc(q["gate"], 1)
                    sweep(act, tiles, full_tiles, last_edges, ADD, step)

                @block.tensor
                def _(pe):
                    def step(tile):
                        t = tile(SUM)
                        if t:
                            n, b = t.rows, t.slot
                            pe.wait_ge(q["m_ready"], t.n + 1)
                            pe.wait_ge(e.eq_in[t.slot], (t.turn + 1) * 16)
                            if positive(t.n - 1):
                                pe.wait_ge(q["ms_out"], t.n - 1)
                            if positive(t.n - 1):
                                pe.wait_ge(q["mv_out"], t.n - 1)
                            nc.tensor.matmul(psA[0:S, b % 2, 0:n], M[0:n, b, 0:S], e.EQ[0:n, b, 0:n], start=True, stop=True)
                            nc.tensor.matmul(psA[0:96, b % 2, P:P + n], M[0:n, b, S:D], e.EQ[0:n, b, 0:n], start=True, stop=True)\
                                .then_inc(q["m_turned"], 1)
                        t = tile(TURN)
                        if t:
                            n, b = t.rows, t.slot
                            pe.wait_ge(q["z_ready"], t.n + 1)
                            pe.wait_ge(q["z_pool"], t.n + 1)
                            if positive(t.n - 1):
                                pe.wait_ge(q["zt_out"], t.n - 1)
                            if positive(t.n):
                                pe.wait_ge(q["rt_out"], t.n)
                            nc.tensor.transpose(psR[0:16, 0:n], e.EA[0:n, b, 4:20], ident[0:n, 0:n])
                            for c in range(4):
                                tr = nc.tensor.transpose(psZ[0:96, b % 2, P * c:P * c + n], Z[0:n, b, c, :], ident[0:n, 0:n])
                            tr.then_inc(q["turned"], 1)
                        t = tile(MESSAGE)
                        if t:
                            n, b = t.rows, t.slot
                            pe.wait_ge(q["rt_out"], t.n + 1)
                            pe.wait_ge(q["zt_out"], t.n + 1)
                            if positive(t.n - 1):
                                pe.wait_ge(q["m_ready"], t.n - 1)
                            nc.tensor.matmul(psM[0:n, b % 2, D:2 * D], RT[:, b, 0:n], w("rad"), start=True, stop=True)
                            nc.tensor.matmul(psM[0:n, b % 2, 0:S], ZT[:, b, 0, 0:n], w("l2_s"), start=True, stop=True)
                            for i in range(3):
                                mm = nc.tensor.matmul(psM[0:n, b % 2, S + i:D:3], ZT[:, b, 1 + i, 0:n], w("l2_v"), start=True, stop=True)
                            mm.then_inc(q["message"], 1)
                        t = tile(LINEAR)
                        if t:
                            n, b = t.rows, t.slot
                            pe.wait_ge(q["ms_out"], t.n + 1)
                            pe.wait_ge(q["mv_out"], t.n + 1)
                            if positive(t.n):
                                pe.wait_ge(q["result"], t.n)
                            nc.tensor.matmul(psO[0:n, 0:S], MsT[:, b, 0:n], w("l2l_s"), start=True, stop=True)
                            nc.tensor.matmul(psO[0:n, S:D], MvT[:, b, 0:n], w("l2l_v"), start=True, stop=True).then_inc(q["linear"], 1)
                    sweep(pe, tiles, full_tiles, last_edges, ADD, step)

        def layer3_edges():
            with nc.cleanup_on_exit(), ExitStack() as ph:
                tag = "e3"
                GATHER, STATS, MAP, TURN, T_OUT, MIX, MIX_OUT, HID_OUT, FILTER, F_OUT, Z_AT, SUM, Z_OUT, LINEAR, RESULT, ADD = \
                    1, 3, 4, 5, 6, 7, 8, 9, 10, 11, 12, 13, 14, 15, 16, 17

                def sb(name, shape, dt=F32):
                    return ph.enter_context(nc.sbuf_tensor(f"{tag}_{name}", shape, dt))

                def pb(name, shape):
                    return ph.enter_context(nc.psum_tensor(f"{tag}_{name}", shape, F32))
                e = EdgePhase(ph, tag, x3, SRC, DST, t3, D, (EA4, EA16), (FILTER - 2, SUM - 2, ADD - 5, ADD))
                norm = Norm(ph, tag, 1)
                NA, ND, AM = sb("NA", [P, NB, 3]), sb("ND", [P, NB, 3]), sb("AM", [P, NB, 2])
                EL = sb("EL", [P, NB, 10])
                na_in, nd_in, el_in = ring_sems(f"{tag}_na_in"), ring_sems(f"{tag}_nd_in"), ring_sems(f"{tag}_el_in")
                H, HT, VT, LT = sb("H", [P, NB, D]), sb("HT", [S, NB, P]), sb("VT", [96, NB, P]), sb("LT", [10, NB, P])
                sg, hidT, A1, XM, Wt = sb("sg", [100, 2, P]), sb("hidT", [100, NB, P]), sb("A1", [P, D]), sb("XM", [P, NB, D]), sb("Wt", [P, NB, 192])
                w1x, VE, VD, DT, W2 = sb("w1x", [P, S]), sb("VE", [P, 3, V]), sb("VD", [P, V]), sb("DT", [P, NB, V]), sb("W2", [P, V])
                Z, ZT, TA = sb("Z", [P, NB, 4, 96]), sb("ZT", [96, NB, 4, P]), sb("TA", [P, D])
                psT, psL, psM, psW = pb("psT", [P, 512]), pb("psL", [P, 2, 512]), pb("psM", [P, 512]), pb("psW", [P, 512])
                psZ, psO = pb("psZ", [P, 2, 512]), pb("psO", [P, 512])
                q = {m: sem(f"{tag}_{m}") for m in (
                    "turned", "t_out", "hidden", "sig", "hid_out", "mixed", "part_a", "mix_out", "filter",
                    "filter_out", "ve", "ve1", "dot", "w1x", "w2e", "z_ready", "z_turned", "z_out", "linear", "am", "part_r", "result")}
                block = ph.enter_context(nc.Block())

                @block.sync
                def _(sp):
                    def index_used(sp, t):
                        if positive(t.turn):
                            sp.wait_ge(e.rows_in[t.slot], t.turn * 16)
                        if positive(t.turn):
                            sp.wait_ge(na_in[t.slot], t.turn * 16)

                    def step(tile):
                        e.loads(sp, tile, index_used, (q["z_ready"], q["dot"]), q["z_turned"])
                        t = tile(TURN - 2)
                        if t:
                            n, b = t.rows, t.slot
                            if positive(t.n - (NB - 1)):
                                sp.wait_ge(q["turned"], t.n - (NB - 1))
                            sp.dma_start(EL[0:n, b, :], ea[bass.ds(t.n * P, n), EA10:EA4]).then_inc(el_in[b], 16)
                    sweep(sp, tiles, full_tiles, last_edges, ADD, step)

                @block.gpsimd
                def _(pool):
                    def step(tile):
                        t = tile(ADD)
                        if t:
                            e.add_rows(pool, t, q["result"])
                        t = tile(GATHER)
                        if t:
                            e.gather_rows(pool, t, norm.done)
                        t = tile(STATS)
                        if t:
                            n, b = t.rows, t.slot
                            if positive(t.n - (NB - 1)):
                                pool.wait_ge(q["mix_out"], t.n - (NB - 1))
                            pool.sem_inc(e.passed, 1)
                            gather(pool, NA[0:n, b, :], nattr, e.index[0:n, b, SRC:SRC + 1]).then_inc(na_in[b], 16)
                        t = tile(Z_OUT)
                        if t:
                            n, b = t.rows, t.slot
                            pool.wait_ge(e.uniq_in[t.slot], (t.turn + 1) * 16)
                            if positive(t.n - (NB - 1)):
                                pool.wait_ge(q["am"], t.n - (NB - 1))
                            pool.sem_inc(e.passed, 1)
                            gather(pool, ND[0:n, b, :], nattr, e.uniq[0:n, b, DST:DST + 1]).then_inc(nd_in[b], 16)
                        t = tile(FILTER)
                        if t:
                            n, b = t.rows, t.slot
                            pool.wait_ge(e.ea_in[t.slot], (t.turn + 1) * 16)
                            pool.wait_ge(q["mix_out"], t.n + 1)
                            if positive(t.n - (NB - 1)):
                                pool.wait_ge(q["z_ready"], t.n - (NB - 1))
                            if positive(t.n):
                                pool.wait_ge(q["dot"], t.n)
                            xv = XM[0:n, b, S:D].rearrange("p (i u) -> p i u", i=3)
                            nc.gpsimd.tensor_tensor(VE[0:n], xv, repeat(e.EA[0:n, b, 1:4], 2, V), ALU.mult).then_inc(q["ve"], 1)
                            pool.wait_ge(q["ve"], t.n + 1)
                            nc.gpsimd.tensor_tensor(VD[0:n], VE[0:n, 0], VE[0:n, 1], ALU.add).then_inc(q["ve1"], 1)
                            pool.wait_ge(q["ve1"], t.n + 1)
                            nc.gpsimd.tensor_tensor(DT[0:n, b], VD[0:n], VE[0:n, 2], ALU.add).then_inc(q["dot"], 1)
                    sweep(pool, tiles, full_tiles, last_edges, ADD, step)
                    pool.wait_ge(e.added, 16 * tiles)

                @block.vector
                def _(dve):
                    def step(tile):
                        t = tile(RESULT)
                        if t:
                            n, b = t.rows, t.slot
                            dve.wait_ge(nd_in[t.slot], (t.turn + 1) * 16)
                            if positive(t.n - (NB - 1)):
                                dve.wait_ge(q["result"], t.n - (NB - 1))
                            nc.vector.tensor_scalar(AM[0:n, b, :], ND[0:n, b, 0:2], ND[0:n, b, 2:3], None, ALU.mult)\
                                .then_inc(q["am"], 1)
                        t = tile(MIX_OUT)
                        if t:
                            n, b = t.rows, t.slot
                            dve.wait_ge(na_in[t.slot], (t.turn + 1) * 16)
                            dve.wait_ge(q["mixed"], t.n + 1)
                            if positive(t.n):
                                dve.wait_ge(q["mix_out"], t.n)
                            nc.vector.tensor_scalar(A1[0:n], psM[0:n, 0:D], NA[0:n, b, 0:1], None, ALU.mult)\
                                .then_inc(q["part_a"], 1)
                            dve.wait_ge(q["part_a"], t.n + 1)
                            if positive(t.n - (NB - 1)):
                                dve.wait_ge(q["z_ready"], t.n - (NB - 1))
                            if positive(t.n - (NB - 1)):
                                dve.wait_ge(q["dot"], t.n - (NB - 1))
                            nc.vector.scalar_tensor_tensor(XM[0:n, b, :], psM[0:n, D:2 * D], NA[0:n, b, 1:2], A1[0:n],
                                                           ALU.mult, ALU.add).then_inc(q["mix_out"], 1)
                        t = tile(HID_OUT)
                        if t:
                            n, b = t.rows, t.slot
                            dve.wait_ge(q["sig"], t.n + 1)
                            if positive(t.n - (NB - 1)):
                                dve.wait_ge(q["filter"], t.n - (NB - 1))
                            nc.vector.tensor_tensor(hidT[:, b, 0:n], psL[0:100, b % 2, 0:n], sg[:, b % 2, 0:n], ALU.mult).then_inc(q["hid_out"], 1)
                        t = tile(Z_AT)
                        if t:
                            n, b = t.rows, t.slot
                            dve.wait_ge(e.ea_in[t.slot], (t.turn + 1) * 16)
                            dve.wait_ge(q["filter_out"], t.n + 1)
                            dve.wait_ge(q["mix_out"], t.n + 1)
                            if positive(t.n - (NB - 1)):
                                dve.wait_ge(q["z_turned"], t.n - (NB - 1))
                            z, wt, xs = Z[0:n, b, :, :], Wt[0:n, b, :], XM[0:n, b, 0:S]
                            xv = XM[0:n, b, S:D].rearrange("p (i u) -> p i u", i=3)
                            es, ev = e.EA[0:n, b, 0:1], e.EA[0:n, b, 1:4]
                            if positive(t.n):
                                dve.wait_ge(q["z_ready"], t.n)
                            nc.vector.tensor_tensor(w1x[0:n], wt[:, 64:128], xs, ALU.mult).then_inc(q["w1x"], 1)
                            nc.vector.tensor_scalar(W2[0:n], wt[:, 128:160], es, None, ALU.mult).then_inc(q["w2e"], 1)
                            nc.vector.scalar_tensor_tensor(z[:, 0, 0:S], wt[:, 0:64], es, xs, ALU.mult, ALU.mult)
                            dve.wait_ge(q["w1x"], t.n + 1)
                            nc.vector.tensor_tensor(z[:, 1:4, 0:S], repeat(w1x[0:n], 1, 3), repeat(ev, 2, S), ALU.mult)
                            dve.wait_ge(q["w2e"], t.n + 1)
                            nc.vector.tensor_tensor(z[:, 1:4, S:96], xv, repeat(W2[0:n], 1, 3), ALU.mult)
                            dve.wait_ge(q["dot"], t.n + 1)
                            nc.vector.tensor_tensor(z[:, 0, S:96], DT[0:n, b], wt[:, 160:192], ALU.mult).then_inc(q["z_ready"], 1)
                        t = tile(RESULT)
                        if t:
                            n, b = t.rows, t.slot
                            dve.wait_ge(q["linear"], t.n + 1)
                            dve.wait_ge(q["am"], t.n + 1)
                            if positive((t.n - (NB - 1)) * 16):
                                dve.wait_ge(e.added, (t.n - (NB - 1)) * 16)
                            if positive(t.n):
                                dve.wait_ge(q["result"], t.n)
                            nc.vector.tensor_scalar(TA[0:n], psO[0:n, 0:D], AM[0:n, b, 0:1], None, ALU.mult).then_inc(q["part_r"], 1)
                            dve.wait_ge(q["part_r"], t.n + 1)
                            nc.vector.scalar_tensor_tensor(e.R[0:n, b, :], psO[0:n, D:2 * D], AM[0:n, b, 1:2], TA[0:n],
                                                           ALU.mult, ALU.add).then_inc(q["result"], 1)
                        t = tile(STATS)
                        if t:
                            n, b = t.rows, t.slot
                            dve.wait_ge(e.rows_in[t.slot], (t.turn + 1) * 16)
                            norm.on_vector(dve, t, [e.X[0:n, b, 0, :]])
                    sweep(dve, tiles, full_tiles, last_edges, ADD, step)

                @block.scalar
                def _(act):
                    def step(tile):
                        t = tile(T_OUT)
                        if t:
                            n, b = t.rows, t.slot
                            act.wait_ge(q["turned"], t.n + 1)
                            if positive(t.n - (NB - 1)):
                                act.wait_ge(q["mixed"], t.n - (NB - 1))
                            nc.scalar.copy(VT[:, b, 0:n], psT[0:96, P:P + n])
                            nc.scalar.copy(HT[:, b, 0:n], psT[0:S, 0:n])
                            nc.scalar.copy(LT[:, b, 0:n], psT[0:10, 2 * P:2 * P + n]).then_inc(q["t_out"], 1)
                        t = tile(F_OUT)
                        if t:
                            n, b = t.rows, t.slot
                            act.wait_ge(q["filter"], t.n + 1)
                            if positive(t.n - (NB - 1)):
                                act.wait_ge(q["z_ready"], t.n - (NB - 1))
                            nc.scalar.copy(Wt[0:n, b, :], psW[0:n, 0:192]).then_inc(q["filter_out"], 1)
                        t = tile(Z_OUT)
                        if t:
                            n, b = t.rows, t.slot
                            act.wait_ge(q["z_turned"], t.n + 1)
                            if positive(t.n - (NB - 1)):
                                act.wait_ge(q["linear"], t.n - (NB - 1))
                            nc.scalar.copy(ZT[:, b, :, 0:n], psZ[0:96, b % 2, :].rearrange("p (c q) -> p c q", c=4)[:, :, 0:n])\
                                .then_inc(q["z_out"], 1)
                        t = tile(MIX_OUT)
                        if t:
                            n, b = t.rows, t.slot
                            act.wait_ge(q["mixed"], t.n + 1)
                            if positive(t.n - 1):
                                act.wait_ge(q["hid_out"], t.n - 1)
                            nc.scalar.activation(sg[:, b % 2, 0:n], psL[0:100, b % 2, 0:n], ACT.Sigmoid).then_inc(q["sig"], 1)
                        t = tile(MAP)
                        if t:
                            n, b = t.rows, t.slot
                            act.wait_ge(norm.ready, t.n + 1)
                            if positive(t.n - (NB - 1)):
                                act.wait_ge(q["turned"], t.n - (NB - 1))
                            norm.map(t, H[0:n, b, :], e.X[0:n, b, 0, :], 0).then_inc(norm.done, 1)
                    sweep(act, tiles, full_tiles, last_edges, ADD, step)

                @block.tensor
                def _(pe):
                    def step(tile):
                        t = tile(SUM)
                        if t:
                            n, b = t.rows, t.slot
                            pe.wait_ge(q["z_ready"], t.n + 1)
                            pe.wait_ge(e.eq_in[t.slot], (t.turn + 1) * 16)
                            if positive(t.n - 1):
                                pe.wait_ge(q["z_out"], t.n - 1)
                            for c in range(4):
                                mm = nc.tensor.matmul(psZ[0:96, b % 2, P * c:P * c + n], Z[0:n, b, c, :], e.EQ[0:n, b, 0:n],
                                                      start=True, stop=True)
                            mm.then_inc(q["z_turned"], 1)
                        t = tile(TURN)
                        if t:
                            n, b = t.rows, t.slot
                            pe.wait_ge(norm.done, t.n + 1)
                            pe.wait_ge(el_in[t.slot], (t.turn + 1) * 16)
                            if positive(t.n):
                                pe.wait_ge(q["t_out"], t.n)
                            nc.tensor.transpose(psT[0:96, P:P + n], H[0:n, b, S:D], ident[0:n, 0:n])
                            nc.tensor.transpose(psT[0:S, 0:n], H[0:n, b, 0:S], ident[0:n, 0:n])
                            nc.tensor.transpose(psT[0:10, 2 * P:2 * P + n], EL[0:n, b, :], ident[0:n, 0:n]).then_inc(q["turned"], 1)
                        t = tile(MIX)
                        if t:
                            n, b = t.rows, t.slot
                            pe.wait_ge(q["t_out"], t.n + 1)
                            if positive(t.n - 1):
                                pe.wait_ge(q["hid_out"], t.n - 1)
                            nc.tensor.matmul(psL[0:100, b % 2, 0:n], w("fcr1"), LT[:, b, 0:n], start=True, stop=True)
                            if positive(t.n):
                                pe.wait_ge(q["mix_out"], t.n)
                            o = psM[0:n, 0:2 * D].rearrange("p (k c) -> p k c", k=2)
                            nc.tensor.matmul(o[:, :, 0:S], HT[:, b, 0:n], w("l1_s").rearrange("p (k c) -> p k c", k=2), start=True, stop=True)
                            nc.tensor.matmul(o[:, :, S:D], VT[:, b, 0:n], w("l1_v").rearrange("p (k c) -> p k c", k=2), start=True, stop=True)\
                                .then_inc(q["mixed"], 1)
                        t = tile(FILTER)
                        if t:
                            n, b = t.rows, t.slot
                            pe.wait_ge(q["hid_out"], t.n + 1)
                            if positive(t.n):
                                pe.wait_ge(q["filter_out"], t.n)
                            nc.tensor.matmul(psW[0:n, 0:192], hidT[:, b, 0:n], w("fcr2"), start=True, stop=True).then_inc(q["filter"], 1)
                        t = tile(LINEAR)
                        if t:
                            n, b = t.rows, t.slot
                            pe.wait_ge(q["z_out"], t.n + 1)
                            if positive(t.n):
                                pe.wait_ge(q["result"], t.n)
                            o = psO[0:n, 0:2 * D].rearrange("p (k c) -> p k c", k=2)
                            nc.tensor.matmul(o[:, :, 0:S], ZT[:, b, 0, 0:n], WLs[:, :].rearrange("p (k c) -> p k c", k=2), start=True, stop=True)
                            for i in range(3):
                                mm = nc.tensor.matmul(o[:, :, S + i:D:3], ZT[:, b, 1 + i, 0:n], WLv[:, :].rearrange("p (k c) -> p k c", k=2),
                                                      start=True, stop=True)
                            mm.then_inc(q["linear"], 1)
                    sweep(pe, tiles, full_tiles, last_edges, ADD, step)


        def layer0_edges():
            with nc.cleanup_on_exit(), ExitStack() as ph:
                tag, LAST = "e0", 6
                HALVES, PIECES = 10, 3

                def sb(name, shape, dt=F32):
                    return ph.enter_context(nc.sbuf_tensor(f"{tag}_{name}", shape, dt))

                def pb(name, shape):
                    return ph.enter_context(nc.psum_tensor(f"{tag}_{name}", shape, F32))
                e = EdgePhase(ph, tag, x, DST, SRC, x1, D, (EA4, EA16), (2, 3, 5, LAST), gathers=2)
                norm = Norm(ph, tag, 2)
                zero = sb("zero", [P, G * D])
                Zm, ZmT, CT = sb("Zm", [P, 2, 544]), sb("ZmT", [P, 2, 4, P]), sb("CT", [V, P])
                VR, VD = sb("VR", [P, 3, V]), sb("VD", [P, V])
                xs, a0, xsT, a0T = sb("xs", [P, NB, S]), sb("a0", [P, NB, S]), sb("xsT", [S, 2, P]), sb("a0T", [S, 2, P])
                ak = sb("ak", [P, NB, 3, S])
                outer_p, outer_t, outer_d, outer_v = sb("outer_p", [P, PIECES, 1024]), sb("outer_t", [P, 2, 512]), sb("outer_d", [P, 1024]), sb("outer_v", [P, 3, 1024])
                prod = sb("prod", [P, 3, 2048])
                T4 = pb("T4", [P, 2048])
                psZ, psU, psM = pb("psZ", [P, 2, 512]), pb("psU", [P, 512]), pb("psM", [P, 512])
                q = {m: sem(f"{tag}_{m}") for m in (
                    "zero_set", "zm_pool", "zm_act", "vr", "vr1", "zm_turned", "c_turned", "zmt_out", "ct_out", "xs_out", "message", "a_out",
                    "a_turned", "a0t_out", "maps", "products", "u1", "piece", "dve_piece", "vv_product", "vv_part", "vv_sum", "half_turned", "half_out", "half_used",
                    "u0")}
                t3_zero, pe_passed = sem("t3_zero"), sem("e0_pe_passed")
                block = ph.enter_context(nc.Block())

                @block.sync
                def _(sp):
                    def step(tile):
                        e.loads(sp, tile, rows_used(e), (q["zm_pool"], q["zm_act"]), q["c_turned"])
                        t = tile(0)
                        if t:
                            if isinstance(t.n, int) and t.n == 0:
                                sp.wait_ge(q["zero_set"], 1)
                            t3_piece(sp, t)

                    def t3_piece(sp, t):
                        if isinstance(t.n, int) and t.n >= full_groups:
                            return
                        sp.dma_start(t3[bass.ds(t.n * (P * G), P * G), :].rearrange("(p g) c -> p (g c)", g=G), zero[:, :])\
                            .then_inc(t3_zero, 16)
                    sweep(sp, tiles, full_tiles, last_edges, LAST, step)
                    for g in range(min(tiles, full_groups), full_groups):
                        t3_piece(sp, Tile(g, 0, 0, P))
                    if groups > full_groups:
                        sp.dma_start(t3[full_groups * P * G:N, :].rearrange("(p g) c -> p (g c)", g=G), zero[0:last_parts, :])\
                            .then_inc(t3_zero, 16)
                    sp.wait_ge(t3_zero, 16 * groups)

                @block.gpsimd
                def _(pool):
                    nc.gpsimd.memset(zero[:, :], 0.0).then_inc(q["zero_set"], 1)

                    def piece(t, j):
                        n, b = t.rows, t.slot
                        if positive(t.n * HALVES + (2 * j - 6)):
                            pool.wait_ge(q["half_turned"], t.n * HALVES + (2 * j - 6))
                        nc.gpsimd.tensor_tensor(outer_p[0:n, j, :].rearrange("p (u v) -> p u v", v=S),
                                                repeat(xs[0:n, b, 16 * j + 16:16 * j + 32], 2, S), repeat(a0[0:n, b, :], 1, 16),
                                                ALU.mult).then_inc(q["piece"], 1)

                    def step(tile):
                        t = tile(1)
                        if t:
                            e.gather_rows(pool, t, norm.done)
                        t = tile(5)
                        if t:
                            pool.wait_ge(q["a_out"], t.n + 1)
                            for j in range(PIECES):
                                piece(t, j)
                        t_ = tile(6)
                        if t_:
                            pool.wait_ge(q["u1"], (t_.n + 1) * 3)
                            e.add_rows(pool, t_, q["u0"])
                        if t:
                            n, b = t.rows, t.slot
                            if positive(t.n * HALVES):
                                pool.wait_ge(q["half_turned"], t.n * HALVES)
                            for i in range(3):
                                nc.gpsimd.tensor_tensor(outer_v[0:n, i, :].rearrange("p (u v) -> p u v", v=V), repeat(ak[0:n, b, i, V:S], 2, V),
                                                        repeat(ak[0:n, b, i, 0:V], 1, V), ALU.mult).then_inc(q["vv_product"], 1)
                        t = tile(3)
                        if t:
                            n, b = t.rows, t.slot
                            pool.wait_ge(norm.done, t.n + 1)
                            pool.wait_ge(e.ea_in[t.slot], (t.turn + 1) * 16)
                            if positive(t.n):
                                pool.wait_ge(q["zm_pool"], t.n)
                            z = Zm[0:n, b % 2, :]
                            zi = z[:, P:512].rearrange("p (i c) -> p i c", i=3)
                            nc.gpsimd.tensor_tensor(VR[0:n], zi[:, :, 96:P], repeat(e.EA[0:n, b, 0:3], 2, V), ALU.mult).then_inc(q["vr"], 1)
                            pool.wait_ge(q["vr"], t.n + 1)
                            nc.gpsimd.tensor_tensor(VD[0:n], VR[0:n, 0], VR[0:n, 1], ALU.add).then_inc(q["vr1"], 1)
                            pool.wait_ge(q["vr1"], t.n + 1)
                            nc.gpsimd.tensor_tensor(z[:, 512:544], VD[0:n], VR[0:n, 2], ALU.add).then_inc(q["zm_pool"], 1)
                    sweep(pool, tiles, full_tiles, last_edges, LAST, step)
                    pool.wait_ge(e.added, 16 * tiles)

                @block.scalar
                def _(act):
                    def half(t, h):
                        n = t.rows
                        act.wait_ge(q["half_turned"], t.n * HALVES + (h + 1))
                        if positive(t.n * HALVES + (h - 1)):
                            act.wait_ge(q["half_used"], t.n * HALVES + (h - 1))
                        nc.scalar.copy(outer_t[:, h % 2, :].rearrange("p (c q) -> p c q", c=4)[:, :, 0:n],
                                       psZ[:, (h + 1) % 2, :].rearrange("p (c q) -> p c q", c=4)[:, :, 0:n]).then_inc(q["half_out"], 1)

                    def step(tile):
                        t4_, t5_ = tile(4), tile(5)
                        if t4_:
                            n, b = t4_.rows, t4_.slot % 2
                            act.wait_ge(q["zm_turned"], t4_.n + 1)
                            if positive(t4_.n - 1):
                                act.wait_ge(q["message"], t4_.n - 1)
                            nc.scalar.copy(ZmT[:, b, :, 0:n], psZ[:, 0, :].rearrange("p (c q) -> p c q", c=4)[:, :, 0:n])\
                                .then_inc(q["zmt_out"], 1)
                            act.wait_ge(q["c_turned"], t4_.n + 1)
                            nc.scalar.copy(CT[:, 0:n], psM[0:V, 0:n]).then_inc(q["ct_out"], 1)
                            if positive(t4_.n - 1):
                                act.wait_ge(q["maps"], t4_.n - 1)
                            nc.scalar.copy(xsT[:, b, 0:n], psM[0:S, P:P + n]).then_inc(q["xs_out"], 1)
                        if t5_:
                            half(t5_, 0)
                            half(t5_, 1)
                        if t4_:
                            n, b = t4_.rows, t4_.slot
                            act.wait_ge(q["message"], t4_.n + 1)
                            if positive((t4_.n - (NB - 1)) * 3):
                                act.wait_ge(q["vv_product"], (t4_.n - (NB - 1)) * 3)
                            if positive((t4_.n - (NB - 1)) * 3):
                                act.wait_ge(q["products"], (t4_.n - (NB - 1)) * 3)
                            nc.scalar.copy(a0[0:n, b, :], psM[0:n, 2 * P:2 * P + S])
                            nc.scalar.copy(ak[0:n, b, :, 0:V], psM[0:n, 2 * P + S:2 * P + D].rearrange("p (i v) -> p i v", i=3))\
                                .then_inc(q["a_out"], 1)
                        if t5_:
                            half(t5_, 2)
                            half(t5_, 3)
                        if t4_:
                            n, b = t4_.rows, t4_.slot % 2
                            act.wait_ge(q["a_turned"], t4_.n + 1)
                            nc.scalar.copy(a0T[:, b, 0:n], psM[0:S, 0:n]).then_inc(q["a0t_out"], 1)
                        if t5_:
                            half(t5_, 4)
                            half(t5_, 5)
                        t = tile(3)
                        if t:
                            n, b = t.rows, t.slot
                            act.wait_ge(norm.ready, t.n + 1)
                            if positive(t.n - 1):
                                act.wait_ge(q["c_turned"], t.n - 1)
                            if positive((t.n - (NB - 1)) * 3):
                                act.wait_ge(q["vv_product"], (t.n - (NB - 1)) * 3)
                            if positive(t.n - (NB - 1)):
                                act.wait_ge(q["dve_piece"], t.n - (NB - 1))
                            if positive((t.n - (NB - 1)) * 3):
                                act.wait_ge(q["products"], (t.n - (NB - 1)) * 3)
                            z = Zm[0:n, b % 2, :]
                            zi = z[:, P:512].rearrange("p (i c) -> p i c", i=3)
                            norm.map(t, z[:, S:P], e.X[0:n, b, 0, 0:S], 0)
                            norm.map(t, zi[:, :, 96:P], e.X[0:n, b, 0, S:D].rearrange("p (u i) -> p i u", i=3), 0)
                            norm.map(t, xs[0:n, b, :], e.X[0:n, b, 1, 0:S], 1)
                            norm.map(t, ak[0:n, b, :, V:S], e.X[0:n, b, 1, S:D].rearrange("p (u i) -> p i u", i=3), 1)\
                                .then_inc(norm.done, 1)
                            act.wait_ge(e.ea_in[t.slot], (t.turn + 1) * 16)
                            act.wait_ge(norm.done, t.n + 1)
                            dist = e.EA[0:n, b, 3:4]
                            nc.scalar.activation(z[:, 0:S], z[:, S:P], ACT.Copy, scale=dist)
                            for i in range(3):
                                nc.scalar.activation(zi[:, i, 0:S], z[:, S:P], ACT.Copy, scale=e.EA[0:n, b, i:i + 1])
                            nc.scalar.activation(zi[:, :, S:96], zi[:, :, 96:P], ACT.Copy, scale=dist).then_inc(q["zm_act"], 1)
                        if t5_:
                            for h in range(6, 8):
                                half(t5_, h)
                        t = tile(2)
                        if t:
                            norm.root(act, t)
                        if t5_:
                            for h in range(8, HALVES):
                                half(t5_, h)
                            n, b = t5_.rows, t5_.slot
                            act.wait_ge(q["half_used"], (t5_.n + 1) * HALVES)
                            if positive((t5_.n - (NB - 1)) * 16):
                                act.wait_ge(e.added, (t5_.n - (NB - 1)) * 16)
                            nc.scalar.copy(e.R[0:n, b, 0:S], psU[0:n, 0:S]).then_inc(q["u0"], 1)
                    sweep(act, tiles, full_tiles, last_edges, LAST, step)

                @block.tensor
                def _(pe):
                    wss = w("u_ss").rearrange("p (c n) -> p c n", n=S)
                    wvv = w("u_vv").rearrange("p (c n) -> p c n", n=S)

                    def turn(t, h):
                        n = t.rows
                        if h < 2:
                            pe.wait_ge(q["dve_piece"], t.n + 1)
                            source = outer_d[0:n, :]
                        elif h < 8:
                            pe.wait_ge(q["piece"], t.n * PIECES + h // 2)
                            source = outer_p[0:n, h // 2 - 1, :]
                        else:
                            pe.wait_ge(q["vv_sum"], t.n + 1)
                            source = outer_v[0:n, 0, :]
                        if positive(t.n * HALVES + (h - 1)):
                            pe.wait_ge(q["half_out"], t.n * HALVES + (h - 1))
                        for c in range(4):
                            at = (h % 2) * 512 + c * P
                            tr = nc.tensor.transpose(psZ[:, (h + 1) % 2, c * P:c * P + n], source[:, at:at + P], ident[0:n, 0:n])
                        tr.then_inc(q["half_turned"], 1)

                    def use(t, h):
                        n = t.rows
                        pe.wait_ge(q["half_out"], t.n * HALVES + (h + 1))
                        if h == 0:
                            if positive(t.n):
                                pe.wait_ge(q["u0"], t.n)
                        for c in range(4):
                            weights = wss[:, 4 * h + c, :] if h < 8 else wvv[:, 4 * (h % 2) + c, :]
                            mm = nc.tensor.matmul(psU[0:n, 0:S], outer_t[:, h % 2, c * P:c * P + n], weights,
                                                  start=(h == 0 and c == 0), stop=(h == HALVES - 1 and c == 3))
                        mm.then_inc(q["half_used"], 1)

                    def step(tile):
                        t4_, t5_ = tile(4), tile(5)
                        if t4_:
                            n, b = t4_.rows, t4_.slot
                            pe.wait_ge(q["zm_pool"], t4_.n + 1)
                            pe.wait_ge(q["zm_act"], t4_.n + 1)
                            pe.wait_ge(e.eq_in[t4_.slot], (t4_.turn + 1) * 16)
                            if positive((t4_.n - 1) * HALVES):
                                pe.wait_ge(q["half_out"], (t4_.n - 1) * HALVES)
                            z, eq = Zm[0:n, b % 2, :], e.EQ[0:n, b, 0:n]
                            for c in range(4):
                                mm = nc.tensor.matmul(psZ[:, 0, c * P:c * P + n], z[:, c * P:(c + 1) * P], eq, start=True, stop=True)
                            mm.then_inc(q["zm_turned"], 1)
                            if positive(t4_.n):
                                pe.wait_ge(q["a0t_out"], t4_.n)
                            nc.tensor.matmul(psM[0:V, 0:n], z[:, 512:544], eq, start=True, stop=True)
                            nc.tensor.transpose(psM[0:S, P:P + n], xs[0:n, b, :], ident[0:n, 0:n]).then_inc(q["c_turned"], 1)
                        if t5_:
                            turn(t5_, 0)
                            if t4_:
                                pe.wait_ge(q["zmt_out"], t4_.n + 1)
                            turn(t5_, 1)
                            use(t5_, 0)
                        if t4_:
                            n, b = t4_.rows, t4_.slot
                            pe.wait_ge(q["zmt_out"], t4_.n + 1)
                            pe.wait_ge(q["ct_out"], t4_.n + 1)
                            pe.wait_ge(q["xs_out"], t4_.n + 1)
                            if positive(t4_.n):
                                pe.wait_ge(q["a_out"], t4_.n)
                            nc.tensor.matmul(psM[0:n, 2 * P:2 * P + S], ZmT[:, b % 2, 0, 0:n], w("m_a"), start=True, stop=False)
                            nc.tensor.matmul(psM[0:n, 2 * P:2 * P + S], CT[:, 0:n], w("m_c"), start=False, stop=True)
                            for i in range(3):
                                at = 2 * P + S + V * i
                                mm = nc.tensor.matmul(psM[0:n, at:at + V], ZmT[:, b % 2, 1 + i, 0:n], w("m_b"), start=True, stop=True)
                            mm.then_inc(q["message"], 1)
                        if t5_:
                            turn(t5_, 2)
                            use(t5_, 1)
                            turn(t5_, 3)
                            use(t5_, 2)
                        if t4_:
                            n, b = t4_.rows, t4_.slot
                            pe.wait_ge(q["a_out"], t4_.n + 1)
                            pe.sem_inc(pe_passed, 1)
                            nc.tensor.transpose(psM[0:S, 0:n], a0[0:n, b, :], ident[0:n, 0:n]).then_inc(q["a_turned"], 1)
                        if t5_:
                            turn(t5_, 4)
                            use(t5_, 3)
                            turn(t5_, 5)
                            use(t5_, 4)
                        if t4_:
                            n, b = t4_.rows, t4_.slot % 2
                            pe.wait_ge(q["xs_out"], t4_.n + 1)
                            pe.wait_ge(q["a0t_out"], t4_.n + 1)
                            if positive(t4_.n * 3):
                                pe.wait_ge(q["products"], t4_.n * 3)
                            for c in range(2):
                                nc.tensor.matmul(T4[0:n, 512 * c:512 * c + 512], xsT[:, b, 0:n], w("u_sv")[:, 512 * c:512 * c + 512],
                                                 start=True, stop=True)
                            for c in range(2):
                                mm = nc.tensor.matmul(T4[0:n, 1024 + 512 * c:1536 + 512 * c], a0T[:, b, 0:n],
                                                      w("u_vs")[:, 512 * c:512 * c + 512], start=True, stop=True)
                            mm.then_inc(q["maps"], 1)
                        if t5_:
                            for h in range(6, HALVES):
                                turn(t5_, h)
                                use(t5_, h - 1)
                            use(t5_, HALVES - 1)
                    sweep(pe, tiles, full_tiles, last_edges, LAST, step)

                @block.vector
                def _(dve):
                    def step(tile):
                        t = tile(5)
                        if t:
                            n, b = t.rows, t.slot
                            dve.wait_ge(q["maps"], t.n + 1)
                            dve.wait_ge(q["a_out"], t.n + 1)
                            t4 = T4[0:n, :].rearrange("p (k w) -> p k w", w=V)
                            for i in range(3):
                                if positive((t.n - 1) * 3 + (i + 1)):
                                    dve.wait_ge(q["u1"], (t.n - 1) * 3 + (i + 1))
                                nc.vector.tensor_tensor(prod[0:n, i, :].rearrange("p (k w) -> p k w", w=V), t4,
                                                        repeat(ak[0:n, b, i, :], 2, V), ALU.mult).then_inc(q["products"], 1)
                        t2 = tile(2)
                        if t2:
                            dve.wait_ge(e.rows_in[t2.slot], (t2.turn + 1) * 32)
                            norm.statistics(dve, t2, [e.X[0:t2.rows, t2.slot, g, :] for g in range(2)])
                        if t:
                            if positive((t.n - (NB - 1)) * 16):
                                dve.wait_ge(e.added, (t.n - (NB - 1)) * 16)
                            for i in range(3):
                                dve.wait_ge(q["products"], t.n * 3 + (i + 1))
                                nc.vector.tensor_reduce(e.R[0:n, b, S + i:D:3], prod[0:n, i, :].rearrange("p (k w) -> p w k", w=V),
                                                        AX_X, ALU.add).then_inc(q["u1"], 1)
                        if t:
                            n = t.rows
                            if positive(t.n * 3 + 2):
                                dve.wait_ge(q["vv_product"], t.n * 3 + 2)
                            nc.vector.tensor_tensor(outer_v[0:n, 0, :], outer_v[0:n, 0, :], outer_v[0:n, 1, :], ALU.add)\
                                .then_inc(q["vv_part"], 1)
                            if positive(t.n * 3 + 3):
                                dve.wait_ge(q["vv_product"], t.n * 3 + 3)
                            dve.wait_ge(q["vv_part"], t.n + 1)
                            nc.vector.tensor_tensor(outer_v[0:n, 0, :], outer_v[0:n, 0, :], outer_v[0:n, 2, :], ALU.add)\
                                .then_inc(q["vv_sum"], 1)
                        if t2:
                            norm.scales(dve, t2)
                        t = tile(4)
                        if t:
                            n, b = t.rows, t.slot
                            dve.wait_ge(q["a_out"], t.n + 1)
                            if positive((t.n - 1) * HALVES + 2):
                                dve.wait_ge(q["half_turned"], (t.n - 1) * HALVES + 2)
                            nc.vector.tensor_tensor(outer_d[0:n, :].rearrange("p (u v) -> p u v", v=S), repeat(xs[0:n, b, 0:16], 2, S),
                                                    repeat(a0[0:n, b, :], 1, 16), ALU.mult).then_inc(q["dve_piece"], 1)
                    sweep(dve, tiles, full_tiles, last_edges, LAST, step)

        dense_phase("d0", 0)
        layer0_edges()
        dense_phase("d1", 1)
        layer1_edges()
        dense_phase("d2", 2)
        layer2_edges()
        layer3_edges()
        dense_phase("d3", 3)


def kernel(**inputs):
    import numpy as _np
    import concourse.bacc as _bacc
    from concourse.bass_utils import run_bass_kernel_spmd as _run

    a = {k: _np.asarray(v) for k, v in inputs.items()}
    N, E = a["x"].shape[0], a["src"].shape[0]

    def kron(m):
        o = _np.zeros((3 * m.shape[0], 3 * m.shape[1]), m.dtype)
        for i in range(3):
            o[i::3, i::3] = m
        return o

    def apart(m):
        r, c = m.shape
        o = _np.zeros((3 * r, 3 * c), m.dtype)
        for i in range(3):
            o[i::3, i * c:(i + 1) * c] = m
        return o

    def chunks(m):
        return m.reshape(-1, P, m.shape[-1]).transpose(1, 0, 2).reshape(P, -1)

    rows, cols = (lambda *m: _np.concatenate(m, 0)), (lambda *m: _np.concatenate(m, 1))
    l0, l1, l2, l3 = (lambda k, g=g: a[f"L{g}_gnn_{k}"] for g in range(4))
    blocks = {
        "u_ss": chunks(l0("Wu_ss").reshape(S * S, S)), "u_vv": chunks(l0("Wu_vv").reshape(V * V, S)),
        "u_sv": l0("Wu_sv").reshape(S, V * V), "u_vs": l0("Wu_vs").transpose(1, 0, 2).reshape(S, V * V),
        "m_a": rows(l0("Wm_ss"), l0("Lm_s")), "m_c": l0("Wm_vv"), "m_b": rows(l0("Wm_sv"), l0("Wm_vs"), l0("Lm_v")),
        "lu_s": l0("Lu_s"), "lu_v": kron(l0("Lu_v")),
        "skip_s": l1("W_skip0"), "skip_v": kron(l1("W_skip1")), "nl_s": l1("W_nl0"), "nl_v": apart(l1("W_nl1")),
        "fc1": l1("W_fc1"), "fc2": l1("W_fc2"), "out_s": l1("W_out_s"), "out_v": l1("W_out_v"),
        "l2_s": rows(l2("W_ss"), l2("W_vv")), "l2_v": rows(l2("W_sv"), l2("W_vs")),
        "rad": rows(l2("W_rad").T, l2("b_rad").reshape(1, -1)), "l2l_s": l2("L_s"), "l2l_v": kron(l2("L_v")),
        "sc_s": cols(l3("Ws_sc_a"), l3("Ws_sc_c")), "sc_v": cols(kron(l3("Wv_sc_a")), kron(l3("Wv_sc_c"))),
        "l1_s": cols(l3("Ws_l1_a"), l3("Ws_l1_c")), "l1_v": cols(apart(l3("Wv_l1_a")), apart(l3("Wv_l1_c"))),
        "fcr1": l3("W_fc1"), "fcr2": l3("W_fc2"),
        "l2aT_s": l3("Ws_l2_a").T, "l2cT_s": l3("Ws_l2_c").T, "l2aT_v": l3("Wv_l2_a").T, "l2cT_v": l3("Wv_l2_c").T,
        "l3_s": l3("Ws_l3"), "l3_v": l3("Wv_l3"),
    }
    start, width = weight_columns()
    wpack, wscale = _np.zeros((P, width), _np.float32), _np.zeros((P, width), _np.float32)
    for name, (r, c, scales) in weight_blocks().items():
        assert blocks[name].shape == (r, c), name
        wpack[0:r, start[name]:start[name] + c] = blocks[name]
        for r0, r1, c0, c1, s in scales:
            wscale[r0:r1, start[name] + c0:start[name] + c1] = s
    consts = _np.zeros((P, K_WIDTH), _np.float32)
    consts[:, K_IDENT:K_IDENT + P] = _np.eye(P)
    consts[:, K_LOWER:K_LOWER + P] = _np.tril(_np.ones((P, P)), -1)
    consts[:, K_JUNK] = N + _np.arange(P)
    consts[:, K_EPS] = EPS
    idx2 = _np.ascontiguousarray(_np.stack([a["src"], a["dst"]], 1))
    arrays = {
        "x": a["x"], "idx2": idx2, "idx2T": _np.ascontiguousarray(idx2.T),
        "ea": _np.ascontiguousarray(cols(a["edge_attr_10"], a["edge_attr_4"], a["edge_attr_16"], a["edge_attr_3"], a["edge_attr_64"])),
        "nattr": _np.pad(cols(a["node_vec1"], a["node_vec1_n2"], a["node_vec1_n3"]), ((0, P), (0, 0))),
        "wpack": wpack, "wscale": wscale, "consts": consts,
    }
    nc = _bacc.Bacc("TRN2", target_bir_lowering=False, num_devices=1)
    args = {k: nc.dram_tensor(k, v.shape, mybir.dt.from_np(v.dtype), kind="ExternalInput").ap() for k, v in arrays.items()}
    out = nc.dram_tensor("out", (N, D), F32, kind="ExternalOutput").ap()
    build(nc, N, E, out=out, **args)
    r = _run(nc, [arrays], core_ids=[0])
    return r.results[0]["out"]
```

```python
from contextlib import ExitStack

import numpy as np

import concourse.bass as bass
from concourse import mybir

F32 = mybir.dt.float32
I32 = mybir.dt.int32
ALU = mybir.AluOpType
ACT = mybir.ActivationFunctionType
AX_X = mybir.AxisListType.X

P = 128
S, V = 64, 32
D = S + 3 * V
G = 4
NB = 6
EPS = 1e-5

EA10, EA4, EA16, EA3, EA64, EAW = 0, 10, 14, 30, 33, 97
K_IDENT, K_LOWER, K_JUNK, K_EPS, K_WIDTH = 0, P, 2 * P, 2 * P + 1, 2 * P + 2

INV_SQRT3 = 3.0 ** -0.5
INV_SQRT32 = 32.0 ** -0.5
INV_SQRT2 = 2.0 ** -0.5
C_S = float(np.sin(np.pi / 8.0))
C_X = float(np.cos(np.pi / 8.0))


def weight_blocks():
    def one(r, c, scale=1.0):
        return (r, c, [(0, r, 0, c, scale)])
    msg_v = INV_SQRT3 * INV_SQRT32
    return {
        "u_ss": one(P, 2048, 1 / 64), "u_vv": one(P, 512, INV_SQRT3 / 32),
        "u_sv": one(S, 1024, 2048.0 ** -0.5), "u_vs": one(S, 1024, 2048.0 ** -0.5),
        "m_a": one(P, S, 0.125), "m_c": one(V, S, msg_v),
        "m_b": (P, V, [(0, S, 0, V, 0.125), (S, P, 0, V, INV_SQRT32)]),
        "lu_s": one(P, P, 0.125), "lu_v": one(96, 96, INV_SQRT32),
        "skip_s": one(P, 192), "skip_v": one(96, 96), "nl_s": one(S, S), "nl_v": one(96, 96),
        "fc1": one(64, 64), "fc2": one(64, 224), "out_s": one(96, 96, 1 / 32),
        "out_v": (P, V, [(0, 96, 0, V, 1 / 32), (96, P, 0, V, INV_SQRT2 / 32)]),
        "l2_s_rad": (113, S + D, [(0, S, 0, S, INV_SQRT2 / 8), (S, 96, 0, S, msg_v * INV_SQRT2), (96, 113, S, S + D, 1.0)]),
        "l2_v": (96, V, [(0, S, 0, V, INV_SQRT3 / 8 * INV_SQRT2), (S, 96, 0, V, msg_v * INV_SQRT2)]),
        "l2l_s": one(P, P, 0.125), "l2l_v": one(96, 96, INV_SQRT32),
        "sc_s": one(P, 2 * S, C_S), "sc_v": one(96, 192, C_S), "l1_s": one(S, 2 * S), "l1_v": one(96, 192),
        "fcr1": one(10, 100), "fcr2": one(100, 192),
        "l2aT_s": (96, 96, [(0, 96, 0, 64, 1.0), (0, 96, 64, 96, INV_SQRT3)]),
        "l2cT_s": (96, 96, [(0, 96, 0, 64, 1.0), (0, 96, 64, 96, INV_SQRT3)]),
        "l2aT_v": one(96, 96), "l2cT_v": one(96, 96),
        "l3_s": one(96, S, C_X / 4), "l3_v": one(96, V, C_X / 4),
    }


def weight_columns():
    at, start = 0, {}
    for name, (_, cols, _) in weight_blocks().items():
        start[name] = at
        at += cols
    return start, at


class Tile:

    def __init__(self, n, slot, turn, rows):
        self.n, self.slot, self.turn, self.rows = n, slot, turn, rows


def sweep(eng, total, full, last_rows, deepest, step):
    def straight(k):
        def tile(lag):
            n = k - lag
            if n < 0 or n >= total:
                return None
            return Tile(n, n % NB, n // NB, P if n < full else last_rows)
        step(tile)

    first = NB * (-(-(deepest + NB) // NB))
    turns = max(0, (full - first) // NB)
    if turns < 2:
        turns = 0
    else:
        for k in range(first):
            straight(k)
        with eng.Fori(0, turns) as j:
            for u in range(NB):
                def tile(lag, k=first + u):
                    n = k - lag
                    return Tile(j * NB + n, n % NB, j + n // NB, P)
                step(tile)
    for k in range(first + turns * NB if turns else 0, total + deepest):
        straight(k)


def positive(count):
    return not isinstance(count, int) or count > 0


def repeat(ap, axis, n):
    shape = list(ap.shape)
    shape.insert(axis, n)
    return ap.unsqueeze(axis).broadcast_to(shape)


def build(nc, N, E, x, idx2, idx2T, ea, nattr, wpack, wscale, consts, out):
    NJ = N + P
    tiles, full_tiles = -(-E // P), E // P
    last_edges = E - (tiles - 1) * P
    groups, full_groups = -(-N // (P * G)), N // (P * G)
    last_parts = (N - (groups - 1) * P * G) // G
    assert N == E * G
    WCOL, WWIDTH = weight_columns()
    BLOCKS = weight_blocks()

    def table(name, cols, rows=NJ, dt=F32):
        return nc.dram_tensor(name, (rows, cols), dt, kind="Internal").ap()

    x1, p1, h2, x3, t3 = table("x1", D), table("p1", 192), table("h2", D, N), table("x3", D), table("t3", D)
    same = table("same", 2 * P, tiles * P)
    unique = table("unique", 2, tiles * P, I32)

    outer = ExitStack()
    with outer:
        def sem(name):
            return nc.alloc_semaphore(name=name)

        def ring_sems(name, n=NB):
            return [sem(f"{name}{i}") for i in range(n)]

        W = outer.enter_context(nc.sbuf_tensor("W", [P, WWIDTH], F32))
        K = outer.enter_context(nc.sbuf_tensor("K", [P, K_WIDTH], F32))
        WLs = outer.enter_context(nc.sbuf_tensor("WLs", [96, 2 * S], F32))
        WLv = outer.enter_context(nc.sbuf_tensor("WLv", [96, 2 * V], F32))
        ident = K[:, K_IDENT:K_IDENT + P]
        lower = K[:, K_LOWER:K_LOWER + P]
        junk = K[:, K_JUNK:K_JUNK + 1]
        epsilon = K[:, K_EPS:K_EPS + 1]

        def w(name):
            r, c, _ = BLOCKS[name]
            return W[0:r, WCOL[name]:WCOL[name] + c]

        with nc.cleanup_on_exit(), ExitStack() as ph:
            scale = ph.enter_context(nc.sbuf_tensor("scale", [P, WWIDTH], F32))
            zero = ph.enter_context(nc.sbuf_tensor("zero", [P, 192], F32))
            pl = ph.enter_context(nc.psum_tensor("pl", [P, 512], F32))
            weights_in, zeroed, junk_clean = sem("weights_in"), sem("zeroed"), sem("junk_clean")
            scaled, folded, folded_out, with_identity = sem("scaled"), sem("folded"), sem("folded_out"), sem("with_identity")
            block = ph.enter_context(nc.Block())

            @block.sync
            def _(sp):
                sp.dma_start(W[:, :], wpack).then_inc(weights_in, 16)
                sp.dma_start(scale[:, :], wscale).then_inc(weights_in, 16)
                sp.dma_start(K[:, :], consts).then_inc(weights_in, 16)
                sp.wait_ge(zeroed, 1)
                for t in (x1, p1, x3, t3):
                    sp.dma_start(t[N:NJ, :], zero[:, 0:t.shape[1]]).then_inc(junk_clean, 16)
                sp.wait_ge(junk_clean, 64)

            @block.vector
            def _(dve):
                nc.vector.memset(zero[:, :], 0.0).then_inc(zeroed, 1)
                dve.wait_ge(weights_in, 48)
                nc.vector.tensor_tensor(W[:, :], W[:, :], scale[:, :], ALU.mult).then_inc(scaled, 1)
                dve.wait_ge(scaled, 1)
                nc.vector.tensor_tensor(w("lu_s"), w("lu_s"), ident, ALU.add).then_inc(with_identity, 1)
                nc.vector.tensor_tensor(w("lu_v"), w("lu_v"), ident[0:96, 0:96], ALU.add).then_inc(with_identity, 1)
                dve.wait_ge(folded, 1)
                nc.vector.tensor_copy(WLs[:, :], pl[0:96, 0:2 * S]).then_inc(folded_out, 1)
                nc.vector.tensor_copy(WLv[:, :], pl[0:96, 2 * S:2 * S + 2 * V]).then_inc(folded_out, 1)
                dve.wait_ge(folded_out, 2)
                dve.wait_ge(with_identity, 2)

            @block.tensor
            def _(pe):
                pe.wait_ge(scaled, 1)
                for n, (a, b, at, m) in enumerate((("l2aT_s", "l3_s", 0, S), ("l2cT_s", "l3_s", S, S),
                                                   ("l2aT_v", "l3_v", 2 * S, V), ("l2cT_v", "l3_v", 2 * S + V, V))):
                    mm = nc.tensor.matmul(pl[0:96, at:at + m], w(a), w(b), start=True, stop=True)
                mm.then_inc(folded, 1)

        NEWTON = 10

        def inverse_root(dve, t, steps, v, bits, tmp, y, at):
            if at:
                if positive(t.n * (NEWTON + 1) + at):
                    dve.wait_ge(steps, t.n * (NEWTON + 1) + at)
            if at == 0:
                ins = nc.vector.tensor_scalar(bits, v.bitcast(I32), 1, None, ALU.logical_shift_right)
            elif at == 1:
                ins = nc.vector.tensor_scalar(y.bitcast(I32), bits, -1.0, float(0x5F3759DF), ALU.mult, ALU.add)
            elif at % 3 == 2:
                ins = nc.vector.scalar_tensor_tensor(tmp, y, -0.5, y, ALU.mult, ALU.mult)
            elif at % 3 == 0:
                ins = nc.vector.tensor_tensor(tmp, tmp, v, ALU.mult)
            else:
                ins = nc.vector.scalar_tensor_tensor(y, tmp, 1.5, y, ALU.add, ALU.mult)
            ins.then_inc(steps, 1)

        class Norm:

            def __init__(self, ph, tag, parts):
                def sb(name, shape, dt=F32):
                    return ph.enter_context(nc.sbuf_tensor(f"{tag}_{name}", shape, dt))
                self.parts = parts
                self.bn, self.mv = sb("bn", [P, 2, parts, 6]), sb("mv", [P, NB, parts, 2])
                self.var, self.tmp, self.bits = sb("var", [P, NB, parts]), sb("tmp", [P, parts]), sb("bits", [P, parts], I32)
                self.rstd, self.shift = sb("rstd", [P, NB, parts]), sb("shift", [P, NB, parts])
                self.stats, self.moments = sem(f"{tag}_stats"), sem(f"{tag}_moments")
                self.widened, self.steps, self.inverted = sem(f"{tag}_widened"), sem(f"{tag}_steps"), sem(f"{tag}_inverted")
                self.passed = sem(f"{tag}_dve_passed")
                self.ready, self.done = sem(f"{tag}_norm_ready"), sem(f"{tag}_norm_done")

            def statistics(self, dve, t, views):
                n, b = t.rows, t.slot
                if positive(t.n - (NB - 1)):
                    dve.wait_ge(self.done, t.n - (NB - 1))
                for q, v in enumerate(views):
                    self.partial(t, q, v)
                dve.wait_ge(self.stats, t.n + 1)
                dve.sem_inc(self.passed, 1)
                for q in range(self.parts):
                    self.moment(t, q)

            def partial(self, t, q, view):
                ins = nc.vector.bn_stats(self.bn[0:t.rows, t.slot % 2, q, :], view)
                if q == self.parts - 1:
                    ins.then_inc(self.stats, 1)

            def moment(self, t, q):
                ins = nc.vector.bn_aggr(self.mv[0:t.rows, t.slot, q, :], self.bn[0:t.rows, t.slot % 2, q, :])
                if q == self.parts - 1:
                    ins.then_inc(self.moments, 1)

            def root(self, act, t):
                n, b = t.rows, t.slot
                act.wait_ge(self.moments, t.n + 1)
                nc.scalar.activation(self.var[0:n, b, :], self.mv[0:n, b, :, 1], ACT.Sqrt, bias=epsilon[0:n, :])\
                    .then_inc(self.widened, 1)

            def scales(self, dve, t):
                n, b = t.rows, t.slot
                dve.wait_ge(self.widened, t.n + 1)
                nc.vector.reciprocal(self.rstd[0:n, b, :], self.var[0:n, b, :]).then_inc(self.inverted, 1)
                dve.wait_ge(self.inverted, t.n + 1)
                self.shifts(dve, t)

            def widen(self, dve, t):
                n, b = t.rows, t.slot
                dve.wait_ge(self.moments, t.n + 1)
                nc.vector.tensor_scalar(self.var[0:n, b, :], self.mv[0:n, b, :, 1], EPS, None, ALU.add).then_inc(self.widened, 1)
                dve.wait_ge(self.widened, t.n + 1)

            def newton(self, dve, t, at):
                n, b = t.rows, t.slot
                inverse_root(dve, t, self.steps, self.var[0:n, b, :], self.bits[0:n], self.tmp[0:n], self.rstd[0:n, b, :], at)

            def newton_shifts(self, dve, t):
                if positive((t.n + 1) * (NEWTON + 1)):
                    dve.wait_ge(self.steps, (t.n + 1) * (NEWTON + 1))
                self.shifts(dve, t)

            def shifts(self, dve, t):
                n, b = t.rows, t.slot
                nc.vector.scalar_tensor_tensor(self.shift[0:n, b, :], self.mv[0:n, b, :, 0], -1.0, self.rstd[0:n, b, :],
                                               ALU.mult, ALU.mult).then_inc(self.ready, 1)

            def map(self, t, out_ap, in_ap, q):
                n, b = t.rows, t.slot
                return nc.scalar.activation(out_ap, in_ap, ACT.Relu, bias=self.shift[0:n, b, q:q + 1],
                                            scale=self.rstd[0:n, b, q:q + 1])

        def rows_of(tab, t):
            return tab[bass.ds(t.n * (P * G), t.rows * G), :].rearrange("(p g) c -> p g c", g=G)

        def dense_phase(tag, kind):
            newton = kind == 2
            STATS = 3 if kind == 2 else 1
            MAP = STATS + 2
            TURN, MUL, STORE = MAP + 1, MAP + 2, MAP + 3
            source = (x, x1, x1, x3)[kind]
            width = (D, 192, D, 2 * D)[kind]
            weights = (("lu_s", "lu_v"), ("skip_s", "skip_v"), ("l2l_s", "l2l_v"), ("sc_s", "sc_v"))[kind]
            loads = (1, 1, 2, 3)[kind]
            with nc.cleanup_on_exit(), ExitStack() as ph:
                def sb(name, shape, dt=F32):
                    return ph.enter_context(nc.sbuf_tensor(f"{tag}_{name}", shape, dt))
                X = sb("X", [P, NB, G, D])
                H = sb("H", [P, NB, 2, 2 * D])
                HsT, HvT = sb("HsT", [P, 2, 256]), sb("HvT", [96, 2, 512])
                Y = sb("Y", [P, NB, G, 192 if kind == 1 else D])
                if kind == 0:
                    col, row = sb("col", [P, NB, 2], I32), sb("row", [P, NB, 2, P], I32)
                    eq, early = sb("eq", [P, NB, 2, P]), sb("early", [P, 2, 2, P])
                    off, rep, moved = sb("off", [P, 2]), sb("rep", [P, 2]), sb("moved", [P, 2])
                    uniq = sb("uniq", [P, NB, 2], I32)
                    index_in, index_stored = ring_sems("ix_in"), ring_sems("ix_stored")
                    ix = {n: sem("ix_" + n) for n in ("compared", "masked", "counted", "offset", "moved", "ready")}
                if kind == 2:
                    Pt, Gt, X2 = sb("Pt", [P, NB, G, 192]), sb("Gt", [P, 2, G, 96]), sb("X2", [P, NB, G, D])
                if kind == 3:
                    T3, NA, XT = sb("T3", [P, NB, G, D]), sb("NA", [P, NB, G, 3]), sb("XT", [P, NB, G, D])
                    A1 = sb("A1", [P, 2, G, D])
                psS = ph.enter_context(nc.psum_tensor(f"{tag}_psS", [P, 2, 512], F32))
                psV = ph.enter_context(nc.psum_tensor(f"{tag}_psV", [P, 2, 512], F32))
                psO = ph.enter_context(nc.psum_tensor(f"{tag}_psO", [P, 4, 512], F32))
                norm = Norm(ph, tag, G)
                loaded, stored = ring_sems(f"{tag}_loaded"), ring_sems(f"{tag}_stored")
                turned, s_out, v_out = sem(f"{tag}_turned"), sem(f"{tag}_s_out"), sem(f"{tag}_v_out")
                product, summed = sem(f"{tag}_product"), sem(f"{tag}_summed")
                pair_used = sem(f"{tag}_pair_used")
                if kind >= 2:
                    gates, gated, residual_ready, part_a = (sem(f"{tag}_{n}") for n in ("gates", "gated", "residual_ready", "part_a"))
                block = ph.enter_context(nc.Block())

                @block.sync
                def _(sp):
                    def step(tile):
                        t = tile(0)
                        if t:
                            n, b = t.rows, t.slot
                            if kind == 1:
                                if positive(t.n - (NB - 1)):
                                    sp.wait_ge(norm.done, t.n - (NB - 1))
                            if kind >= 2:
                                if positive(t.n - (NB - 1)):
                                    sp.wait_ge(residual_ready, t.n - (NB - 1))
                            if kind == 3:
                                if positive(t.n - (NB - 1)):
                                    sp.wait_ge(norm.done, t.n - (NB - 1))
                            if kind in (0, 3):
                                if positive(t.n - (NB - 1)):
                                    sp.wait_ge(summed, t.n - (NB - 1))
                            sp.dma_start(X[0:n, b, :, :], rows_of(source, t)).then_inc(loaded[b], 16)
                            if kind == 2:
                                sp.dma_start(Pt[0:n, b, :, :], rows_of(p1, t)).then_inc(loaded[b], 16)
                            if kind == 3:
                                sp.dma_start(T3[0:n, b, :, :], rows_of(t3, t)).then_inc(loaded[b], 16)
                                sp.dma_start(NA[0:n, b, :, :], rows_of(nattr, t)).then_inc(loaded[b], 16)
                        t = tile(STORE)
                        if t:
                            n, b = t.rows, t.slot
                            sp.wait_ge(summed, t.n + 1)
                            target = (x1, p1, x3, out)[kind]
                            sp.dma_start(rows_of(target, t), Y[0:n, b, :, :]).then_inc(stored[b], 16)
                            if kind == 2:
                                rows = rows_of(h2, t).rearrange("p (k q) c -> p k q c", k=2)
                                sp.dma_start(rows[:, :, 0, S:D], H[0:n, b, :, 0:96]).then_inc(stored[b], 16)
                                sp.dma_start(rows[:, :, 0, 0:S], H[0:n, b, :, 96:D]).then_inc(stored[b], 16)
                                sp.dma_start(rows[:, :, 1, :], H[0:n, b, :, D:2 * D]).then_inc(stored[b], 16)
                        if kind == 0:
                            index_step(tile)

                    def index_step(tile):
                        t = tile(0)
                        if t:
                            n, b = t.rows, t.slot
                            if positive(t.n - (NB - 1)):
                                sp.wait_ge(ix["ready"], t.n - (NB - 1))
                            sp.dma_start(col[0:n, b, :], idx2[bass.ds(t.n * P, n), :]).then_inc(index_in[b], 16)
                            for a in range(2):
                                sp.dma_start(row[0:n, b, a, 0:n], idx2T[a:a + 1, bass.ds(t.n * P, n)].broadcast_to([n, n]))\
                                  .then_inc(index_in[b], 16)
                        t = tile(5)
                        if t:
                            n, b = t.rows, t.slot
                            sp.wait_ge(ix["ready"], t.n + 1)
                            sp.dma_start(unique[bass.ds(t.n * P, n), :], uniq[0:n, b, :]).then_inc(index_stored[b], 16)
                            sp.dma_start(same[bass.ds(t.n * P, n), :].rearrange("p (a q) -> p a q", a=2)[:, :, 0:n],
                                         eq[0:n, b, :, 0:n]).then_inc(index_stored[b], 16)
                    sweep(sp, groups, full_groups, last_parts, STORE, step)
                    for b in range(NB):
                        sp.wait_ge(stored[b], (64 if kind == 2 else 16) * ((groups - 1 - b) // NB + 1))
                        if kind == 0:
                            sp.wait_ge(index_stored[b], 32 * ((tiles - 1 - b) // NB + 1))

                @block.scalar
                def _(act):
                    def step(tile):
                        t = tile(MAP)
                        if t:
                            n, b = t.rows, t.slot
                            act.wait_ge(norm.ready, t.n + 1)
                            if kind == 2:
                                if positive(t.turn):
                                    act.wait_ge(stored[t.slot], t.turn * 64)
                            else:
                                if positive(t.n - (NB - 1)):
                                    act.wait_ge(turned, t.n - (NB - 1))
                            src = X2 if kind == 2 else X
                            for p in range(2):
                                norm.map(t, H[0:n, b, p, 0:96], src[0:n, b, 2 * p, S:D], 2 * p)
                                norm.map(t, H[0:n, b, p, 96:D], src[0:n, b, 2 * p, 0:S], 2 * p)
                                ins = norm.map(t, H[0:n, b, p, D:2 * D], src[0:n, b, 2 * p + 1, :], 2 * p + 1)
                            ins.then_inc(norm.done, 1)
                        t = tile(STATS + 1)
                        if t and not newton:
                            norm.root(act, t)
                        t = tile(1)
                        if t and kind == 2:
                            n, b = t.rows, t.slot
                            act.wait_ge(loaded[t.slot], (t.turn + 1) * (16 * (loads)))
                            if positive(t.n - 1):
                                act.wait_ge(gated, t.n - 1)
                            nc.scalar.activation(Gt[0:n, b % 2, :, :], Pt[0:n, b, :, 0:96], ACT.Sigmoid)\
                                .then_inc(gates, 1)
                        t = tile(TURN)
                        if t:
                            b = t.slot % 2
                            act.wait_ge(turned, t.n + 1)
                            if positive((t.n - 1) * (2 if kind == 3 else 1)):
                                act.wait_ge(product, (t.n - 1) * (2 if kind == 3 else 1))
                            nc.scalar.copy(HvT[:, b, 0:G * t.rows], psV[0:96, b, 0:G * t.rows]).then_inc(v_out, 1)
                            nc.scalar.copy(HsT[:, b, 0:2 * t.rows], psS[:, b, 0:2 * t.rows]).then_inc(s_out, 1)
                    sweep(act, groups, full_groups, last_parts, STORE, step)

                @block.tensor
                def _(pe):
                    ws, wv = w(weights[0]), w(weights[1])
                    if kind == 3:
                        ws, wv = ws.rearrange("p (k c) -> p k c", k=2), wv.rearrange("p (k c) -> p k c", k=2)
                    else:
                        ws = ws.rearrange("p (q c) -> p q c", q=2)

                    def step(tile):
                        t = tile(TURN)
                        if t:
                            n, b = t.rows, t.slot
                            pe.wait_ge(norm.done, t.n + 1)
                            if positive(t.n - 1):
                                pe.wait_ge(s_out, t.n - 1)
                            if positive(t.n - 1):
                                pe.wait_ge(v_out, t.n - 1)
                            for q in range(G):
                                at = 224 * (q % 2)
                                nc.tensor.transpose(psV[0:96, b % 2, q * n:(q + 1) * n], H[0:n, b, q // 2, at:at + 96], ident[0:n, 0:n])
                            for p in range(2):
                                tr = nc.tensor.transpose(psS[:, b % 2, p * n:(p + 1) * n], H[0:n, b, p, 96:224], ident[0:n, 0:n])
                            tr.then_inc(turned, 1)
                        t = tile(MUL)
                        if t:
                            n, b = t.rows, t.slot
                            pe.wait_ge(s_out, t.n + 1)
                            pe.wait_ge(v_out, t.n + 1)
                            if kind == 3:
                                for q in range(G):
                                    if q % 2 == 0:
                                        if positive(2 * t.n + q // 2 - 1):
                                            pe.wait_ge(pair_used, 2 * t.n + q // 2 - 1)
                                    o = psO[0:n, q, 0:2 * D].rearrange("p (k c) -> p k c", k=2)
                                    half = slice(S * (q % 2), S * (q % 2) + S)
                                    nc.tensor.matmul(o[:, :, 0:S], HsT[half, b % 2, (q // 2) * n:(q // 2 + 1) * n], ws[half], start=True, stop=True)
                                    mm = nc.tensor.matmul(o[:, :, S:D], HvT[:, b % 2, q * n:(q + 1) * n], wv, start=True, stop=True)
                                    if q % 2 == 1:
                                        mm.then_inc(product, 1)
                            else:
                                if positive(t.n - 1):
                                    pe.wait_ge(summed, t.n - 1)
                                ns = 96 if kind == 1 else S
                                for p in range(2):
                                    o = psO[0:n, (b % 2) * 2 + p, 0:2 * width].rearrange("p (q c) -> p q c", q=2)
                                    nc.tensor.matmul(o[:, :, 0:ns], HsT[:, b % 2, p * n:(p + 1) * n], ws, start=True, stop=True)
                                    for q in range(2):
                                        at = (2 * p + q) * n
                                        mm = nc.tensor.matmul(o[:, q, ns:width], HvT[:, b % 2, at:at + n], wv, start=True, stop=True)
                                mm.then_inc(product, 1)
                    sweep(pe, groups, full_groups, last_parts, STORE, step)

                if kind == 0:
                    @block.gpsimd
                    def _(pool):
                        def step(tile):
                            t = tile(3)
                            if t:
                                n, b = t.rows, t.slot
                                pool.wait_ge(ix["compared"], t.n + 1)
                                if positive(t.n - 1):
                                    pool.wait_ge(ix["counted"], t.n - 1)
                                nc.gpsimd.tensor_tensor(early[0:n, b % 2, :, 0:n], eq[0:n, b, :, 0:n],
                                                        repeat(lower[0:n, 0:n], 1, 2), ALU.mult).then_inc(ix["masked"], 1)
                        sweep(pool, groups, full_groups, last_parts, STORE, step)

                if kind >= 2:
                    @block.gpsimd
                    def _(pool):
                        def step(tile):
                            t = tile(2 if kind == 2 else 1)
                            if not t:
                                return
                            n, b = t.rows, t.slot
                            if kind == 2:
                                pool.wait_ge(gates, t.n + 1)
                                g = Gt[0:n, b % 2, :, :]
                                pv = Pt[0:n, b, :, 96:192].rearrange("p g (k i) -> p g k i", i=3)
                                nc.gpsimd.tensor_tensor(Pt[0:n, b, :, 0:S], Pt[0:n, b, :, 0:S], g[:, :, 0:S], ALU.mult)
                                for q in range(G):
                                    ins = nc.gpsimd.tensor_tensor(pv[:, q], pv[:, q], repeat(g[:, q, S:96], 2, 3), ALU.mult)
                                ins.then_inc(gated, 1)
                                pool.wait_ge(gated, t.n + 1)
                                if positive(t.n - (NB - 1)):
                                    pool.wait_ge(summed, t.n - (NB - 1))
                                nc.gpsimd.tensor_tensor(X2[0:n, b, :, 0:S], Pt[0:n, b, :, 0:S], X[0:n, b, :, 0:S], ALU.add)
                                nc.gpsimd.tensor_tensor(X2[0:n, b, :, S:D], Pt[0:n, b, :, 96:192], X[0:n, b, :, S:D], ALU.add)\
                                    .then_inc(residual_ready, 1)
                            else:
                                pool.wait_ge(loaded[t.slot], (t.turn + 1) * (16 * (loads)))
                                if positive(t.n - (NB - 1)):
                                    pool.wait_ge(summed, t.n - (NB - 1))
                                nc.gpsimd.tensor_tensor(XT[0:n, b, :, :], X[0:n, b, :, :], T3[0:n, b, :, :], ALU.add)\
                                    .then_inc(residual_ready, 1)
                        sweep(pool, groups, full_groups, last_parts, STORE, step)

                @block.vector
                def _(dve):
                    def add_half(t):
                        n, b = t.rows, t.slot
                        if kind == 3:
                            dve.wait_ge(residual_ready, t.n + 1)
                            if positive(t.turn):
                                dve.wait_ge(stored[t.slot], t.turn * 16)
                            if positive(t.n - 1):
                                dve.wait_ge(summed, t.n - 1)
                            for p in range(2):
                                if positive(2 * t.n + p + 1):
                                    dve.wait_ge(product, 2 * t.n + p + 1)
                                for q in (2 * p, 2 * p + 1):
                                    ins = nc.vector.scalar_tensor_tensor(A1[0:n, b % 2, q, :], psO[0:n, q, 0:D], NA[0:n, b, q, 0:1],
                                                                         XT[0:n, b, q, :], ALU.mult, ALU.add)
                                ins.then_inc(part_a, 1)
                                if positive(2 * t.n + p + 1):
                                    dve.wait_ge(part_a, 2 * t.n + p + 1)
                                for q in (2 * p, 2 * p + 1):
                                    ins = nc.vector.scalar_tensor_tensor(Y[0:n, b, q, :], psO[0:n, q, D:2 * D], NA[0:n, b, q, 1:2],
                                                                         A1[0:n, b % 2, q, :], ALU.mult, ALU.add)
                                ins.then_inc(pair_used, 1)
                            if positive(2 * (t.n + 1)):
                                dve.wait_ge(pair_used, 2 * (t.n + 1))
                            dve.sem_inc(summed, 1)
                            return
                        dve.wait_ge(product, t.n + 1)
                        if positive(t.turn):
                            dve.wait_ge(stored[t.slot], t.turn * (16 * (4 if kind == 2 else 1)))
                        pairs = psO[0:n, (b % 2) * 2:(b % 2) * 2 + 2, 0:2 * width]
                        yv = Y[0:n, b, :, :].rearrange("p (k g) c -> p k (g c)", k=2)
                        if kind == 1:
                            ins = nc.vector.tensor_copy(yv, pairs)
                        else:
                            xv = (X if kind == 0 else X2)[0:n, b, :, :].rearrange("p (k g) c -> p k (g c)", k=2)
                            ins = nc.vector.tensor_tensor(yv, xv, pairs, ALU.add)
                        ins.then_inc(summed, 1)

                    def index_step(tile):
                        t = tile(4)
                        if t:
                            n, b = t.rows, t.slot
                            dve.wait_ge(ix["masked"], t.n + 1)
                            if positive(t.n):
                                dve.wait_ge(ix["moved"], t.n)
                            nc.vector.tensor_reduce(rep[0:n, :], early[0:n, b % 2, :, 0:n], AX_X, ALU.max)\
                                .then_inc(ix["counted"], 1)
                            nc.vector.tensor_scalar(off[0:n, :], col[0:n, b, :], -1.0, junk[0:n, :], ALU.mult, ALU.add)\
                                .then_inc(ix["offset"], 1)
                        t_ = tile(2)
                        if t_:
                            n, b = t_.rows, t_.slot
                            dve.wait_ge(index_in[t_.slot], (t_.turn + 1) * 48)
                            if positive(t_.turn):
                                dve.wait_ge(index_stored[t_.slot], t_.turn * 32)
                            if positive(t_.n - (NB - 1)):
                                dve.wait_ge(ix["masked"], t_.n - (NB - 1))
                            nc.vector.tensor_tensor(eq[0:n, b, :, 0:n], row[0:n, b, :, 0:n], repeat(col[0:n, b, :], 2, n),
                                                    ALU.is_equal).then_inc(ix["compared"], 1)
                        if t:
                            n, b = t.rows, t.slot
                            dve.wait_ge(ix["counted"], t.n + 1)
                            dve.wait_ge(ix["offset"], t.n + 1)
                            if positive(t.n):
                                dve.wait_ge(ix["ready"], t.n)
                            nc.vector.tensor_tensor(moved[0:n, :], off[0:n, :], rep[0:n, :], ALU.mult)\
                                .then_inc(ix["moved"], 1)
                            dve.wait_ge(ix["moved"], t.n + 1)
                            nc.vector.tensor_tensor(uniq[0:n, b, :], moved[0:n, :], col[0:n, b, :], ALU.add)\
                                .then_inc(ix["ready"], 1)

                    def step(tile):
                        if kind == 0:
                            index_step(tile)
                        t, tr, tm = tile(STATS), tile(STATS + 1), tile(MUL)
                        if kind == 2:
                            if t:
                                dve.wait_ge(residual_ready, t.n + 1)
                                if positive(t.n - (NB - 1)):
                                    dve.wait_ge(norm.done, t.n - (NB - 1))
                            if tr:
                                norm.widen(dve, tr)
                            for q in range(G):
                                if t:
                                    norm.partial(t, q, X2[0:t.rows, t.slot, q, :])
                                if tr:
                                    norm.newton(dve, tr, q)
                            if tm:
                                add_half(tm)
                            if t:
                                dve.wait_ge(norm.stats, t.n + 1)
                                dve.sem_inc(norm.passed, 1)
                            for q in range(G):
                                if tr:
                                    norm.newton(dve, tr, G + q)
                                if t:
                                    norm.moment(t, q)
                            if tr:
                                for at in range(2 * G, NEWTON + 1):
                                    norm.newton(dve, tr, at)
                                norm.newton_shifts(dve, tr)
                        else:
                            if t:
                                dve.wait_ge(loaded[t.slot], (t.turn + 1) * (16 * (loads)))
                                norm.statistics(dve, t, [X[0:t.rows, t.slot, q, :] for q in range(G)])
                            if tm:
                                add_half(tm)
                            if tr:
                                norm.scales(dve, tr)
                    sweep(dve, groups, full_groups, last_parts, STORE, step)

        def gather(pool, out_ap, tab, index):
            return pool.indirect_dma_start(out=out_ap, out_offset=None, in_=tab,
                                           in_offset=bass.IndirectOffsetOnAxis(ap=index, axis=0))

        def scatter_add(pool, tab, index, in_ap):
            return pool.indirect_dma_start(out=tab, out_offset=bass.IndirectOffsetOnAxis(ap=index, axis=0),
                                           in_=in_ap, in_offset=None, compute_op=ALU.add)

        SRC, DST = 0, 1

        class EdgePhase:

            def __init__(self, ph, tag, table_in, at, to, table_out, width, ea_cols, lags, gathers=1):
                self.tag, self.table_in, self.at, self.to, self.table_out = tag, table_in, at, to, table_out
                self.width, self.ea_cols, self.gathers, self.row_dmas = width, ea_cols, gathers, gathers
                self.ea_lag, self.eq_lag, self.uq_lag = lags

                def sb(name, shape, dt=F32):
                    return ph.enter_context(nc.sbuf_tensor(f"{tag}_{name}", shape, dt))
                self.index, self.uniq = sb("index", [P, NB, 2], I32), sb("uniq", [P, NB, 2], I32)
                self.X = sb("X", [P, NB, gathers, D])
                self.EA = sb("EA", [P, NB, ea_cols[1] - ea_cols[0]])
                self.EQ, self.R = sb("EQ", [P, NB, P]), sb("R", [P, NB, width])
                self.index_in, self.ea_in = ring_sems(f"{tag}_index_in"), ring_sems(f"{tag}_ea_in")
                self.eq_in, self.uniq_in = ring_sems(f"{tag}_eq_in"), ring_sems(f"{tag}_uniq_in")
                self.rows_in = ring_sems(f"{tag}_rows_in")
                self.added, self.passed = sem(f"{tag}_added"), sem(f"{tag}_pool_passed")

            def loads(self, sp, tile, index_used, ea_used, eq_used):
                t = tile(0)
                if t:
                    n, b = t.rows, t.slot
                    index_used(sp, t)
                    sp.dma_start(self.index[0:n, b, :], idx2[bass.ds(t.n * P, n), :]).then_inc(self.index_in[b], 16)
                t = tile(self.ea_lag)
                if t:
                    n, b = t.rows, t.slot
                    for read in ea_used:
                        if positive(t.n - (NB - 1)):
                            sp.wait_ge(read, t.n - (NB - 1))
                    sp.dma_start(self.EA[0:n, b, :], ea[bass.ds(t.n * P, n), self.ea_cols[0]:self.ea_cols[1]])\
                      .then_inc(self.ea_in[b], 16)
                t = tile(self.eq_lag)
                if t:
                    n, b = t.rows, t.slot
                    if positive(t.n - (NB - 1)):
                        sp.wait_ge(eq_used, t.n - (NB - 1))
                    sp.dma_start(self.EQ[0:n, b, 0:n], same[bass.ds(t.n * P, n), self.to * P:self.to * P + n])\
                      .then_inc(self.eq_in[b], 16)
                t = tile(self.uq_lag)
                if t:
                    n, b = t.rows, t.slot
                    if positive((t.n - (NB - 1)) * 16):
                        sp.wait_ge(self.added, (t.n - (NB - 1)) * 16)
                    sp.dma_start(self.uniq[0:n, b, :], unique[bass.ds(t.n * P, n), :]).then_inc(self.uniq_in[b], 16)

            def gather_rows(self, pool, t, rows_free):
                n, b = t.rows, t.slot
                pool.wait_ge(self.index_in[t.slot], (t.turn + 1) * 16)
                if positive(t.n - (NB - 1)):
                    pool.wait_ge(rows_free, t.n - (NB - 1))
                pool.sem_inc(self.passed, 1)
                for g in range(self.gathers):
                    a = self.at if self.gathers == 1 else (DST, SRC)[g]
                    gather(pool, self.X[0:n, b, g, :], self.table_in, self.index[0:n, b, a:a + 1])\
                        .then_inc(self.rows_in[b], 16)

            def add_rows(self, pool, t, result, per=1):
                n, b = t.rows, t.slot
                pool.wait_ge(self.uniq_in[t.slot], (t.turn + 1) * 16)
                pool.wait_ge(result, (t.n + 1) * per)
                if positive(t.n * 16):
                    pool.wait_ge(self.added, t.n * 16)
                pool.sem_inc(self.passed, 1)
                scatter_add(pool, self.table_out, self.uniq[0:n, b, self.to:self.to + 1], self.R[0:n, b, :])\
                    .then_inc(self.added, 16)

        def rows_used(e):
            def wait(sp, t):
                if positive(t.turn):
                    sp.wait_ge(e.rows_in[t.slot], t.turn * (16 * (e.row_dmas)))
            return wait

        def layer1_edges():
            with nc.cleanup_on_exit(), ExitStack() as ph:
                tag = "e1"
                GATHER, STATS, ROOT, SCALES, MAP, TURN, MIX, SH, SPREAD, FILTER, FOLD, Z_AT, SUM, Z_OUT, LINEAR, RESULT, ADD = \
                    1, 3, 4, 5, 6, 7, 9, 9, 10, 11, 12, 13, 14, 15, 16, 17, 18

                def sb(name, shape, dt=F32):
                    return ph.enter_context(nc.sbuf_tensor(f"{tag}_{name}", shape, dt))

                def pb(name, shape):
                    return ph.enter_context(nc.psum_tensor(f"{tag}_{name}", shape, F32))
                e = EdgePhase(ph, tag, x1, DST, SRC, p1, 192, (EA3, EAW), (TURN - 2, SUM - 2, ADD - 2))
                norm = Norm(ph, tag, 1)
                H, XT, VT, hidT = sb("H", [P, NB, D]), sb("XT", [S, NB, 2, P]), sb("VT", [96, NB, P]), sb("hidT", [64, NB, P])
                XS, XV = sb("XS", [P, NB, S]), sb("XV", [P, NB, 5, V])
                n2, root, rn = sb("n2", [P, NB]), sb("root", [P, NB]), sb("rn", [P, NB])
                rhat, sh = sb("rhat", [P, NB, 3]), sb("sh", [P, NB, 5])
                sq, w1x, Wt = sb("sq", [P, 3]), sb("w1x", [P, S]), sb("Wt", [P, NB, 224])
                ca, cb, dp = sb("ca", [P, 3, V]), sb("cb", [P, 3, V]), sb("dp", [P, 3, V])
                CR, DT = sb("CR", [P, NB, 3, V]), sb("DT", [P, NB, V])
                Z, ZT = sb("Z", [P, NB, 480]), sb("ZT", [P, NB, 4, P])
                psT, psM, psW, psZ, psO = pb("psT", [P, 2, 512]), pb("psM", [P, 2, 512]), pb("psW", [P, 512]), pb("psZ", [P, 2, 512]), pb("psO", [P, 512])
                q = {m: sem(f"{tag}_{m}") for m in (
                    "turned", "xt_out", "vt_out", "mixed", "hid_out", "xv_out", "filter", "filter_out",
                    "squared", "n2", "root", "rn", "rhat", "sh", "pool_products", "cross", "dot_products", "dot", "w1x", "z_ready",
                    "z_turned", "z_out", "linear", "result")}
                block = ph.enter_context(nc.Block())

                @block.sync
                def _(sp):
                    def step(tile):
                        e.loads(sp, tile, rows_used(e), (q["turned"], q["sh"]), q["z_turned"])
                    sweep(sp, tiles, full_tiles, last_edges, ADD, step)

                @block.gpsimd
                def _(pool):
                    def step(tile):
                        t = tile(ADD)
                        if t:
                            e.add_rows(pool, t, q["result"])
                        t = tile(GATHER)
                        if t:
                            e.gather_rows(pool, t, norm.done)
                        t = tile(FILTER)
                        if t:
                            n, b = t.rows, t.slot
                            pool.wait_ge(q["xv_out"], t.n + 1)
                            pool.wait_ge(q["sh"], t.n + 1)
                            if positive(t.n - (NB - 1)):
                                pool.wait_ge(q["z_ready"], t.n - (NB - 1))
                            if positive(t.n):
                                pool.wait_ge(q["cross"], t.n)
                            v = XV[0:n, b, :, :]
                            nc.gpsimd.tensor_tensor(ca[0:n], v[:, 1:4, :], repeat(sh[0:n, b, 2:5], 2, V), ALU.mult)
                            nc.gpsimd.tensor_tensor(cb[0:n], v[:, 2:5, :], repeat(sh[0:n, b, 1:4], 2, V), ALU.mult)\
                                .then_inc(q["pool_products"], 1)
                            pool.wait_ge(q["pool_products"], t.n + 1)
                            nc.gpsimd.tensor_tensor(CR[0:n, b], ca[0:n], cb[0:n], ALU.subtract).then_inc(q["cross"], 1)
                    sweep(pool, tiles, full_tiles, last_edges, ADD, step)
                    pool.wait_ge(e.added, 16 * tiles)

                @block.scalar
                def _(act):
                    def step(tile):
                        t = tile(RESULT)
                        if t:
                            n, b = t.rows, t.slot
                            act.wait_ge(q["linear"], t.n + 1)
                            if positive((t.n - (NB - 1)) * 16):
                                act.wait_ge(e.added, (t.n - (NB - 1)) * 16)
                            nc.scalar.copy(e.R[0:n, b, :], psO[0:n, 0:192]).then_inc(q["result"], 1)
                        t = tile(FOLD)
                        if t:
                            n, b = t.rows, t.slot
                            act.wait_ge(q["filter"], t.n + 1)
                            if positive(t.n - (NB - 1)):
                                act.wait_ge(q["z_ready"], t.n - (NB - 1))
                            nc.scalar.copy(Wt[0:n, b, :], psW[0:n, 0:224]).then_inc(q["filter_out"], 1)
                        t = tile(Z_OUT)
                        if t:
                            n, b = t.rows, t.slot
                            act.wait_ge(q["z_turned"], t.n + 1)
                            if positive(t.n - (NB - 1)):
                                act.wait_ge(q["linear"], t.n - (NB - 1))
                            nc.scalar.copy(ZT[0:P, b, 1:4, 0:n], psZ[:, b % 2, P:512].rearrange("p (c q) -> p c q", c=3)[:, :, 0:n])
                            nc.scalar.copy(ZT[0:96, b, 0, 0:n], psZ[0:96, b % 2, 0:n]).then_inc(q["z_out"], 1)
                        t = tile(SPREAD)
                        if t:
                            n, b = t.rows, t.slot
                            act.wait_ge(q["mixed"], t.n + 1)
                            if positive(t.n - (NB - 1)):
                                act.wait_ge(q["filter"], t.n - (NB - 1))
                            nc.scalar.activation(hidT[:, b, 0:n], psM[0:64, b % 2, D:D + n], ACT.Relu).then_inc(q["hid_out"], 1)
                            if positive(t.n - (NB - 1)):
                                act.wait_ge(q["z_ready"], t.n - (NB - 1))
                            nc.scalar.copy(XS[0:n, b, :], psM[0:n, b % 2, 0:S])
                            v = psM[0:n, b % 2, S:D].rearrange("p (i u) -> p i u", i=3)
                            nc.scalar.copy(XV[0:n, b, 0:3, :], v)
                            nc.scalar.copy(XV[0:n, b, 3:5, :], v[:, 0:2, :]).then_inc(q["xv_out"], 1)
                        t = tile(TURN + 1)
                        if t:
                            n, b = t.rows, t.slot
                            act.wait_ge(q["n2"], t.n + 1)
                            nc.scalar.activation(root[0:n, b:b + 1], n2[0:n, b:b + 1], ACT.Sqrt).then_inc(q["root"], 1)
                        t = tile(MAP)
                        if t:
                            n, b = t.rows, t.slot
                            act.wait_ge(norm.ready, t.n + 1)
                            if positive(t.n - (NB - 1)):
                                act.wait_ge(q["turned"], t.n - (NB - 1))
                            norm.map(t, H[0:n, b, :], e.X[0:n, b, 0, :], 0).then_inc(norm.done, 1)
                        t = tile(ROOT)
                        if t:
                            norm.root(act, t)
                    sweep(act, tiles, full_tiles, last_edges, ADD, step)

                @block.tensor
                def _(pe):
                    def step(tile):
                        t = tile(SUM)
                        if t:
                            n, b = t.rows, t.slot
                            pe.wait_ge(q["z_ready"], t.n + 1)
                            pe.wait_ge(e.eq_in[t.slot], (t.turn + 1) * 16)
                            if positive(t.n - 1):
                                pe.wait_ge(q["z_out"], t.n - 1)
                            nc.tensor.matmul(psZ[0:96, b % 2, 0:n], Z[0:n, b, 0:96], e.EQ[0:n, b, 0:n], start=True, stop=True)
                            for i in range(3):
                                mm = nc.tensor.matmul(psZ[:, b % 2, P * (i + 1):P * (i + 1) + n], Z[0:n, b, 96 + P * i:96 + P * (i + 1)],
                                                      e.EQ[0:n, b, 0:n], start=True, stop=True)
                            mm.then_inc(q["z_turned"], 1)
                        t = tile(TURN)
                        if t:
                            n, b = t.rows, t.slot
                            pe.wait_ge(norm.done, t.n + 1)
                            pe.wait_ge(e.ea_in[t.slot], (t.turn + 1) * 16)
                            if positive(t.n - 1):
                                pe.wait_ge(q["xt_out"], t.n - 1)
                            if positive(t.n - 1):
                                pe.wait_ge(q["vt_out"], t.n - 1)
                            nc.tensor.transpose(psT[0:96, b % 2, 2 * P:2 * P + n], H[0:n, b, S:D], ident[0:n, 0:n])
                            nc.tensor.transpose(psT[0:S, b % 2, 0:n], H[0:n, b, 0:S], ident[0:n, 0:n])
                            nc.tensor.transpose(psT[0:S, b % 2, P:P + n], e.EA[0:n, b, 3:67], ident[0:n, 0:n])\
                                .then_inc(q["turned"], 1)
                        t = tile(MIX)
                        if t:
                            n, b = t.rows, t.slot
                            pe.wait_ge(q["xt_out"], t.n + 1)
                            pe.wait_ge(q["vt_out"], t.n + 1)
                            if positive(t.n - 1):
                                pe.wait_ge(q["xv_out"], t.n - 1)
                            nc.tensor.matmul(psM[0:n, b % 2, 0:S], XT[0:S, b, 0, 0:n], w("nl_s"), start=True, stop=True)
                            nc.tensor.matmul(psM[0:n, b % 2, S:D], VT[0:96, b, 0:n], w("nl_v"), start=True, stop=True)
                            nc.tensor.matmul(psM[0:64, b % 2, D:D + n], w("fc1"), XT[0:64, b, 1, 0:n], start=True, stop=True)\
                                .then_inc(q["mixed"], 1)
                        t = tile(FILTER)
                        if t:
                            n, b = t.rows, t.slot
                            pe.wait_ge(q["hid_out"], t.n + 1)
                            if positive(t.n):
                                pe.wait_ge(q["filter_out"], t.n)
                            nc.tensor.matmul(psW[0:n, 0:224], hidT[:, b, 0:n], w("fc2"), start=True, stop=True)\
                                .then_inc(q["filter"], 1)
                        t = tile(LINEAR)
                        if t:
                            n, b = t.rows, t.slot
                            pe.wait_ge(q["z_out"], t.n + 1)
                            if positive(t.n):
                                pe.wait_ge(q["result"], t.n)
                            nc.tensor.matmul(psO[0:n, 0:96], ZT[0:96, b, 0, 0:n], w("out_s"), start=True, stop=True)
                            for i in range(3):
                                mm = nc.tensor.matmul(psO[0:n, 96 + i:192:3], ZT[:, b, 1 + i, 0:n], w("out_v"), start=True, stop=True)
                            mm.then_inc(q["linear"], 1)
                    sweep(pe, tiles, full_tiles, last_edges, ADD, step)

                @block.vector
                def _(dve):
                    def step(tile):
                        t = tile(Z_AT)
                        if t:
                            n, b = t.rows, t.slot
                            dve.wait_ge(q["xv_out"], t.n + 1)
                            dve.wait_ge(q["filter_out"], t.n + 1)
                            if positive(t.n - (NB - 1)):
                                dve.wait_ge(q["z_turned"], t.n - (NB - 1))
                            z, wt = Z[0:n, b, :], Wt[0:n, b, :]
                            zv = z[:, 96:480].rearrange("p (i c) -> p i c", i=3)
                            if positive(t.n):
                                dve.wait_ge(q["z_ready"], t.n)
                            nc.vector.tensor_tensor(w1x[0:n], wt[:, 64:128], XS[0:n, b, :], ALU.mult).then_inc(q["w1x"], 1)
                            nc.vector.tensor_tensor(z[:, 0:S], wt[:, 0:64], XS[0:n, b, :], ALU.mult)
                            nc.vector.tensor_tensor(zv[:, :, S:96], XV[0:n, b, 0:3, :], repeat(wt[:, 128:160], 1, 3), ALU.mult)
                            dve.wait_ge(q["w1x"], t.n + 1)
                            dve.wait_ge(q["sh"], t.n + 1)
                            nc.vector.tensor_tensor(zv[:, :, 0:S], repeat(w1x[0:n], 1, 3), repeat(sh[0:n, b, 0:3], 2, S), ALU.mult)
                            dve.wait_ge(q["cross"], t.n + 1)
                            nc.vector.tensor_tensor(zv[:, :, 96:P], CR[0:n, b], repeat(wt[:, 192:224], 1, 3), ALU.mult)
                            dve.wait_ge(q["dot"], t.n + 1)
                            nc.vector.tensor_tensor(z[:, S:96], DT[0:n, b], wt[:, 160:192], ALU.mult).then_inc(q["z_ready"], 1)
                        t = tile(TURN + 1)
                        if t:
                            n, b = t.rows, t.slot
                            dve.wait_ge(q["turned"], t.n + 1)
                            if positive(t.n - (NB - 1)):
                                dve.wait_ge(q["mixed"], t.n - (NB - 1))
                            nc.vector.tensor_copy(XT[0:S, b, :, 0:n], psT[0:S, b % 2, 0:2 * P].rearrange("p (c q) -> p c q", c=2)[:, :, 0:n])\
                                .then_inc(q["xt_out"], 1)
                            nc.vector.tensor_copy(VT[:, b, 0:n], psT[0:96, b % 2, 2 * P:2 * P + n]).then_inc(q["vt_out"], 1)
                        tr, ts, tf = tile(SH), tile(TURN), tile(FILTER)
                        if tf:
                            n, b = tf.rows, tf.slot
                            dve.wait_ge(q["xv_out"], tf.n + 1)
                            dve.wait_ge(q["sh"], tf.n + 1)
                            if positive(tf.n):
                                dve.wait_ge(q["dot"], tf.n)
                            nc.vector.tensor_tensor(dp[0:n], XV[0:n, b, 0:3, :], repeat(rhat[0:n, b, :], 2, V), ALU.mult)\
                                .then_inc(q["dot_products"], 1)
                        if tr:
                            n, b = tr.rows, tr.slot
                            dve.wait_ge(q["root"], tr.n + 1)
                            nc.vector.reciprocal(rn[0:n, b:b + 1], root[0:n, b:b + 1]).then_inc(q["rn"], 1)
                        if ts:
                            n, b = ts.rows, ts.slot
                            dve.wait_ge(e.ea_in[ts.slot], (ts.turn + 1) * 16)
                            if positive(ts.n):
                                dve.wait_ge(q["n2"], ts.n)
                            if positive(ts.n - (NB - 1)):
                                dve.wait_ge(q["root"], ts.n - (NB - 1))
                            nc.vector.tensor_tensor(sq[0:n], e.EA[0:n, b, 0:3], e.EA[0:n, b, 0:3], ALU.mult).then_inc(q["squared"], 1)
                        if tf:
                            n, b = tf.rows, tf.slot
                            dve.wait_ge(q["dot_products"], tf.n + 1)
                            if positive(tf.n - (NB - 1)):
                                dve.wait_ge(q["z_ready"], tf.n - (NB - 1))
                            nc.vector.tensor_reduce(DT[0:n, b], dp[0:n].rearrange("p i u -> p u i"), AX_X, ALU.add).then_inc(q["dot"], 1)
                        if tr:
                            n, b = tr.rows, tr.slot
                            a = e.EA[0:n, b, 0:3]
                            dve.wait_ge(q["rn"], tr.n + 1)
                            if positive(tr.n - (NB - 1)):
                                dve.wait_ge(q["dot"], tr.n - (NB - 1))
                            if positive(tr.n - (NB - 1)):
                                dve.wait_ge(q["cross"], tr.n - (NB - 1))
                            nc.vector.tensor_scalar(rhat[0:n, b, :], a, rn[0:n, b:b + 1], None, ALU.mult).then_inc(q["rhat"], 1)
                            nc.vector.tensor_scalar(sh[0:n, b, 0:3], a, rn[0:n, b:b + 1], 3.0 ** 0.5, ALU.mult, ALU.mult)
                            nc.vector.tensor_scalar(sh[0:n, b, 3:5], a[:, 0:2], rn[0:n, b:b + 1], 3.0 ** 0.5, ALU.mult, ALU.mult)\
                                .then_inc(q["sh"], 1)
                        if ts:
                            n, b = ts.rows, ts.slot
                            dve.wait_ge(q["squared"], ts.n + 1)
                            nc.vector.tensor_reduce(n2[0:n, b:b + 1], sq[0:n], AX_X, ALU.add).then_inc(q["n2"], 1)
                        t = tile(STATS)
                        if t:
                            n, b = t.rows, t.slot
                            dve.wait_ge(e.rows_in[t.slot], (t.turn + 1) * 16)
                            norm.statistics(dve, t, [e.X[0:n, b, 0, :]])
                        t = tile(SCALES)
                        if t:
                            norm.scales(dve, t)
                    sweep(dve, tiles, full_tiles, last_edges, ADD, step)

        def layer2_edges():
            with nc.cleanup_on_exit(), ExitStack() as ph:
                tag = "e2"
                GATHER, Z_AT, TURN, Z_OUT, MESSAGE, GATE, M_AT, SUM, M_OUT, LINEAR, RESULT, ADD = 1, 3, 4, 5, 6, 7, 8, 9, 10, 11, 12, 13

                def sb(name, shape, dt=F32):
                    return ph.enter_context(nc.sbuf_tensor(f"{tag}_{name}", shape, dt))

                def pb(name, shape):
                    return ph.enter_context(nc.psum_tensor(f"{tag}_{name}", shape, F32))
                e = EdgePhase(ph, tag, h2, SRC, DST, x3, D, (EA4, EA16), (1, SUM - 2, ADD - 2))
                VE, VD = sb("VE", [P, 3, V]), sb("VD", [P, V])
                Z0, Z, Z0T, ZT = sb("Z0", [P, NB, 113]), sb("Z", [P, NB, 3, 96]), sb("Z0T", [113, NB, P]), sb("ZT", [96, NB, 3, P])
                radial_in = ring_sems(f"{tag}_radial_in")
                gate, M = sb("gate", [P, NB, D]), sb("M", [P, NB, D])
                MsT, MvT = sb("MsT", [S, NB, P]), sb("MvT", [96, NB, P])
                psZ, psM = pb("psZ", [P, 2, 512]), pb("psM", [P, 2, 512])
                psA, psO = pb("psA", [P, 2, 512]), pb("psO", [P, 512])
                q = {m: sem(f"{tag}_{m}") for m in (
                    "ones", "ve", "ve1", "z_pool", "z_ready", "turned", "zt_out", "message",
                    "gate", "m_ready", "m_turned", "ms_out", "mv_out", "linear", "result")}
                block = ph.enter_context(nc.Block())

                @block.sync
                def _(sp):
                    def step(tile):
                        t = tile(1)
                        if t:
                            n, b = t.rows, t.slot
                            if isinstance(t.n, int) and t.n == 0:
                                sp.wait_ge(q["ones"], 1)
                            if positive(t.n - (NB - 1)):
                                sp.wait_ge(q["turned"], t.n - (NB - 1))
                            sp.dma_start(Z0[0:n, b, 96:112], ea[bass.ds(t.n * P, n), EA16:EA3]).then_inc(radial_in[b], 16)
                        e.loads(sp, tile, rows_used(e), (q["z_ready"], q["z_pool"]), q["m_turned"])
                    sweep(sp, tiles, full_tiles, last_edges, ADD, step)

                @block.gpsimd
                def _(pool):
                    nc.gpsimd.memset(Z0[:, :, :], 1.0).then_inc(q["ones"], 1)

                    def step(tile):
                        t = tile(ADD)
                        if t:
                            e.add_rows(pool, t, q["result"])
                        t = tile(GATHER)
                        if t:
                            e.gather_rows(pool, t, q["z_ready"])
                        t = tile(Z_AT)
                        if t:
                            n, b = t.rows, t.slot
                            pool.wait_ge(e.rows_in[t.slot], (t.turn + 1) * 16)
                            pool.wait_ge(e.ea_in[t.slot], (t.turn + 1) * 16)
                            if positive(t.n - (NB - 1)):
                                pool.wait_ge(q["turned"], t.n - (NB - 1))
                            if positive(t.n):
                                pool.wait_ge(q["z_pool"], t.n)
                            xv = e.X[0:n, b, 0, S:D].rearrange("p (u i) -> p i u", i=3)
                            ev = e.EA[0:n, b, 1:4]
                            nc.gpsimd.tensor_tensor(VE[0:n], xv, repeat(ev, 2, V), ALU.mult).then_inc(q["ve"], 1)
                            pool.wait_ge(q["ve"], t.n + 1)
                            nc.gpsimd.tensor_tensor(VD[0:n], VE[0:n, 0], VE[0:n, 1], ALU.add).then_inc(q["ve1"], 1)
                            pool.wait_ge(q["ve1"], t.n + 1)
                            nc.gpsimd.tensor_tensor(Z0[0:n, b, S:96], VD[0:n], VE[0:n, 2], ALU.add).then_inc(q["z_pool"], 1)
                    sweep(pool, tiles, full_tiles, last_edges, ADD, step)
                    pool.wait_ge(e.added, 16 * tiles)

                @block.vector
                def _(dve):
                    dve.wait_ge(q["ones"], 1)

                    def step(tile):
                        t = tile(M_AT)
                        if t:
                            n, b = t.rows, t.slot
                            dve.wait_ge(q["message"], t.n + 1)
                            dve.wait_ge(q["gate"], t.n + 1)
                            if positive(t.n - (NB - 1)):
                                dve.wait_ge(q["m_turned"], t.n - (NB - 1))
                            nc.vector.tensor_tensor(M[0:n, b, :], psM[0:n, b % 2, 0:D], gate[0:n, b, :], ALU.mult)\
                                .then_inc(q["m_ready"], 1)
                        t = tile(M_OUT)
                        if t:
                            n, b = t.rows, t.slot
                            dve.wait_ge(q["m_turned"], t.n + 1)
                            if positive(t.n - (NB - 1)):
                                dve.wait_ge(q["linear"], t.n - (NB - 1))
                            nc.vector.tensor_copy(MsT[:, b, 0:n], psA[0:S, b % 2, 0:n]).then_inc(q["ms_out"], 1)
                            nc.vector.tensor_copy(MvT[:, b, 0:n], psA[0:96, b % 2, P:P + n]).then_inc(q["mv_out"], 1)
                        t = tile(Z_AT)
                        if t:
                            n, b = t.rows, t.slot
                            dve.wait_ge(e.rows_in[t.slot], (t.turn + 1) * 16)
                            dve.wait_ge(e.ea_in[t.slot], (t.turn + 1) * 16)
                            if positive(t.n - (NB - 1)):
                                dve.wait_ge(q["turned"], t.n - (NB - 1))
                            xs = e.X[0:n, b, 0, 0:S]
                            xv = e.X[0:n, b, 0, S:D].rearrange("p (u i) -> p i u", i=3)
                            es, ev = e.EA[0:n, b, 0:1], e.EA[0:n, b, 1:4]
                            nc.vector.tensor_scalar(Z0[0:n, b, 0:S], xs, es, None, ALU.mult)
                            nc.vector.tensor_scalar(Z[0:n, b, :, S:96], xv, es, None, ALU.mult)
                            nc.vector.tensor_tensor(Z[0:n, b, :, 0:S], repeat(xs, 1, 3), repeat(ev, 2, S), ALU.mult)\
                                .then_inc(q["z_ready"], 1)
                    sweep(dve, tiles, full_tiles, last_edges, ADD, step)

                @block.scalar
                def _(act):
                    def step(tile):
                        t = tile(RESULT)
                        if t:
                            n, b = t.rows, t.slot
                            act.wait_ge(q["linear"], t.n + 1)
                            if positive((t.n - (NB - 1)) * 16):
                                act.wait_ge(e.added, (t.n - (NB - 1)) * 16)
                            nc.scalar.copy(e.R[0:n, b, :], psO[0:n, 0:D]).then_inc(q["result"], 1)
                        t = tile(Z_OUT)
                        if t:
                            n, b = t.rows, t.slot
                            act.wait_ge(q["turned"], t.n + 1)
                            if positive(t.n - (NB - 1)):
                                act.wait_ge(q["message"], t.n - (NB - 1))
                            nc.scalar.copy(Z0T[:, b, 0:n], psZ[0:113, b % 2, 0:n])
                            nc.scalar.copy(ZT[:, b, :, 0:n], psZ[0:96, b % 2, P:512].rearrange("p (c q) -> p c q", c=3)[:, :, 0:n])\
                                .then_inc(q["zt_out"], 1)
                        t = tile(GATE)
                        if t:
                            n, b = t.rows, t.slot
                            act.wait_ge(q["message"], t.n + 1)
                            if positive(t.n - (NB - 1)):
                                act.wait_ge(q["m_ready"], t.n - (NB - 1))
                            nc.scalar.activation(gate[0:n, b, :], psM[0:n, b % 2, D:2 * D], ACT.Sigmoid).then_inc(q["gate"], 1)
                    sweep(act, tiles, full_tiles, last_edges, ADD, step)

                @block.tensor
                def _(pe):
                    def step(tile):
                        t = tile(SUM)
                        if t:
                            n, b = t.rows, t.slot
                            pe.wait_ge(q["m_ready"], t.n + 1)
                            pe.wait_ge(e.eq_in[t.slot], (t.turn + 1) * 16)
                            if positive(t.n - 1):
                                pe.wait_ge(q["ms_out"], t.n - 1)
                            if positive(t.n - 1):
                                pe.wait_ge(q["mv_out"], t.n - 1)
                            nc.tensor.matmul(psA[0:S, b % 2, 0:n], M[0:n, b, 96:D], e.EQ[0:n, b, 0:n], start=True, stop=True)
                            nc.tensor.matmul(psA[0:96, b % 2, P:P + n], M[0:n, b, 0:96], e.EQ[0:n, b, 0:n], start=True, stop=True)\
                                .then_inc(q["m_turned"], 1)
                        t = tile(TURN)
                        if t:
                            n, b = t.rows, t.slot
                            pe.wait_ge(q["z_ready"], t.n + 1)
                            pe.wait_ge(q["z_pool"], t.n + 1)
                            if positive(t.n - 1):
                                pe.wait_ge(q["zt_out"], t.n - 1)
                            pe.wait_ge(radial_in[t.slot], (t.turn + 1) * 16)
                            nc.tensor.transpose(psZ[0:113, b % 2, 0:n], Z0[0:n, b, :], ident[0:n, 0:n])
                            for i in range(3):
                                tr = nc.tensor.transpose(psZ[0:96, b % 2, P * (i + 1):P * (i + 1) + n], Z[0:n, b, i, :], ident[0:n, 0:n])
                            tr.then_inc(q["turned"], 1)
                        t = tile(MESSAGE)
                        if t:
                            n, b = t.rows, t.slot
                            pe.wait_ge(q["zt_out"], t.n + 1)
                            if positive(t.n - 1):
                                pe.wait_ge(q["m_ready"], t.n - 1)
                            nc.tensor.matmul(psM[0:n, b % 2, 96:2 * D], Z0T[:, b, 0:n], w("l2_s_rad"), start=True, stop=True)
                            for i in range(3):
                                mm = nc.tensor.matmul(psM[0:n, b % 2, i:96:3], ZT[:, b, i, 0:n], w("l2_v"), start=True, stop=True)
                            mm.then_inc(q["message"], 1)
                        t = tile(LINEAR)
                        if t:
                            n, b = t.rows, t.slot
                            pe.wait_ge(q["ms_out"], t.n + 1)
                            pe.wait_ge(q["mv_out"], t.n + 1)
                            if positive(t.n):
                                pe.wait_ge(q["result"], t.n)
                            nc.tensor.matmul(psO[0:n, 0:S], MsT[:, b, 0:n], w("l2l_s")[0:S, 0:S], start=True, stop=True)
                            nc.tensor.matmul(psO[0:n, S:D], MvT[:, b, 0:n], w("l2l_v"), start=True, stop=True).then_inc(q["linear"], 1)
                    sweep(pe, tiles, full_tiles, last_edges, ADD, step)

        def layer3_edges():
            with nc.cleanup_on_exit(), ExitStack() as ph:
                tag = "e3"
                GATHER, STATS, MAP, TURN, T_OUT, MIX, MIX_OUT, HID_OUT, FILTER, F_OUT, Z_AT, SUM, Z_OUT, LINEAR, RESULT, ADD = \
                    1, 3, 4, 5, 6, 7, 8, 9, 10, 11, 12, 13, 14, 15, 16, 17

                def sb(name, shape, dt=F32):
                    return ph.enter_context(nc.sbuf_tensor(f"{tag}_{name}", shape, dt))

                def pb(name, shape):
                    return ph.enter_context(nc.psum_tensor(f"{tag}_{name}", shape, F32))
                e = EdgePhase(ph, tag, x3, SRC, DST, t3, D, (EA4, EA16), (FILTER - 2, SUM - 2, ADD - 5))
                norm = Norm(ph, tag, 1)
                NA, ND, AM = sb("NA", [P, NB, 3]), sb("ND", [P, NB, 3]), sb("AM", [P, NB, 2])
                EL = sb("EL", [P, NB, 10])
                na_in, nd_in, el_in = ring_sems(f"{tag}_na_in"), ring_sems(f"{tag}_nd_in"), ring_sems(f"{tag}_el_in")
                H, HT, VT, LT = sb("H", [P, NB, D]), sb("HT", [S, NB, P]), sb("VT", [96, NB, P]), sb("LT", [10, NB, P])
                sg, hidT, A1, XM, Wt = sb("sg", [100, 2, P]), sb("hidT", [100, NB, P]), sb("A1", [P, 2, D]), sb("XM", [P, NB, D]), sb("Wt", [P, NB, 192])
                w1x, VE, DT, W2 = sb("w1x", [P, S]), sb("VE", [P, 3, V]), sb("DT", [P, NB, V]), sb("W2", [P, V])
                Z, ZT, TA = sb("Z", [P, NB, 4, 96]), sb("ZT", [96, NB, 4, P]), sb("TA", [P, D])
                psT, psL, psM, psW = pb("psT", [P, 512]), pb("psL", [P, 2, 512]), pb("psM", [P, 512]), pb("psW", [P, 512])
                psZ, psO = pb("psZ", [P, 2, 512]), pb("psO", [P, 512])
                q = {m: sem(f"{tag}_{m}") for m in (
                    "turned", "t_out", "hidden", "sig", "hid_out", "mixed", "part_a", "mix_out", "filter",
                    "filter_out", "ve", "dot", "w1x", "w2e", "z_ready", "z_turned", "z_out", "linear", "am", "part_r", "result")}
                block = ph.enter_context(nc.Block())

                @block.sync
                def _(sp):
                    def index_used(sp, t):
                        if positive(t.turn):
                            sp.wait_ge(e.rows_in[t.slot], t.turn * 16)
                        if positive(t.turn):
                            sp.wait_ge(na_in[t.slot], t.turn * 16)

                    def step(tile):
                        e.loads(sp, tile, index_used, (q["z_ready"], q["dot"]), q["z_turned"])
                        t = tile(TURN - 2)
                        if t:
                            n, b = t.rows, t.slot
                            if positive(t.n - (NB - 1)):
                                sp.wait_ge(q["turned"], t.n - (NB - 1))
                            sp.dma_start(EL[0:n, b, :], ea[bass.ds(t.n * P, n), EA10:EA4]).then_inc(el_in[b], 16)
                    sweep(sp, tiles, full_tiles, last_edges, ADD, step)

                @block.gpsimd
                def _(pool):
                    def step(tile):
                        t = tile(ADD)
                        if t:
                            e.add_rows(pool, t, q["result"])
                        t = tile(GATHER)
                        if t:
                            e.gather_rows(pool, t, norm.done)
                        t = tile(STATS)
                        if t:
                            n, b = t.rows, t.slot
                            if positive(t.n - (NB - 1)):
                                pool.wait_ge(q["mix_out"], t.n - (NB - 1))
                            pool.sem_inc(e.passed, 1)
                            gather(pool, NA[0:n, b, :], nattr, e.index[0:n, b, SRC:SRC + 1]).then_inc(na_in[b], 16)
                        t = tile(Z_OUT)
                        if t:
                            n, b = t.rows, t.slot
                            pool.wait_ge(e.uniq_in[t.slot], (t.turn + 1) * 16)
                            if positive(t.n - (NB - 1)):
                                pool.wait_ge(q["am"], t.n - (NB - 1))
                            pool.sem_inc(e.passed, 1)
                            gather(pool, ND[0:n, b, :], nattr, e.uniq[0:n, b, DST:DST + 1]).then_inc(nd_in[b], 16)
                    sweep(pool, tiles, full_tiles, last_edges, ADD, step)
                    pool.wait_ge(e.added, 16 * tiles)

                @block.vector
                def _(dve):
                    def root_steps(t, *steps):
                        if t:
                            for at in steps:
                                norm.newton(dve, t, at)

                    def step(tile):
                        tn, tr, tx, th, tf, tz = tile(STATS), tile(RESULT), tile(MIX_OUT), tile(HID_OUT), tile(FILTER), tile(Z_AT)
                        if tn:
                            dve.wait_ge(e.rows_in[tn.slot], (tn.turn + 1) * 16)
                            norm.statistics(dve, tn, [e.X[0:tn.rows, tn.slot, 0, :]])
                        if tr:
                            n, b = tr.rows, tr.slot
                            dve.wait_ge(nd_in[tr.slot], (tr.turn + 1) * 16)
                            if positive(tr.n - (NB - 1)):
                                dve.wait_ge(q["result"], tr.n - (NB - 1))
                            nc.vector.tensor_scalar(AM[0:n, b, :], ND[0:n, b, 0:2], ND[0:n, b, 2:3], None, ALU.mult)\
                                .then_inc(q["am"], 1)
                        if tf:
                            n, b = tf.rows, tf.slot
                            dve.wait_ge(e.ea_in[tf.slot], (tf.turn + 1) * 16)
                            dve.wait_ge(q["mix_out"], tf.n + 1)
                            if positive(tf.n):
                                dve.wait_ge(q["dot"], tf.n)
                            nc.vector.tensor_tensor(VE[0:n], XM[0:n, b, S:D].rearrange("p (i u) -> p i u", i=3),
                                                    repeat(e.EA[0:n, b, 1:4], 2, V), ALU.mult).then_inc(q["ve"], 1)
                        if tn:
                            norm.widen(dve, tn)
                        root_steps(tn, 0)
                        if tf:
                            n, b = tf.rows, tf.slot
                            dve.wait_ge(q["ve"], tf.n + 1)
                            if positive(tf.n - (NB - 1)):
                                dve.wait_ge(q["z_ready"], tf.n - (NB - 1))
                            nc.vector.tensor_reduce(DT[0:n, b], VE[0:n].rearrange("p i u -> p u i"), AX_X, ALU.add).then_inc(q["dot"], 1)
                        if tx:
                            n, b = tx.rows, tx.slot
                            dve.wait_ge(na_in[tx.slot], (tx.turn + 1) * 16)
                            dve.wait_ge(q["part_a"], tx.n + 1)
                            if positive(tx.n - (NB - 1)):
                                dve.wait_ge(q["z_ready"], tx.n - (NB - 1))
                            if positive(tx.n - (NB - 1)):
                                dve.wait_ge(q["dot"], tx.n - (NB - 1))
                            nc.vector.scalar_tensor_tensor(XM[0:n, b, :], psM[0:n, D:2 * D], NA[0:n, b, 1:2], A1[0:n, b % 2, :],
                                                           ALU.mult, ALU.add).then_inc(q["mix_out"], 1)
                        root_steps(tn, 1)
                        if th:
                            n, b = th.rows, th.slot
                            dve.wait_ge(q["sig"], th.n + 1)
                            if positive(th.n - (NB - 1)):
                                dve.wait_ge(q["filter"], th.n - (NB - 1))
                            nc.vector.tensor_tensor(hidT[:, b, 0:n], psL[0:100, b % 2, 0:n], sg[:, b % 2, 0:n], ALU.mult).then_inc(q["hid_out"], 1)
                        root_steps(tn, 2)
                        if tz:
                            n, b = tz.rows, tz.slot
                            dve.wait_ge(e.ea_in[tz.slot], (tz.turn + 1) * 16)
                            dve.wait_ge(q["filter_out"], tz.n + 1)
                            dve.wait_ge(q["mix_out"], tz.n + 1)
                            if positive(tz.n - (NB - 1)):
                                dve.wait_ge(q["z_turned"], tz.n - (NB - 1))
                            if positive(tz.n):
                                dve.wait_ge(q["z_ready"], tz.n)
                            z, wt, xs = Z[0:n, b, :, :], Wt[0:n, b, :], XM[0:n, b, 0:S]
                            xv = XM[0:n, b, S:D].rearrange("p (i u) -> p i u", i=3)
                            es, ev = e.EA[0:n, b, 0:1], e.EA[0:n, b, 1:4]
                            nc.vector.tensor_tensor(w1x[0:n], wt[:, 64:128], xs, ALU.mult).then_inc(q["w1x"], 1)
                        root_steps(tn, 3)
                        if tz:
                            nc.vector.tensor_scalar(W2[0:n], wt[:, 128:160], es, None, ALU.mult).then_inc(q["w2e"], 1)
                        root_steps(tn, 4)
                        if tz:
                            dve.wait_ge(q["w1x"], tz.n + 1)
                            nc.vector.tensor_tensor(z[:, 1:4, 0:S], repeat(w1x[0:n], 1, 3), repeat(ev, 2, S), ALU.mult)
                        root_steps(tn, 5)
                        if tz:
                            dve.wait_ge(q["w2e"], tz.n + 1)
                            nc.vector.tensor_tensor(z[:, 1:4, S:96], xv, repeat(W2[0:n], 1, 3), ALU.mult)
                        root_steps(tn, 6)
                        if tz:
                            nc.vector.scalar_tensor_tensor(z[:, 0, 0:S], wt[:, 0:64], es, xs, ALU.mult, ALU.mult)
                        root_steps(tn, 7)
                        if tz:
                            dve.wait_ge(q["dot"], tz.n + 1)
                            nc.vector.tensor_tensor(z[:, 0, S:96], DT[0:n, b], wt[:, 160:192], ALU.mult).then_inc(q["z_ready"], 1)
                        root_steps(tn, 8)
                        if tr:
                            n, b = tr.rows, tr.slot
                            dve.wait_ge(q["linear"], tr.n + 1)
                            dve.wait_ge(q["am"], tr.n + 1)
                            if positive((tr.n - (NB - 1)) * 16):
                                dve.wait_ge(e.added, (tr.n - (NB - 1)) * 16)
                            if positive(tr.n):
                                dve.wait_ge(q["result"], tr.n)
                            nc.vector.tensor_scalar(TA[0:n], psO[0:n, 0:D], AM[0:n, b, 0:1], None, ALU.mult).then_inc(q["part_r"], 1)
                        root_steps(tn, 9)
                        if tr:
                            dve.wait_ge(q["part_r"], tr.n + 1)
                            nc.vector.scalar_tensor_tensor(e.R[0:n, b, :], psO[0:n, D:2 * D], AM[0:n, b, 1:2], TA[0:n],
                                                           ALU.mult, ALU.add).then_inc(q["result"], 1)
                        root_steps(tn, 10)
                        if tn:
                            norm.newton_shifts(dve, tn)
                    sweep(dve, tiles, full_tiles, last_edges, ADD, step)

                @block.scalar
                def _(act):
                    def step(tile):
                        t = tile(MIX_OUT)
                        if t:
                            n, b = t.rows, t.slot
                            act.wait_ge(na_in[t.slot], (t.turn + 1) * 16)
                            act.wait_ge(q["mixed"], t.n + 1)
                            if positive(t.n - 1):
                                act.wait_ge(q["mix_out"], t.n - 1)
                            nc.scalar.activation(A1[0:n, b % 2, :], psM[0:n, 0:D], ACT.Copy, scale=NA[0:n, b, 0:1]).then_inc(q["part_a"], 1)
                        t = tile(T_OUT)
                        if t:
                            n, b = t.rows, t.slot
                            act.wait_ge(q["turned"], t.n + 1)
                            if positive(t.n - (NB - 1)):
                                act.wait_ge(q["mixed"], t.n - (NB - 1))
                            nc.scalar.copy(VT[:, b, 0:n], psT[0:96, P:P + n])
                            nc.scalar.copy(HT[:, b, 0:n], psT[0:S, 0:n])
                            nc.scalar.copy(LT[:, b, 0:n], psT[0:10, 2 * P:2 * P + n]).then_inc(q["t_out"], 1)
                        t = tile(F_OUT)
                        if t:
                            n, b = t.rows, t.slot
                            act.wait_ge(q["filter"], t.n + 1)
                            if positive(t.n - (NB - 1)):
                                act.wait_ge(q["z_ready"], t.n - (NB - 1))
                            nc.scalar.copy(Wt[0:n, b, :], psW[0:n, 0:192]).then_inc(q["filter_out"], 1)
                        t = tile(Z_OUT)
                        if t:
                            n, b = t.rows, t.slot
                            act.wait_ge(q["z_turned"], t.n + 1)
                            if positive(t.n - (NB - 1)):
                                act.wait_ge(q["linear"], t.n - (NB - 1))
                            nc.scalar.copy(ZT[:, b, :, 0:n], psZ[0:96, b % 2, :].rearrange("p (c q) -> p c q", c=4)[:, :, 0:n])\
                                .then_inc(q["z_out"], 1)
                        t = tile(MIX_OUT)
                        if t:
                            n, b = t.rows, t.slot
                            act.wait_ge(q["mixed"], t.n + 1)
                            if positive(t.n - 1):
                                act.wait_ge(q["hid_out"], t.n - 1)
                            nc.scalar.activation(sg[:, b % 2, 0:n], psL[0:100, b % 2, 0:n], ACT.Sigmoid).then_inc(q["sig"], 1)
                        t = tile(MAP)
                        if t:
                            n, b = t.rows, t.slot
                            act.wait_ge(norm.ready, t.n + 1)
                            if positive(t.n - (NB - 1)):
                                act.wait_ge(q["turned"], t.n - (NB - 1))
                            norm.map(t, H[0:n, b, :], e.X[0:n, b, 0, :], 0).then_inc(norm.done, 1)
                    sweep(act, tiles, full_tiles, last_edges, ADD, step)

                @block.tensor
                def _(pe):
                    def step(tile):
                        t = tile(SUM)
                        if t:
                            n, b = t.rows, t.slot
                            pe.wait_ge(q["z_ready"], t.n + 1)
                            pe.wait_ge(e.eq_in[t.slot], (t.turn + 1) * 16)
                            if positive(t.n - 1):
                                pe.wait_ge(q["z_out"], t.n - 1)
                            for c in range(4):
                                mm = nc.tensor.matmul(psZ[0:96, b % 2, P * c:P * c + n], Z[0:n, b, c, :], e.EQ[0:n, b, 0:n],
                                                      start=True, stop=True)
                            mm.then_inc(q["z_turned"], 1)
                        t = tile(TURN)
                        if t:
                            n, b = t.rows, t.slot
                            pe.wait_ge(norm.done, t.n + 1)
                            pe.wait_ge(el_in[t.slot], (t.turn + 1) * 16)
                            if positive(t.n):
                                pe.wait_ge(q["t_out"], t.n)
                            nc.tensor.transpose(psT[0:96, P:P + n], H[0:n, b, S:D], ident[0:n, 0:n])
                            nc.tensor.transpose(psT[0:S, 0:n], H[0:n, b, 0:S], ident[0:n, 0:n])
                            nc.tensor.transpose(psT[0:10, 2 * P:2 * P + n], EL[0:n, b, :], ident[0:n, 0:n]).then_inc(q["turned"], 1)
                        t = tile(MIX)
                        if t:
                            n, b = t.rows, t.slot
                            pe.wait_ge(q["t_out"], t.n + 1)
                            if positive(t.n - 1):
                                pe.wait_ge(q["hid_out"], t.n - 1)
                            nc.tensor.matmul(psL[0:100, b % 2, 0:n], w("fcr1"), LT[:, b, 0:n], start=True, stop=True)
                            if positive(t.n):
                                pe.wait_ge(q["mix_out"], t.n)
                            o = psM[0:n, 0:2 * D].rearrange("p (k c) -> p k c", k=2)
                            nc.tensor.matmul(o[:, :, 0:S], HT[:, b, 0:n], w("l1_s").rearrange("p (k c) -> p k c", k=2), start=True, stop=True)
                            nc.tensor.matmul(o[:, :, S:D], VT[:, b, 0:n], w("l1_v").rearrange("p (k c) -> p k c", k=2), start=True, stop=True)\
                                .then_inc(q["mixed"], 1)
                        t = tile(FILTER)
                        if t:
                            n, b = t.rows, t.slot
                            pe.wait_ge(q["hid_out"], t.n + 1)
                            if positive(t.n):
                                pe.wait_ge(q["filter_out"], t.n)
                            nc.tensor.matmul(psW[0:n, 0:192], hidT[:, b, 0:n], w("fcr2"), start=True, stop=True).then_inc(q["filter"], 1)
                        t = tile(LINEAR)
                        if t:
                            n, b = t.rows, t.slot
                            pe.wait_ge(q["z_out"], t.n + 1)
                            if positive(t.n):
                                pe.wait_ge(q["result"], t.n)
                            o = psO[0:n, 0:2 * D].rearrange("p (k c) -> p k c", k=2)
                            nc.tensor.matmul(o[:, :, 0:S], ZT[:, b, 0, 0:n], WLs[:, :].rearrange("p (k c) -> p k c", k=2), start=True, stop=True)
                            for i in range(3):
                                mm = nc.tensor.matmul(o[:, :, S + i:D:3], ZT[:, b, 1 + i, 0:n], WLv[:, :].rearrange("p (k c) -> p k c", k=2),
                                                      start=True, stop=True)
                            mm.then_inc(q["linear"], 1)
                    sweep(pe, tiles, full_tiles, last_edges, ADD, step)


        def layer0_edges():
            with nc.cleanup_on_exit(), ExitStack() as ph:
                tag, LAST = "e0", 6
                HALVES, PIECES = 10, 3

                def sb(name, shape, dt=F32):
                    return ph.enter_context(nc.sbuf_tensor(f"{tag}_{name}", shape, dt))

                def pb(name, shape):
                    return ph.enter_context(nc.psum_tensor(f"{tag}_{name}", shape, F32))
                e = EdgePhase(ph, tag, x, DST, SRC, x1, D, (EA4, EA16), (2, 3, 5), gathers=2)
                norm = Norm(ph, tag, 2)
                zero = sb("zero", [P, G * D])
                Zm, ZmT, CT = sb("Zm", [P, 2, 544]), sb("ZmT", [P, 2, 4, P]), sb("CT", [V, P])
                VR, VD = sb("VR", [P, 3, V]), sb("VD", [P, V])
                xs, a0, xsT, a0T = sb("xs", [P, NB, S]), sb("a0", [P, NB, S]), sb("xsT", [S, 2, P]), sb("a0T", [S, 2, P])
                ak = sb("ak", [P, NB, 3, S])
                outer_p, outer_t, outer_d, outer_v = sb("outer_p", [P, PIECES, 1024]), sb("outer_t", [P, 2, 512]), sb("outer_d", [P, 1024]), sb("outer_v", [P, 3, 1024])
                prod = sb("prod", [P, 3, 2048])
                T4 = pb("T4", [P, 2048])
                psZ, psU, psM = pb("psZ", [P, 2, 512]), pb("psU", [P, 512]), pb("psM", [P, 512])
                q = {m: sem(f"{tag}_{m}") for m in (
                    "zero_set", "zm_pool", "zm_act", "vr", "vr1", "zm_turned", "c_turned", "zmt_out", "ct_out", "xs_out", "message", "a_out",
                    "a_turned", "a0t_out", "maps", "products", "u1", "piece", "dve_piece", "vv_product", "vv_part", "vv_sum", "half_turned", "half_out", "half_used",
                    "u0")}
                t3_zero, pe_passed = sem("t3_zero"), sem("e0_pe_passed")
                block = ph.enter_context(nc.Block())

                @block.sync
                def _(sp):
                    def step(tile):
                        e.loads(sp, tile, rows_used(e), (q["zm_pool"], q["zm_act"]), q["c_turned"])
                        t = tile(0)
                        if t:
                            if isinstance(t.n, int) and t.n == 0:
                                sp.wait_ge(q["zero_set"], 1)
                            t3_piece(sp, t)

                    def t3_piece(sp, t):
                        if isinstance(t.n, int) and t.n >= full_groups:
                            return
                        sp.dma_start(t3[bass.ds(t.n * (P * G), P * G), :].rearrange("(p g) c -> p (g c)", g=G), zero[:, :])\
                            .then_inc(t3_zero, 16)
                    sweep(sp, tiles, full_tiles, last_edges, LAST, step)
                    for g in range(min(tiles, full_groups), full_groups):
                        t3_piece(sp, Tile(g, 0, 0, P))
                    if groups > full_groups:
                        sp.dma_start(t3[full_groups * P * G:N, :].rearrange("(p g) c -> p (g c)", g=G), zero[0:last_parts, :])\
                            .then_inc(t3_zero, 16)
                    sp.wait_ge(t3_zero, 16 * groups)

                @block.gpsimd
                def _(pool):
                    nc.gpsimd.memset(zero[:, :], 0.0).then_inc(q["zero_set"], 1)

                    def piece(t, j):
                        n, b = t.rows, t.slot
                        if positive(t.n * HALVES + (2 * j - 6)):
                            pool.wait_ge(q["half_turned"], t.n * HALVES + (2 * j - 6))
                        nc.gpsimd.tensor_tensor(outer_p[0:n, j, :].rearrange("p (u v) -> p u v", v=S),
                                                repeat(xs[0:n, b, 16 * j + 16:16 * j + 32], 2, S), repeat(a0[0:n, b, :], 1, 16),
                                                ALU.mult).then_inc(q["piece"], 1)

                    def step(tile):
                        t = tile(1)
                        if t:
                            e.gather_rows(pool, t, norm.done)
                        t = tile(5)
                        if t:
                            pool.wait_ge(q["a_out"], t.n + 1)
                            for j in range(PIECES):
                                piece(t, j)
                        t_ = tile(6)
                        if t_:
                            pool.wait_ge(q["u1"], (t_.n + 1) * 3)
                            e.add_rows(pool, t_, q["u0"])
                        if t:
                            n, b = t.rows, t.slot
                            if positive(t.n * HALVES):
                                pool.wait_ge(q["half_turned"], t.n * HALVES)
                            for i in range(3):
                                nc.gpsimd.tensor_tensor(outer_v[0:n, i, :].rearrange("p (u v) -> p u v", v=V), repeat(ak[0:n, b, i, V:S], 2, V),
                                                        repeat(ak[0:n, b, i, 0:V], 1, V), ALU.mult).then_inc(q["vv_product"], 1)
                        t = tile(3)
                        if t:
                            n, b = t.rows, t.slot
                            pool.wait_ge(norm.done, t.n + 1)
                            pool.wait_ge(e.ea_in[t.slot], (t.turn + 1) * 16)
                            if positive(t.n):
                                pool.wait_ge(q["zm_pool"], t.n)
                            z = Zm[0:n, b % 2, :]
                            zi = z[:, P:512].rearrange("p (i c) -> p i c", i=3)
                            nc.gpsimd.tensor_tensor(VR[0:n], zi[:, :, 96:P], repeat(e.EA[0:n, b, 0:3], 2, V), ALU.mult).then_inc(q["vr"], 1)
                            pool.wait_ge(q["vr"], t.n + 1)
                            nc.gpsimd.tensor_tensor(VD[0:n], VR[0:n, 0], VR[0:n, 1], ALU.add).then_inc(q["vr1"], 1)
                            pool.wait_ge(q["vr1"], t.n + 1)
                            nc.gpsimd.tensor_tensor(z[:, 512:544], VD[0:n], VR[0:n, 2], ALU.add).then_inc(q["zm_pool"], 1)
                    sweep(pool, tiles, full_tiles, last_edges, LAST, step)
                    pool.wait_ge(e.added, 16 * tiles)

                @block.scalar
                def _(act):
                    def half(t, h):
                        n = t.rows
                        act.wait_ge(q["half_turned"], t.n * HALVES + (h + 1))
                        if positive(t.n * HALVES + (h - 1)):
                            act.wait_ge(q["half_used"], t.n * HALVES + (h - 1))
                        nc.scalar.copy(outer_t[:, h % 2, :].rearrange("p (c q) -> p c q", c=4)[:, :, 0:n],
                                       psZ[:, (h + 1) % 2, :].rearrange("p (c q) -> p c q", c=4)[:, :, 0:n]).then_inc(q["half_out"], 1)

                    def step(tile):
                        t4_, t5_ = tile(4), tile(5)
                        if t4_:
                            n, b = t4_.rows, t4_.slot % 2
                            act.wait_ge(q["zm_turned"], t4_.n + 1)
                            if positive(t4_.n - 1):
                                act.wait_ge(q["message"], t4_.n - 1)
                            nc.scalar.copy(ZmT[:, b, :, 0:n], psZ[:, 0, :].rearrange("p (c q) -> p c q", c=4)[:, :, 0:n])\
                                .then_inc(q["zmt_out"], 1)
                            act.wait_ge(q["c_turned"], t4_.n + 1)
                            nc.scalar.copy(CT[:, 0:n], psM[0:V, 0:n]).then_inc(q["ct_out"], 1)
                            if positive(t4_.n - 1):
                                act.wait_ge(q["maps"], t4_.n - 1)
                            nc.scalar.copy(xsT[:, b, 0:n], psM[0:S, P:P + n]).then_inc(q["xs_out"], 1)
                        if t5_:
                            half(t5_, 0)
                            half(t5_, 1)
                        if t4_:
                            n, b = t4_.rows, t4_.slot
                            act.wait_ge(q["message"], t4_.n + 1)
                            if positive((t4_.n - (NB - 1)) * 3):
                                act.wait_ge(q["vv_product"], (t4_.n - (NB - 1)) * 3)
                            if positive((t4_.n - (NB - 1)) * 3):
                                act.wait_ge(q["products"], (t4_.n - (NB - 1)) * 3)
                            nc.scalar.copy(a0[0:n, b, :], psM[0:n, 2 * P:2 * P + S])
                            nc.scalar.copy(ak[0:n, b, :, 0:V], psM[0:n, 2 * P + S:2 * P + D].rearrange("p (i v) -> p i v", i=3))\
                                .then_inc(q["a_out"], 1)
                        if t5_:
                            half(t5_, 2)
                            half(t5_, 3)
                        if t4_:
                            n, b = t4_.rows, t4_.slot % 2
                            act.wait_ge(q["a_turned"], t4_.n + 1)
                            nc.scalar.copy(a0T[:, b, 0:n], psM[0:S, 0:n]).then_inc(q["a0t_out"], 1)
                        if t5_:
                            half(t5_, 4)
                            half(t5_, 5)
                        t = tile(3)
                        if t:
                            n, b = t.rows, t.slot
                            act.wait_ge(norm.ready, t.n + 1)
                            if positive(t.n - 1):
                                act.wait_ge(q["c_turned"], t.n - 1)
                            if positive((t.n - (NB - 1)) * 3):
                                act.wait_ge(q["vv_product"], (t.n - (NB - 1)) * 3)
                            if positive(t.n - (NB - 1)):
                                act.wait_ge(q["dve_piece"], t.n - (NB - 1))
                            if positive((t.n - (NB - 1)) * 3):
                                act.wait_ge(q["products"], (t.n - (NB - 1)) * 3)
                            z = Zm[0:n, b % 2, :]
                            zi = z[:, P:512].rearrange("p (i c) -> p i c", i=3)
                            norm.map(t, z[:, S:P], e.X[0:n, b, 0, 0:S], 0)
                            norm.map(t, zi[:, :, 96:P], e.X[0:n, b, 0, S:D].rearrange("p (u i) -> p i u", i=3), 0)
                            norm.map(t, xs[0:n, b, :], e.X[0:n, b, 1, 0:S], 1)
                            norm.map(t, ak[0:n, b, :, V:S], e.X[0:n, b, 1, S:D].rearrange("p (u i) -> p i u", i=3), 1)\
                                .then_inc(norm.done, 1)
                            act.wait_ge(e.ea_in[t.slot], (t.turn + 1) * 16)
                            act.wait_ge(norm.done, t.n + 1)
                            dist = e.EA[0:n, b, 3:4]
                            nc.scalar.activation(z[:, 0:S], z[:, S:P], ACT.Copy, scale=dist)
                            for i in range(3):
                                nc.scalar.activation(zi[:, i, 0:S], z[:, S:P], ACT.Copy, scale=e.EA[0:n, b, i:i + 1])
                            nc.scalar.activation(zi[:, :, S:96], zi[:, :, 96:P], ACT.Copy, scale=dist).then_inc(q["zm_act"], 1)
                        if t5_:
                            for h in range(6, 8):
                                half(t5_, h)
                        t = tile(2)
                        if t:
                            norm.root(act, t)
                        if t5_:
                            for h in range(8, HALVES):
                                half(t5_, h)
                            n, b = t5_.rows, t5_.slot
                            act.wait_ge(q["half_used"], (t5_.n + 1) * HALVES)
                            if positive((t5_.n - (NB - 1)) * 16):
                                act.wait_ge(e.added, (t5_.n - (NB - 1)) * 16)
                            nc.scalar.copy(e.R[0:n, b, 0:S], psU[0:n, 0:S]).then_inc(q["u0"], 1)
                    sweep(act, tiles, full_tiles, last_edges, LAST, step)

                @block.tensor
                def _(pe):
                    wss = w("u_ss").rearrange("p (c n) -> p c n", n=S)
                    wvv = w("u_vv").rearrange("p (c n) -> p c n", n=S)

                    def turn(t, h):
                        n = t.rows
                        if h < 2:
                            pe.wait_ge(q["dve_piece"], t.n + 1)
                            source = outer_d[0:n, :]
                        elif h < 8:
                            pe.wait_ge(q["piece"], t.n * PIECES + h // 2)
                            source = outer_p[0:n, h // 2 - 1, :]
                        else:
                            pe.wait_ge(q["vv_sum"], t.n + 1)
                            source = outer_v[0:n, 0, :]
                        if positive(t.n * HALVES + (h - 1)):
                            pe.wait_ge(q["half_out"], t.n * HALVES + (h - 1))
                        for c in range(4):
                            at = (h % 2) * 512 + c * P
                            tr = nc.tensor.transpose(psZ[:, (h + 1) % 2, c * P:c * P + n], source[:, at:at + P], ident[0:n, 0:n])
                        tr.then_inc(q["half_turned"], 1)

                    def use(t, h):
                        n = t.rows
                        pe.wait_ge(q["half_out"], t.n * HALVES + (h + 1))
                        if h == 0:
                            if positive(t.n):
                                pe.wait_ge(q["u0"], t.n)
                        for c in range(4):
                            weights = wss[:, 4 * h + c, :] if h < 8 else wvv[:, 4 * (h % 2) + c, :]
                            mm = nc.tensor.matmul(psU[0:n, 0:S], outer_t[:, h % 2, c * P:c * P + n], weights,
                                                  start=(h == 0 and c == 0), stop=(h == HALVES - 1 and c == 3))
                        mm.then_inc(q["half_used"], 1)

                    def step(tile):
                        t4_, t5_ = tile(4), tile(5)
                        if t4_:
                            n, b = t4_.rows, t4_.slot
                            pe.wait_ge(q["zm_pool"], t4_.n + 1)
                            pe.wait_ge(q["zm_act"], t4_.n + 1)
                            pe.wait_ge(e.eq_in[t4_.slot], (t4_.turn + 1) * 16)
                            if positive((t4_.n - 1) * HALVES):
                                pe.wait_ge(q["half_out"], (t4_.n - 1) * HALVES)
                            z, eq = Zm[0:n, b % 2, :], e.EQ[0:n, b, 0:n]
                            for c in range(4):
                                mm = nc.tensor.matmul(psZ[:, 0, c * P:c * P + n], z[:, c * P:(c + 1) * P], eq, start=True, stop=True)
                            mm.then_inc(q["zm_turned"], 1)
                            if positive(t4_.n):
                                pe.wait_ge(q["a0t_out"], t4_.n)
                            nc.tensor.matmul(psM[0:V, 0:n], z[:, 512:544], eq, start=True, stop=True)
                            nc.tensor.transpose(psM[0:S, P:P + n], xs[0:n, b, :], ident[0:n, 0:n]).then_inc(q["c_turned"], 1)
                        if t5_:
                            turn(t5_, 0)
                            if t4_:
                                pe.wait_ge(q["zmt_out"], t4_.n + 1)
                            turn(t5_, 1)
                            use(t5_, 0)
                        if t4_:
                            n, b = t4_.rows, t4_.slot
                            pe.wait_ge(q["zmt_out"], t4_.n + 1)
                            pe.wait_ge(q["ct_out"], t4_.n + 1)
                            pe.wait_ge(q["xs_out"], t4_.n + 1)
                            if positive(t4_.n):
                                pe.wait_ge(q["a_out"], t4_.n)
                            nc.tensor.matmul(psM[0:n, 2 * P:2 * P + S], ZmT[:, b % 2, 0, 0:n], w("m_a"), start=True, stop=False)
                            nc.tensor.matmul(psM[0:n, 2 * P:2 * P + S], CT[:, 0:n], w("m_c"), start=False, stop=True)
                            for i in range(3):
                                at = 2 * P + S + V * i
                                mm = nc.tensor.matmul(psM[0:n, at:at + V], ZmT[:, b % 2, 1 + i, 0:n], w("m_b"), start=True, stop=True)
                            mm.then_inc(q["message"], 1)
                        if t5_:
                            turn(t5_, 2)
                            use(t5_, 1)
                            turn(t5_, 3)
                            use(t5_, 2)
                        if t4_:
                            n, b = t4_.rows, t4_.slot
                            pe.wait_ge(q["a_out"], t4_.n + 1)
                            pe.sem_inc(pe_passed, 1)
                            nc.tensor.transpose(psM[0:S, 0:n], a0[0:n, b, :], ident[0:n, 0:n]).then_inc(q["a_turned"], 1)
                        if t5_:
                            turn(t5_, 4)
                            use(t5_, 3)
                            turn(t5_, 5)
                            use(t5_, 4)
                        if t4_:
                            n, b = t4_.rows, t4_.slot % 2
                            pe.wait_ge(q["xs_out"], t4_.n + 1)
                            pe.wait_ge(q["a0t_out"], t4_.n + 1)
                            if positive(t4_.n * 3):
                                pe.wait_ge(q["products"], t4_.n * 3)
                            for c in range(2):
                                nc.tensor.matmul(T4[0:n, 512 * c:512 * c + 512], xsT[:, b, 0:n], w("u_sv")[:, 512 * c:512 * c + 512],
                                                 start=True, stop=True)
                            for c in range(2):
                                mm = nc.tensor.matmul(T4[0:n, 1024 + 512 * c:1536 + 512 * c], a0T[:, b, 0:n],
                                                      w("u_vs")[:, 512 * c:512 * c + 512], start=True, stop=True)
                            mm.then_inc(q["maps"], 1)
                        if t5_:
                            for h in range(6, HALVES):
                                turn(t5_, h)
                                use(t5_, h - 1)
                            use(t5_, HALVES - 1)
                    sweep(pe, tiles, full_tiles, last_edges, LAST, step)

                @block.vector
                def _(dve):
                    def step(tile):
                        t = tile(5)
                        if t:
                            n, b = t.rows, t.slot
                            dve.wait_ge(q["maps"], t.n + 1)
                            dve.wait_ge(q["a_out"], t.n + 1)
                            t4 = T4[0:n, :].rearrange("p (k w) -> p k w", w=V)
                            for i in range(3):
                                if positive((t.n - 1) * 3 + (i + 1)):
                                    dve.wait_ge(q["u1"], (t.n - 1) * 3 + (i + 1))
                                nc.vector.tensor_tensor(prod[0:n, i, :].rearrange("p (k w) -> p k w", w=V), t4,
                                                        repeat(ak[0:n, b, i, :], 2, V), ALU.mult).then_inc(q["products"], 1)
                        t2 = tile(2)
                        if t2:
                            dve.wait_ge(e.rows_in[t2.slot], (t2.turn + 1) * 32)
                            norm.statistics(dve, t2, [e.X[0:t2.rows, t2.slot, g, :] for g in range(2)])
                        if t:
                            if positive((t.n - (NB - 1)) * 16):
                                dve.wait_ge(e.added, (t.n - (NB - 1)) * 16)
                            for i in range(3):
                                dve.wait_ge(q["products"], t.n * 3 + (i + 1))
                                nc.vector.tensor_reduce(e.R[0:n, b, S + i:D:3], prod[0:n, i, :].rearrange("p (k w) -> p w k", w=V),
                                                        AX_X, ALU.add).then_inc(q["u1"], 1)
                        if t:
                            n = t.rows
                            if positive(t.n * 3 + 2):
                                dve.wait_ge(q["vv_product"], t.n * 3 + 2)
                            nc.vector.tensor_tensor(outer_v[0:n, 0, :], outer_v[0:n, 0, :], outer_v[0:n, 1, :], ALU.add)\
                                .then_inc(q["vv_part"], 1)
                            if positive(t.n * 3 + 3):
                                dve.wait_ge(q["vv_product"], t.n * 3 + 3)
                            dve.wait_ge(q["vv_part"], t.n + 1)
                            nc.vector.tensor_tensor(outer_v[0:n, 0, :], outer_v[0:n, 0, :], outer_v[0:n, 2, :], ALU.add)\
                                .then_inc(q["vv_sum"], 1)
                        if t2:
                            norm.scales(dve, t2)
                        t = tile(4)
                        if t:
                            n, b = t.rows, t.slot
                            dve.wait_ge(q["a_out"], t.n + 1)
                            if positive((t.n - 1) * HALVES + 2):
                                dve.wait_ge(q["half_turned"], (t.n - 1) * HALVES + 2)
                            nc.vector.tensor_tensor(outer_d[0:n, :].rearrange("p (u v) -> p u v", v=S), repeat(xs[0:n, b, 0:16], 2, S),
                                                    repeat(a0[0:n, b, :], 1, 16), ALU.mult).then_inc(q["dve_piece"], 1)
                    sweep(dve, tiles, full_tiles, last_edges, LAST, step)

        dense_phase("d0", 0)
        layer0_edges()
        dense_phase("d1", 1)
        layer1_edges()
        dense_phase("d2", 2)
        layer2_edges()
        layer3_edges()
        dense_phase("d3", 3)


def kernel(**inputs):
    import numpy as _np
    import concourse.bacc as _bacc
    from concourse.bass_utils import run_bass_kernel_spmd as _run

    a = {k: _np.asarray(v) for k, v in inputs.items()}
    N, E = a["x"].shape[0], a["src"].shape[0]

    def kron(m):
        o = _np.zeros((3 * m.shape[0], 3 * m.shape[1]), m.dtype)
        for i in range(3):
            o[i::3, i::3] = m
        return o

    def apart(m):
        r, c = m.shape
        o = _np.zeros((3 * r, 3 * c), m.dtype)
        for i in range(3):
            o[i::3, i * c:(i + 1) * c] = m
        return o

    def twice(m):
        o = _np.zeros((2 * m.shape[0], 2 * m.shape[1]), m.dtype)
        o[:m.shape[0], :m.shape[1]] = o[m.shape[0]:, m.shape[1]:] = m
        return o

    def chunks(m):
        return m.reshape(-1, P, m.shape[-1]).transpose(1, 0, 2).reshape(P, -1)

    rows, cols = (lambda *m: _np.concatenate(m, 0)), (lambda *m: _np.concatenate(m, 1))
    l0, l1, l2, l3 = (lambda k, g=g: a[f"L{g}_gnn_{k}"] for g in range(4))
    radial = rows(l2("W_rad").T, l2("b_rad").reshape(1, -1))
    l2_s_rad = _np.zeros((113, S + D), radial.dtype)
    l2_s_rad[:96, :S] = rows(l2("W_ss"), l2("W_vv"))
    l2_s_rad[96:, S:] = cols(radial[:, S:], radial[:, :S])
    blocks = {
        "u_ss": chunks(l0("Wu_ss").reshape(S * S, S)), "u_vv": chunks(l0("Wu_vv").reshape(V * V, S)),
        "u_sv": l0("Wu_sv").reshape(S, V * V), "u_vs": l0("Wu_vs").transpose(1, 0, 2).reshape(S, V * V),
        "m_a": rows(l0("Wm_ss"), l0("Lm_s")), "m_c": l0("Wm_vv"), "m_b": rows(l0("Wm_sv"), l0("Wm_vs"), l0("Lm_v")),
        "lu_s": twice(l0("Lu_s")), "lu_v": kron(l0("Lu_v")),
        "skip_s": twice(l1("W_skip0")), "skip_v": kron(l1("W_skip1")), "nl_s": l1("W_nl0"), "nl_v": apart(l1("W_nl1")),
        "fc1": l1("W_fc1"), "fc2": l1("W_fc2"), "out_s": l1("W_out_s"), "out_v": l1("W_out_v"),
        "l2_s_rad": l2_s_rad, "l2_v": rows(l2("W_sv"), l2("W_vs")),
        "l2l_s": twice(l2("L_s")), "l2l_v": kron(l2("L_v")),
        "sc_s": _np.tile(cols(l3("Ws_sc_a"), l3("Ws_sc_c")), (2, 1)), "sc_v": cols(kron(l3("Wv_sc_a")), kron(l3("Wv_sc_c"))),
        "l1_s": cols(l3("Ws_l1_a"), l3("Ws_l1_c")), "l1_v": cols(apart(l3("Wv_l1_a")), apart(l3("Wv_l1_c"))),
        "fcr1": l3("W_fc1"), "fcr2": l3("W_fc2"),
        "l2aT_s": l3("Ws_l2_a").T, "l2cT_s": l3("Ws_l2_c").T, "l2aT_v": l3("Wv_l2_a").T, "l2cT_v": l3("Wv_l2_c").T,
        "l3_s": l3("Ws_l3"), "l3_v": l3("Wv_l3"),
    }
    start, width = weight_columns()
    wpack, wscale = _np.zeros((P, width), _np.float32), _np.zeros((P, width), _np.float32)
    for name, (r, c, scales) in weight_blocks().items():
        assert blocks[name].shape == (r, c), name
        wpack[0:r, start[name]:start[name] + c] = blocks[name]
        for r0, r1, c0, c1, s in scales:
            wscale[r0:r1, start[name] + c0:start[name] + c1] = s
    consts = _np.zeros((P, K_WIDTH), _np.float32)
    consts[:, K_IDENT:K_IDENT + P] = _np.eye(P)
    consts[:, K_LOWER:K_LOWER + P] = _np.tril(_np.ones((P, P)), -1)
    consts[:, K_JUNK] = N + _np.arange(P)
    consts[:, K_EPS] = EPS
    idx2 = _np.ascontiguousarray(_np.stack([a["src"], a["dst"]], 1))
    arrays = {
        "x": a["x"], "idx2": idx2, "idx2T": _np.ascontiguousarray(idx2.T),
        "ea": _np.ascontiguousarray(cols(a["edge_attr_10"], a["edge_attr_4"], a["edge_attr_16"], a["edge_attr_3"], a["edge_attr_64"])),
        "nattr": _np.pad(cols(a["node_vec1"], a["node_vec1_n2"], a["node_vec1_n3"]), ((0, P), (0, 0))),
        "wpack": wpack, "wscale": wscale, "consts": consts,
    }
    nc = _bacc.Bacc("TRN2", target_bir_lowering=False, num_devices=1)
    args = {k: nc.dram_tensor(k, v.shape, mybir.dt.from_np(v.dtype), kind="ExternalInput").ap() for k, v in arrays.items()}
    out = nc.dram_tensor("out", (N, D), F32, kind="ExternalOutput").ap()
    build(nc, N, E, out=out, **args)
    r = _run(nc, [arrays], core_ids=[0])
    return r.results[0]["out"]
```
